# Optimizing a Trainium2 kernel written in Bass

```python
import numpy as np
import jax
import jax.numpy as jnp

def _softmax(x, axis=-1):
    return jax.nn.softmax(x, axis=axis)

def _gelu(x):
    return jax.nn.gelu(x, approximate=True)

def _silu(x):
    return jax.nn.silu(x)

def _sigmoid(x):
    return jax.nn.sigmoid(x)

def _layernorm(x, axis=-1, eps=1e-05):
    m = jnp.mean(x, axis=axis, keepdims=True)
    v = jnp.var(x, axis=axis, keepdims=True)
    return (x - m) / jnp.sqrt(v + eps)

def _scatter_add(tgt, idx, src, axis=0):
    return tgt.at[idx].add(src)

def _segment_sum(src, seg, n):
    return jax.ops.segment_sum(src, seg, n)
kernel_name = 'mk_lm_tower_d2_tok_ids1024_r4_830126'

def setup_inputs(seed: int=0):
    np.random.seed(seed)
    _w = jnp.asarray

    def _rec_inputs():
        import jax
        import jax.numpy as jnp
        _rk = jax.random.key(seed)
        x = jax.random.randint(jax.random.fold_in(_rk, 1), (16, 128), 0, 12564, jnp.int32)
        return x
    x = _rec_inputs()

    def _L0_tok_setup():
        import jax, jax.numpy as jnp
        import numpy as np
        VOCAB, DIM, N_DOM, EXP = (50257, 256, 8, 32)
        B, S = (4, 1024)
        key = jax.random.key(seed)
        k1, k2, k3, k4, k5, k6 = jax.random.split(key, 6)
        token_ids = jax.random.randint(k1, (B, S), 0, VOCAB, dtype=jnp.int32)
        dom = jax.random.randint(k2, (VOCAB,), 0, N_DOM, dtype=jnp.int32)
        routed = jax.random.uniform(k3, (VOCAB,)) < 0.2
        domain_map = jnp.where(routed, dom, jnp.int32(-1))
        emb_table = jax.random.normal(k4, (VOCAB, DIM), dtype=jnp.float32) * 0.02
        lim_e = 0.1 * np.sqrt(6.0 / (DIM + EXP))
        lim_p = 0.1 * np.sqrt(6.0 / (EXP + DIM))
        W_exp = jax.random.uniform(k5, (N_DOM, EXP, DIM), minval=-lim_e, maxval=lim_e, dtype=jnp.float32)
        W_proj = jax.random.uniform(k6, (N_DOM, DIM, EXP), minval=-lim_p, maxval=lim_p, dtype=jnp.float32)
        return {'token_ids': token_ids, 'domain_map': domain_map, 'emb_table': emb_table, 'W_exp': W_exp, 'W_proj': W_proj}
    _L0_tok_all = _L0_tok_setup()
    _L0_tok_in = {k: v for k, v in _L0_tok_all.items() if k in ('domain_map', 'emb_table', 'W_exp', 'W_proj')}
    del _L0_tok_all

    def _L0_attn_setup():
        import jax, jax.numpy as jnp
        import numpy as np
        S, B, F = (512, 2, 256)
        H, D = (16, 64)
        P = H * D
        key = jax.random.key(seed)
        k1, k2, k3 = jax.random.split(key, 3)
        return {'src': jax.random.normal(k1, (S, B, F), dtype=jnp.float32), 'in_proj_weight': jax.random.normal(k2, (3 * P, F), dtype=jnp.float32) * (1.0 / np.sqrt(F)), 'in_proj_bias': jnp.zeros((3 * P,), dtype=jnp.float32), 'out_proj_weight': jax.random.normal(k3, (F, P), dtype=jnp.float32) * (1.0 / np.sqrt(P)), 'out_proj_bias': jnp.zeros((F,), dtype=jnp.float32)}
    _L0_attn_all = _L0_attn_setup()
    _L0_attn_in = {k: v for k, v in _L0_attn_all.items() if k in ('in_proj_weight', 'in_proj_bias', 'out_proj_weight', 'out_proj_bias')}
    del _L0_attn_all

    def _L0_ffn_setup():
        import jax, jax.numpy as jnp
        import numpy as np
        D, FF, E, K = (256, 256, 8, 2)
        B, S = (4, 256)

        def _gelu(x):
            return jax.nn.gelu(x, approximate=False)
        key = jax.random.key(seed)
        ks = jax.random.split(key, 12)
        s = 0.02
        return {'x': jax.random.normal(ks[0], (B, S, D), jnp.float32), 'gate_w': jax.random.normal(ks[1], (D, E), jnp.float32) * s, 'gate_b': jnp.zeros((E,), jnp.float32), 'sw1': jax.random.normal(ks[2], (D, FF), jnp.float32) * s, 'sb1': jnp.zeros((FF,), jnp.float32), 'sw2': jax.random.normal(ks[3], (FF, D), jnp.float32) * s, 'sb2': jnp.zeros((D,), jnp.float32), 'w1': jax.random.normal(ks[4], (E, D, FF), jnp.float32) * s, 'b1': jnp.zeros((E, FF), jnp.float32), 'w2': jax.random.normal(ks[5], (E, FF, D), jnp.float32) * s, 'b2': jnp.zeros((E, D), jnp.float32)}
    _L0_ffn_all = _L0_ffn_setup()
    _L0_ffn_in = {k: v for k, v in _L0_ffn_all.items() if k in ('gate_w', 'gate_b', 'sw1', 'sb1', 'sw2', 'sb2', 'w1', 'b1', 'w2', 'b2')}
    del _L0_ffn_all

    def _L1_attn_setup():
        import jax, jax.numpy as jnp
        import numpy as np
        T, B, E, H = (256, 2, 256, 16)
        D = E // H
        R = 2 * T - 1

        def _rel_shift(x):
            b, h, q, r = x.shape
            zp = jnp.zeros((b, h, q, 1), x.dtype)
            xp = jnp.concatenate([zp, x], axis=3)
            xp = xp.reshape(b, h, r + 1, q)[:, :, 1:, :]
            return xp.reshape(b, h, q, r)
        key = jax.random.key(seed)
        ks = jax.random.split(key, 8)
        std = (2.0 / (E + E)) ** 0.5
        return {'x': jax.random.normal(ks[0], (T, B, E), jnp.float32), 'pos': jax.random.normal(ks[1], (R, 1, E), jnp.float32), 'in_proj_weight': jax.random.normal(ks[2], (3 * E, E), jnp.float32) * std, 'in_proj_bias': jnp.zeros((3 * E,), jnp.float32), 'pos_proj_weight': jax.random.normal(ks[3], (E, E), jnp.float32) * std, 'pos_proj_bias': jnp.zeros((E,), jnp.float32), 'out_proj_weight': jax.random.normal(ks[4], (E, E), jnp.float32) * std, 'out_proj_bias': jnp.zeros((E,), jnp.float32), 'r_w_bias': jax.random.normal(ks[5], (H, D), jnp.float32) * 0.02, 'r_r_bias': jax.random.normal(ks[6], (H, D), jnp.float32) * 0.02}
    _L1_attn_all = _L1_attn_setup()
    _L1_attn_in = {k: v for k, v in _L1_attn_all.items() if k in ('pos', 'in_proj_weight', 'in_proj_bias', 'pos_proj_weight', 'pos_proj_bias', 'out_proj_weight', 'out_proj_bias', 'r_w_bias', 'r_r_bias')}
    del _L1_attn_all

    def _L1_ffn_setup():
        import jax, jax.numpy as jnp
        import numpy as np
        import math
        B, S, D = (4, 512, 256)
        E, DFF = (16, 512)
        CAP_FACTOR = 2.0
        ROUTER_HIDDEN = 128
        CAPACITY = int(math.ceil(S * CAP_FACTOR / E))
        key = jax.random.key(seed)
        ks = jax.random.split(key, 6)

        def uinit(k, shape, fan_in):
            bound = math.sqrt(3.0) * math.sqrt(1.0 / 3.0) / math.sqrt(fan_in)
            return jax.random.uniform(k, shape, jnp.float32, -bound, bound)
        return {'hidden_states': jax.random.normal(ks[0], (B, S, D), jnp.float32), 'router_w1': jax.random.normal(ks[1], (D, ROUTER_HIDDEN), jnp.float32) / math.sqrt(D), 'router_w2': jax.random.normal(ks[2], (ROUTER_HIDDEN, E), jnp.float32) / math.sqrt(ROUTER_HIDDEN), 'w1': uinit(ks[3], (E, D, DFF), D), 'w2': uinit(ks[4], (E, D, DFF), D), 'w3': uinit(ks[5], (E, DFF, D), DFF)}
    _L1_ffn_all = _L1_ffn_setup()
    _L1_ffn_in = {k: v for k, v in _L1_ffn_all.items() if k in ('router_w1', 'router_w2', 'w1', 'w2', 'w3')}
    del _L1_ffn_all
    return {'x': x, 'L0_tok_domain_map': _L0_tok_in['domain_map'], 'L0_tok_emb_table': _L0_tok_in['emb_table'], 'L0_tok_W_exp': _L0_tok_in['W_exp'], 'L0_tok_W_proj': _L0_tok_in['W_proj'], 'L0_attn_in_proj_weight': _L0_attn_in['in_proj_weight'], 'L0_attn_in_proj_bias': _L0_attn_in['in_proj_bias'], 'L0_attn_out_proj_weight': _L0_attn_in['out_proj_weight'], 'L0_attn_out_proj_bias': _L0_attn_in['out_proj_bias'], 'L0_ffn_gate_w': _L0_ffn_in['gate_w'], 'L0_ffn_gate_b': _L0_ffn_in['gate_b'], 'L0_ffn_sw1': _L0_ffn_in['sw1'], 'L0_ffn_sb1': _L0_ffn_in['sb1'], 'L0_ffn_sw2': _L0_ffn_in['sw2'], 'L0_ffn_sb2': _L0_ffn_in['sb2'], 'L0_ffn_w1': _L0_ffn_in['w1'], 'L0_ffn_b1': _L0_ffn_in['b1'], 'L0_ffn_w2': _L0_ffn_in['w2'], 'L0_ffn_b2': _L0_ffn_in['b2'], 'L1_attn_pos': _L1_attn_in['pos'], 'L1_attn_in_proj_weight': _L1_attn_in['in_proj_weight'], 'L1_attn_in_proj_bias': _L1_attn_in['in_proj_bias'], 'L1_attn_pos_proj_weight': _L1_attn_in['pos_proj_weight'], 'L1_attn_pos_proj_bias': _L1_attn_in['pos_proj_bias'], 'L1_attn_out_proj_weight': _L1_attn_in['out_proj_weight'], 'L1_attn_out_proj_bias': _L1_attn_in['out_proj_bias'], 'L1_attn_r_w_bias': _L1_attn_in['r_w_bias'], 'L1_attn_r_r_bias': _L1_attn_in['r_r_bias'], 'L1_ffn_router_w1': _L1_ffn_in['router_w1'], 'L1_ffn_router_w2': _L1_ffn_in['router_w2'], 'L1_ffn_w1': _L1_ffn_in['w1'], 'L1_ffn_w2': _L1_ffn_in['w2'], 'L1_ffn_w3': _L1_ffn_in['w3']}

def reference(x, L0_tok_domain_map, L0_tok_emb_table, L0_tok_W_exp, L0_tok_W_proj, L0_attn_in_proj_weight, L0_attn_in_proj_bias, L0_attn_out_proj_weight, L0_attn_out_proj_bias, L0_ffn_gate_w, L0_ffn_gate_b, L0_ffn_sw1, L0_ffn_sb1, L0_ffn_sw2, L0_ffn_sb2, L0_ffn_w1, L0_ffn_b1, L0_ffn_w2, L0_ffn_b2, L1_attn_pos, L1_attn_in_proj_weight, L1_attn_in_proj_bias, L1_attn_pos_proj_weight, L1_attn_pos_proj_bias, L1_attn_out_proj_weight, L1_attn_out_proj_bias, L1_attn_r_w_bias, L1_attn_r_r_bias, L1_ffn_router_w1, L1_ffn_router_w2, L1_ffn_w1, L1_ffn_w2, L1_ffn_w3):
    import jax
    import jax.numpy as jnp

    def _L0_tok_ref(token_ids, domain_map, emb_table, W_exp, W_proj):
        import jax, jax.numpy as jnp
        import numpy as np
        VOCAB, DIM, N_DOM, EXP = (50257, 256, 8, 32)
        B, S = (4, 1024)
        base = emb_table[token_ids]
        dom = domain_map[token_ids]
        out = base
        n_domains = W_exp.shape[0]
        for d in range(n_domains):
            mask = (dom == d)[..., None].astype(base.dtype)
            expanded = jnp.einsum('bsd,ed->bse', base, W_exp[d])
            corr = jnp.einsum('bse,de->bsd', expanded, W_proj[d])
            out = out + 0.1 * corr * mask
        return out

    def _L0_attn_ref(src, in_proj_weight, in_proj_bias, out_proj_weight, out_proj_bias):
        import jax, jax.numpy as jnp
        import numpy as np
        S, B, F = (512, 2, 256)
        H, D = (16, 64)
        P = H * D
        s, b, f = src.shape
        h, d = (H, D)
        qkv = jnp.einsum('sbf,pf->sbp', src, in_proj_weight) + in_proj_bias
        q, k, v = jnp.split(qkv, 3, axis=-1)

        def to_heads(x):
            return jnp.swapaxes(x.reshape(s, b * h, d), 0, 1)
        q = to_heads(q) / np.sqrt(d)
        k = to_heads(k)
        v = to_heads(v)
        attn = jnp.einsum('nsd,ntd->nst', q, k)
        attn = jax.nn.softmax(attn, axis=-1)
        out = jnp.einsum('nst,ntd->nsd', attn, v)
        out = jnp.swapaxes(out, 0, 1).reshape(s * b, h * d)
        out = out @ out_proj_weight.T + out_proj_bias
        return out.reshape(s, b, f)

    def _L0_ffn_ref(x, gate_w, gate_b, sw1, sb1, sw2, sb2, w1, b1, w2, b2):
        import jax, jax.numpy as jnp
        import numpy as np
        D, FF, E, K = (256, 256, 8, 2)
        B, S = (4, 256)

        def _gelu(x):
            return jax.nn.gelu(x, approximate=False)
        Bb, Ss, Dm = x.shape
        t = x.reshape(-1, Dm)
        T = t.shape[0]
        shared = _gelu(t @ sw1 + sb1) @ sw2 + sb2
        probs = jax.nn.softmax(t @ gate_w + gate_b, axis=-1)
        topk_p, topk_i = jax.lax.top_k(probs, K)
        combine = jnp.zeros((T, E), t.dtype).at[jnp.arange(T)[:, None], topk_i].set(topk_p)
        h = _gelu(jnp.einsum('td,edf->etf', t, w1) + b1[:, None, :])
        y = jnp.einsum('etf,efd->etd', h, w2) + b2[:, None, :]
        routed = jnp.einsum('te,etd->td', combine, y)
        return (routed + shared).reshape(Bb, Ss, Dm)

    def _L1_attn_ref(x, pos, in_proj_weight, in_proj_bias, pos_proj_weight, pos_proj_bias, out_proj_weight, out_proj_bias, r_w_bias, r_r_bias):
        import jax, jax.numpy as jnp
        import numpy as np
        T, B, E, H = (256, 2, 256, 16)
        D = E // H
        R = 2 * T - 1

        def _rel_shift(x):
            b, h, q, r = x.shape
            zp = jnp.zeros((b, h, q, 1), x.dtype)
            xp = jnp.concatenate([zp, x], axis=3)
            xp = xp.reshape(b, h, r + 1, q)[:, :, 1:, :]
            return xp.reshape(b, h, q, r)
        t, b, e = x.shape
        h, d = r_w_bias.shape
        qkv = x @ in_proj_weight.T + in_proj_bias
        q, k, v = jnp.split(qkv, 3, axis=-1)
        q = q.reshape(t, b, h, d)
        k = k.reshape(t, b, h, d)
        v = v.reshape(t, b, h, d)
        p = (pos @ pos_proj_weight.T + pos_proj_bias).reshape(-1, h, d)
        scale = 1.0 / jnp.sqrt(jnp.asarray(d, x.dtype))
        ac = jnp.einsum('tbhd,sbhd->bhts', q + r_w_bias, k)
        bd = jnp.einsum('tbhd,rhd->bhtr', q + r_r_bias, p)
        bd = _rel_shift(bd)[..., :t]
        attn = jax.nn.softmax((ac + bd) * scale, axis=-1)
        ctx = jnp.einsum('bhts,sbhd->tbhd', attn, v).reshape(t, b, e)
        return ctx @ out_proj_weight.T + out_proj_bias

    def _L1_ffn_ref(hidden_states, router_w1, router_w2, w1, w2, w3):
        import jax, jax.numpy as jnp
        import numpy as np
        import math
        B, S, D = (4, 512, 256)
        E, DFF = (16, 512)
        CAP_FACTOR = 2.0
        ROUTER_HIDDEN = 128
        CAPACITY = int(math.ceil(S * CAP_FACTOR / E))
        b, s, d = hidden_states.shape
        e = w1.shape[0]
        cap = CAPACITY
        router_logits = jax.nn.silu(hidden_states @ router_w1) @ router_w2
        expert_probs = jax.nn.softmax(router_logits.transpose(0, 2, 1), axis=-1)
        expert_weights, token_indices = jax.lax.top_k(expert_probs, cap)
        expert_weights = expert_weights / (expert_weights.sum(-1, keepdims=True) + 1e-09)
        expert_inputs = jax.vmap(lambda h, i: h[i])(hidden_states, token_indices)
        gate = jax.nn.silu(jnp.einsum('becd,edf->becf', expert_inputs, w1))
        value = jnp.einsum('becd,edf->becf', expert_inputs, w2)
        expert_out = jnp.einsum('becf,efd->becd', gate * value, w3)
        weighted = expert_out * expert_weights[..., None]

        def combine(idx, vals):
            return jnp.zeros((s, d), vals.dtype).at[idx.reshape(-1)].add(vals.reshape(-1, d))
        output = jax.vmap(combine)(token_indices, weighted)
        return output
    h = _L0_tok_ref(x, L0_tok_domain_map, L0_tok_emb_table, L0_tok_W_exp, L0_tok_W_proj)
    h = h + _L0_attn_ref(_layernorm(h, axis=-1), L0_attn_in_proj_weight, L0_attn_in_proj_bias, L0_attn_out_proj_weight, L0_attn_out_proj_bias)
    h = h + _L0_ffn_ref(_layernorm(h, axis=-1), L0_ffn_gate_w, L0_ffn_gate_b, L0_ffn_sw1, L0_ffn_sb1, L0_ffn_sw2, L0_ffn_sb2, L0_ffn_w1, L0_ffn_b1, L0_ffn_w2, L0_ffn_b2)
    h = h + _L1_attn_ref(_layernorm(h, axis=-1), L1_attn_pos, L1_attn_in_proj_weight, L1_attn_in_proj_bias, L1_attn_pos_proj_weight, L1_attn_pos_proj_bias, L1_attn_out_proj_weight, L1_attn_out_proj_bias, L1_attn_r_w_bias, L1_attn_r_r_bias)
    h = h + _L1_ffn_ref(_layernorm(h, axis=-1), L1_ffn_router_w1, L1_ffn_router_w2, L1_ffn_w1, L1_ffn_w2, L1_ffn_w3)
    return h

_drawn_inputs = setup_inputs


def setup_inputs(seed=0):
    import zlib

    import numpy as np

    out = dict(_drawn_inputs(seed))
    spreads = {'L0_attn_in_proj_bias': (0.0, 0.1),
     'L0_attn_out_proj_bias': (0.0, 0.1),
     'L0_ffn_gate_b': (0.0, 0.1),
     'L0_ffn_sb1': (0.0, 0.1),
     'L0_ffn_sb2': (0.0, 0.1),
     'L0_ffn_b1': (0.0, 0.719),
     'L0_ffn_b2': (0.0, 0.1),
     'L1_attn_in_proj_bias': (0.0, 0.1),
     'L1_attn_pos_proj_bias': (0.0, 0.8),
     'L1_attn_out_proj_bias': (0.0, 0.1)}
    factors = {'L0_tok_W_exp': 8.0,
     'L0_tok_W_proj': 8.0,
     'L1_attn_r_w_bias': 8.0,
     'L1_attn_r_r_bias': 8.0,
     'L1_ffn_router_w1': 8.0,
     'L1_ffn_router_w2': 8.0,
     'L1_ffn_w1': 8.0,
     'L1_ffn_w2': 8.0,
     'L1_ffn_w3': 8.0}
    for name, (base, spread) in spreads.items():
        noise = np.random.default_rng([zlib.crc32(name.encode()), seed]).standard_normal(out[name].shape)
        drawn = base * np.exp(spread * noise) if base else spread * noise
        out[name] = jnp.asarray(drawn.astype(out[name].dtype))
    for name, factor in factors.items():
        out[name] = (out[name] * factor).astype(out[name].dtype)
    return out
```

```python
from contextlib import ExitStack

import concourse.bass as bass
import numpy as np
from concourse import mybir

F32 = mybir.dt.float32
F32R = mybir.dt.float32r
BF16 = mybir.dt.bfloat16
I32 = mybir.dt.int32
U32 = mybir.dt.uint32
ALU = mybir.AluOpType
ACT = mybir.ActivationFunctionType
X = mybir.AxisListType.X

P = 128
S = 16
F = 256
K = F // P
T = S * P
GB = P // S
NG = P // GB
BANK = 512
CH = T // BANK
EPS = 1e-5

NDOM, DEXP = 8, 32

H0, D0 = 16, 64
PAIRS = H0 // 2
VW0 = D0 + 1

E0, FF0 = 8, 256

H1, D1 = 16, 16
HG = 4
VW1 = D1 + 1
NPOS = 2 * S - 1

E1, FF1, CAP = 16, 512, 64
RH = 128
M1 = FF1 // P


def wait(engine, sem, value):
    if isinstance(value, int) and value <= 0:
        return
    engine.wait_ge(sem, value)


def three(hi_l, lo_l, hi_r, lo_r):
    return [(hi_l, hi_r), (hi_l, lo_r), (lo_l, hi_r)]


def accumulate(pe, out, pairs, first=True, last=True):
    for n, (lhs, rhs) in enumerate(pairs):
        mm = pe.matmul(out, lhs, rhs, start=first and n == 0, stop=last and n == len(pairs) - 1)
    return mm


class Chain:

    def __init__(self, engine, sem):
        self.engine, self.sem, self.n = engine, sem, 0

    def __call__(self, ins):
        self.n += 1
        ins.then_inc(self.sem, 1)
        self.engine.wait_ge(self.sem, self.n)


def group_view(x):
    return x.rearrange("p k (g t c) -> p k g t c", t=S, c=GB)


class Space:

    def __init__(self, nc, ctx, stage):
        self.nc, self.ctx, self.stage, self.sems = nc, ctx, stage, []

    def sb(self, name, shape, dt=F32):
        return self.ctx.enter_context(self.nc.sbuf_tensor(f"{self.stage}_{name}", shape, dt))

    def ps(self, name, shape, dt=F32):
        return self.ctx.enter_context(self.nc.psum_tensor(f"{self.stage}_{name}", shape, dt))

    def sem(self, name):
        self.sems.append(self.nc.alloc_semaphore(f"{self.stage}_{name}"))
        return self.sems[-1]

    def close(self):
        self.nc.clear_and_free_semaphores(self.sems)
        self.nc.all_engine_barrier()


def build_constants(nc, c):
    with ExitStack() as ctx:
        sp = Space(nc, ctx, "const")
        written = sp.sem("written")
        filled = sp.sem("filled")
        diag = sp.sem("diag")
        block = ctx.enter_context(nc.Block())

        @block.gpsimd
        def _(pool):
            pool.memset(c["ident"][:], 0.0).then_inc(filled, 1)
            pool.wait_ge(filled, 1)
            pool.affine_select(out=c["ident"][:], in_=c["ident"][:], compare_op=ALU.not_equal, fill=1.0,
                               base=0, pattern=[[-1, P]], channel_multiplier=1).then_inc(diag, 1)
            pool.iota(c["iota_p"][:], pattern=[[1, P]], base=0, channel_multiplier=0,
                      allow_small_or_imprecise_dtypes=True).then_inc(diag, 1)
            pool.iota(c["block_i"][:], pattern=[[0, S], [1, GB]], base=P, channel_multiplier=-1)\
                .then_inc(diag, 1)

        @block.vector
        def _(dve):
            dve.wait_ge(diag, 3)
            dve.tensor_copy(c["ident_b"][:], c["ident"][:]).then_inc(written, 1)
            dve.tensor_single_scalar(c["block_i"][:], c["block_i"][:], GB - 1, op=ALU.bitwise_and)\
                .then_inc(written, 1)
            dve.wait_ge(written, 2)
            dve.tensor_copy(c["block_f"][:], c["block_i"][:]).then_inc(written, 1)
            dve.wait_ge(written, 3)
            dve.tensor_scalar(c["mask"][:], c["block_f"][:], 0.0, -1e30, ALU.not_equal, ALU.mult)\
                .then_inc(written, 1)
    sp.close()


def build_tokens(nc, c, h, ids_d, dmap_d, emb_d, wexp_d, wproj_d):
    with ExitStack() as ctx:
        sp = Space(nc, ctx, "tok")
        ids = sp.sb("ids", [P, S], I32)
        dom = sp.sb("dom", [P, S], I32)
        dom_f = sp.sb("dom_f", [P, S])
        keep = sp.sb("keep", [P, S, NDOM])
        wexp = sp.sb("wexp", [P, K, F])
        wproj = sp.sb("wproj", [P, K, F])
        base_t = [sp.sb(f"base_t{i}", [P, K, P]) for i in range(2)]
        kept = [sp.sb(f"kept{i}", [P, F]) for i in range(2)]
        kept_t = [sp.sb(f"kept_t{i}", [P, K, P]) for i in range(2)]
        p_base = [sp.ps(f"p_base{i}", [P, BANK]) for i in range(2)]
        p_exp = [sp.ps(f"p_exp{i}", [P, BANK]) for i in range(2)]
        p_kept = [sp.ps(f"p_kept{i}", [P, BANK]) for i in range(2)]
        p_corr = [sp.ps(f"p_corr{i}", [P, BANK]) for i in range(2)]
        ids_in, w_in = sp.sem("ids_in"), sp.sem("w_in")
        row_in = [sp.sem(f"row_in{s}") for s in range(S)]
        dom_ok, keep_ok = sp.sem("dom_ok"), sp.sem("keep_ok")
        base_turned, base_copied = sp.sem("base_turned"), sp.sem("base_copied")
        expanded, masked = sp.sem("expanded"), sp.sem("masked")
        kept_turned, kept_copied = sp.sem("kept_turned"), sp.sem("kept_copied")
        corrected, added = sp.sem("corrected"), sp.sem("added")
        block = ctx.enter_context(nc.Block())

        @block.sync
        def _(sync):
            sync.dma_start(ids[:], ids_d).then_inc(ids_in, 16)
            sync.dma_start(wexp[:], wexp_d).then_inc(w_in, 16)
            sync.dma_start(wproj[:], wproj_d).then_inc(w_in, 16)

        @block.gpsimd
        def _(pool):
            pool.wait_ge(ids_in, 16)
            for s in range(S):
                at = bass.IndirectOffsetOnAxis(ap=ids[:, s:s + 1].bitcast(U32), axis=0)
                pool.indirect_dma_start(out=h[:, s, :], out_offset=None, in_=emb_d, in_offset=at)\
                    .then_inc(row_in[s], 16)
                pool.indirect_dma_start(out=dom[:, s:s + 1], out_offset=None, in_=dmap_d, in_offset=at)\
                    .then_inc(row_in[s], 16)

        @block.tensor
        def _(pe):
            pe.wait_ge(w_in, 32)
            for t in range(S + 3):
                if t < S:
                    pe.wait_ge(row_in[t], 32)
                    wait(pe, base_copied, t - 1)
                    for k in range(K):
                        mm = pe.transpose(p_base[t % 2][:, k * P:(k + 1) * P], h[:, t, k * P:(k + 1) * P],
                                          c["ident"][:])
                    mm.then_inc(base_turned, 1)
                if 0 <= t - 1 < S:
                    s = t - 1
                    pe.wait_ge(base_copied, s + 1)
                    wait(pe, masked, s - 1)
                    accumulate(pe, p_exp[s % 2][:, 0:F],
                               [(base_t[s % 2][:, k, :], wexp[:, k, :]) for k in range(K)]).then_inc(expanded, 1)
                if 0 <= t - 2 < S:
                    s = t - 2
                    pe.wait_ge(masked, s + 1)
                    wait(pe, kept_copied, s - 1)
                    for k in range(K):
                        mm = pe.transpose(p_kept[s % 2][:, k * P:(k + 1) * P],
                                          kept[s % 2][:, k * P:(k + 1) * P], c["ident"][:])
                    mm.then_inc(kept_turned, 1)
                if 0 <= t - 3 < S:
                    s = t - 3
                    pe.wait_ge(kept_copied, s + 1)
                    wait(pe, added, s - 1)
                    accumulate(pe, p_corr[s % 2][:, 0:F],
                               [(kept_t[s % 2][:, k, :], wproj[:, k, :]) for k in range(K)]).then_inc(corrected, 1)

        @block.scalar
        def _(act):
            for t in range(S + 2):
                if t < S:
                    act.wait_ge(base_turned, t + 1)
                    wait(act, expanded, t - 1)
                    act.copy(base_t[t % 2][:], p_base[t % 2][:, 0:F]
                             .rearrange("p (k c) -> p k c", k=K)).then_inc(base_copied, 1)
                if t >= 2:
                    s = t - 2
                    act.wait_ge(kept_turned, s + 1)
                    wait(act, corrected, s - 1)
                    act.copy(kept_t[s % 2][:], p_kept[s % 2][:, 0:F]
                             .rearrange("p (k c) -> p k c", k=K)).then_inc(kept_copied, 1)

        @block.vector
        def _(dve):
            for t in range(S + 3):
                if t < S:
                    dve.wait_ge(row_in[t], 32)
                    dve.tensor_copy(dom_f[:, t:t + 1], dom[:, t:t + 1]).then_inc(dom_ok, 1)
                    dve.wait_ge(dom_ok, t + 1)
                    dve.tensor_scalar(keep[:, t, :], c["iota_p"][:, 0:NDOM], dom_f[:, t:t + 1], 0.1,
                                      ALU.is_equal, ALU.mult).then_inc(keep_ok, 1)
                if 0 <= t - 1 < S:
                    s = t - 1
                    dve.wait_ge(expanded, s + 1)
                    dve.wait_ge(keep_ok, s + 1)
                    wait(dve, kept_turned, s - 1)
                    dve.tensor_tensor(kept[s % 2][:].rearrange("p (d e) -> p d e", e=DEXP),
                                      p_exp[s % 2][:, 0:F].rearrange("p (d e) -> p d e", e=DEXP),
                                      keep[:, s, :].unsqueeze(2).to_broadcast([P, NDOM, DEXP]),
                                      ALU.mult).then_inc(masked, 1)
                if t >= 3:
                    s = t - 3
                    dve.wait_ge(corrected, s + 1)
                    dve.tensor_tensor(h[:, s, :], h[:, s, :], p_corr[s % 2][:, 0:F], ALU.add)\
                        .then_inc(added, 1)
    sp.close()


class Norm:

    def __init__(self, sp, c, h, x_hi, x_lo, grouped, bank, keep=None):
        self.c, self.h, self.x_hi, self.x_lo, self.grouped, self.keep = c, h, x_hi, x_lo, grouped, keep
        self.stats = sp.sb("ln_stats", [P, S, 6])
        self.mv = sp.sb("ln_mv", [P, S, 2])
        self.var = sp.sb("ln_var", [P, S])
        self.std = sp.sb("ln_std", [P, S])
        self.rstd = sp.sb("ln_rstd", [P, S])
        self.xn = sp.sb("ln_xn", [P, 4, F])
        self.bank = bank
        self.stats_ok, self.mv_ok, self.var_ok = sp.sem("ln_stats_ok"), sp.sem("ln_mv_ok"), sp.sem("ln_var_ok")
        self.std_ok, self.rstd_ok = sp.sem("ln_std_ok"), sp.sem("ln_rstd_ok")
        self.xn_ok, self.turned = sp.sem("ln_xn_ok"), sp.sem("ln_turned")
        self.hi_ok, self.lo_ok = sp.sem("ln_hi_ok"), sp.sem("ln_lo_ok")
        if keep:
            self.rest = sp.sb("ln_rest", [P, 4, F])
            self.kept, self.rest_ok, self.kept3 = sp.sem("ln_kept"), sp.sem("ln_rest_ok"), sp.sem("ln_kept3")

    def columns(self, x, s):
        if self.grouped:
            return group_view(x)[:, :, :, s, :]
        return x[:, :, s * P:(s + 1) * P].rearrange("p k (g c) -> p k g c", c=GB)

    def turned_bank(self, s):
        return self.bank[s % 2][:, 0:F].rearrange("p (k g c) -> p k g c", k=K, c=GB)

    def vector(self, dve):
        for s in range(S):
            dve.bn_stats(self.stats[:, s, :], self.h[:, s, :]).then_inc(self.stats_ok, 1)
        for s in range(S):
            dve.wait_ge(self.stats_ok, s + 1)
            dve.bn_aggr(self.mv[:, s, :], self.stats[:, s, :]).then_inc(self.mv_ok, 1)
        dve.wait_ge(self.mv_ok, S)
        dve.tensor_scalar_add(self.var[:], self.mv[:, :, 1], EPS).then_inc(self.var_ok, 1)
        dve.wait_ge(self.std_ok, 1)
        dve.reciprocal(self.rstd[:], self.std[:]).then_inc(self.rstd_ok, 1)
        dve.wait_ge(self.rstd_ok, 1)
        for s in range(S + 1):
            if s < S:
                wait(dve, self.turned, s - 3)
                if self.keep:
                    wait(dve, self.rest_ok, s - 3)
                dve.tensor_scalar(self.xn[:, s % 4, :], self.h[:, s, :], self.mv[:, s, 0:1],
                                  self.rstd[:, s:s + 1], ALU.subtract, ALU.mult).then_inc(self.xn_ok, 1)
            if s >= 1:
                z = s - 1
                dve.wait_ge(self.hi_ok, z + 1)
                dve.tensor_tensor(self.columns(self.x_lo, z), self.turned_bank(z),
                                  self.columns(self.x_hi, z).bitcast(F32), ALU.subtract)\
                    .then_inc(self.lo_ok, 1)
                if self.keep and z >= 2:
                    self.third(dve, z - 2)
        if self.keep:
            for z in (S - 2, S - 1):
                self.third(dve, z)

    def third(self, dve, s):
        dve.wait_ge(self.kept, min(2 * s + 3, 2 * S))
        dve.tensor_tensor(self.keep[2][:, s, :], self.rest[:, s % 4, :], self.keep[1][:, s, :], ALU.subtract)\
            .then_inc(self.kept3, 1)

    def second(self, act, s):
        act.wait_ge(self.rest_ok, s + 1)
        act.copy(self.keep[1][:, s, :], self.rest[:, s % 4, :]).then_inc(self.kept, 1)

    def gpsimd(self, pool):
        for s in range(S):
            pool.wait_ge(self.kept, 2 * s + 1 if s == 0 else 2 * s)
            wait(pool, self.kept3, s - 3)
            pool.tensor_tensor(self.rest[:, s % 4, :], self.xn[:, s % 4, :], self.keep[0][:, s, :], ALU.subtract)\
                .then_inc(self.rest_ok, 1)

    def scalar(self, act):
        act.wait_ge(self.var_ok, 1)
        act.activation(self.std[:], self.var[:], ACT.Sqrt).then_inc(self.std_ok, 1)
        for s in range(S):
            act.wait_ge(self.turned, s + 1)
            act.copy(self.columns(self.x_hi, s), self.turned_bank(s)).then_inc(self.hi_ok, 1)
            if self.keep:
                act.copy(self.keep[0][:, s, :], self.xn[:, s % 4, :]).then_inc(self.kept, 1)
                if s >= 1:
                    self.second(act, s - 1)
        if self.keep:
            self.second(act, S - 1)

    def tensor(self, pe):
        for s in range(S):
            pe.wait_ge(self.xn_ok, s + 1)
            wait(pe, self.lo_ok, s - 1)
            for k in range(K):
                mm = pe.transpose(self.bank[s % 2][:, k * P:(k + 1) * P],
                                  self.xn[:, s % 4, k * P:(k + 1) * P], self.c["ident"][:])
            mm.then_inc(self.turned, 1)


def build_attention0(nc, c, h, w_d, bqk_d, bv_d, wo_d, bo_d):
    with ExitStack() as ctx:
        sp = Space(nc, ctx, "a0")
        x_hi, x_lo = sp.sb("x_hi", [P, K, T], F32R), sp.sb("x_lo", [P, K, T], F32R)
        w_raw = [sp.sb(f"w_raw{i}", [P, K, 3 * P]) for i in range(2)]
        w_hi, w_lo = sp.sb("w_hi", [P, K, 3 * P], F32R), sp.sb("w_lo", [P, K, 3 * P], F32R)
        bqk = sp.sb("bqk", [P, PAIRS, 2])
        bias = sp.sb("bias", [P, 2])
        bv = sp.sb("bv", [P, H0 * D0])
        bo = sp.sb("bo", [P, F])
        wo = sp.sb("wo", [P, PAIRS, F])
        wo_hi, wo_lo = sp.sb("wo_hi", [P, F], F32R), sp.sb("wo_lo", [P, F], F32R)
        q_k = [sp.sb(f"q_k{i}", [P, 2, T]) for i in range(2)]
        v = [sp.sb(f"v{i}", [P, NG, 2, VW0]) for i in range(2)]
        prob = [sp.sb(f"prob{i}", [P, 4, P]) for i in range(4)]
        prob_t = [sp.sb(f"prob_t{i}", [P, 4, P]) for i in range(2)]
        top = [sp.sb(f"top{i}", [P, 4]) for i in range(2)]
        inv = [sp.sb(f"inv{i}", [P, 4]) for i in range(2)]
        o = [sp.sb(f"o{i}", [P, NG, P]) for i in range(2)]
        ot_hi, ot_lo = sp.sb("ot_hi", [P, T], F32R), sp.sb("ot_lo", [P, T], F32R)
        p_s = [sp.ps(f"p_s{i}", [P, BANK]) for i in range(2)]
        p_t, p_o = sp.ps("p_t", [P, BANK]), sp.ps("p_o", [P, BANK])
        p_qk, p_v = sp.ps("p_qk", [P, BANK]), sp.ps("p_v", [P, BANK])
        p_out = [sp.ps(f"p_out{i}", [P, BANK]) for i in range(2)]
        norm = Norm(sp, c, h, x_hi, x_lo, True, p_out)

        w_in = [sp.sem(f"w_in{i}") for i in range(2)]
        small_in, ones_ok, bo_ok = sp.sem("small_in"), sp.sem("ones_ok"), sp.sem("bo_ok")
        bias_ok = sp.sem("bias_ok")
        w_hi_ok, w_lo_ok = sp.sem("w_hi_ok"), sp.sem("w_lo_ok")
        wo_hi_ok, wo_lo_ok = sp.sem("wo_hi_ok"), sp.sem("wo_lo_ok")
        qk_made, qk_copied = sp.sem("qk_made"), sp.sem("qk_copied")
        v_made, v_copied = sp.sem("v_made"), sp.sem("v_copied")
        scored, top_ok, shifted, exped = sp.sem("scored"), sp.sem("top_ok"), sp.sem("shifted"), sp.sem("exped")
        turned, t_copied = sp.sem("turned"), sp.sem("t_copied")
        valued, inv_ok, o_ok = sp.sem("valued"), sp.sem("inv_ok"), sp.sem("o_ok")
        o_turned, ot_hi_ok, ot_lo_ok = sp.sem("o_turned"), sp.sem("ot_hi_ok"), sp.sem("ot_lo_ok")
        out_made, out_added = sp.sem("out_made"), sp.sem("out_added")
        block = ctx.enter_context(nc.Block())

        def run(engine, unit):
            unit(-1, 1, project=True, attend=False, finish=False)
            unit(0, 0, project=True, attend=True, finish=False)
            unit(1, 1, project=True, attend=True, finish=True)
            with engine.Fori(1, PAIRS // 2 - 1) as i:
                unit(2 * i, 0, project=True, attend=True, finish=True)
                unit(2 * i + 1, 1, project=True, attend=True, finish=True)
            unit(PAIRS - 2, 0, project=True, attend=True, finish=True)
            unit(PAIRS - 1, 1, project=False, attend=True, finish=True)
            unit(PAIRS, 0, project=False, attend=False, finish=True)

        def turns(j, attend, finish):
            return (attend and j >= 2) or (finish and j < 2)

        def values(j, attend, finish):
            return (attend and j >= 3) or (finish and j < 3)

        def ungrouped(x, j):
            return x[:].rearrange("p (t g c) -> p g t c", t=S, g=NG)[:, 4 * j:4 * j + 4, :, :]

        def out_view(bank):
            return bank[:].rearrange("p (g t c) -> p g t c", t=S, c=GB)

        @block.sync
        def _(sync):
            for p in range(2):
                sync.dma_start(w_raw[p][:], w_d[p]).then_inc(w_in[p], 16)
            for dst, src in ((bqk[:], bqk_d), (bv[:], bv_d[0:1].partition_broadcast(P)),
                             (bo[:], bo_d[0:1].partition_broadcast(P)), (wo[:], wo_d)):
                sync.dma_start(dst, src).then_inc(small_in, 16)
            for p in range(2, PAIRS):
                sync.wait_ge(w_lo_ok, p - 1)
                sync.dma_start(w_raw[p % 2][:], w_d[p]).then_inc(w_in[p % 2], 16)

        @block.gpsimd
        def _(pool):
            for i in range(2):
                pool.memset(v[i][:, :, :, D0:VW0], 1.0).then_inc(ones_ok, 1)
            pool.wait_ge(norm.xn_ok, S)
            pool.wait_ge(small_in, 64)
            for s in range(S):
                pool.tensor_tensor(h[:, s, :], h[:, s, :], bo[:], ALU.add).then_inc(bo_ok, 1)

        @block.tensor
        def _(pe):
            norm.tensor(pe)
            pe.wait_ge(norm.lo_ok, S)
            pe.wait_ge(ones_ok, 2)

            def project_qk(p, j):
                pe.wait_ge(w_lo_ok, p + 1)
                wait(pe, qk_copied, 8 * p + j)
                cols = slice((j // 4) * P, (j // 4 + 1) * P)
                toks = slice((j % 4) * BANK, (j % 4 + 1) * BANK)
                accumulate(pe, p_qk[:], [t for k in range(K) for t in three(
                    w_hi[:, k, cols], w_lo[:, k, cols], x_hi[:, k, toks], x_lo[:, k, toks])]).then_inc(qk_made, 1)

            def project_v(p, j):
                wait(pe, v_copied, 8 * p + j)
                for g in range(2):
                    toks = slice((2 * j + g) * P, (2 * j + g + 1) * P)
                    mm = accumulate(pe, p_v[:, g * P:(g + 1) * P], [t for k in range(K) for t in three(
                        x_hi[:, k, toks], x_lo[:, k, toks], w_hi[:, k, 2 * P:], w_lo[:, k, 2 * P:])])
                mm.then_inc(v_made, 1)

            def project_out(p, q):
                pe.wait_ge(ot_lo_ok, 4 * p + 4)
                pe.wait_ge(wo_lo_ok, p + 1)
                if q >= 2:
                    pe.wait_ge(out_added, 8 * p + q - 1)
                for t in range(2):
                    toks = slice((2 * q + t) * P, (2 * q + t + 1) * P)
                    mm = accumulate(pe, p_out[q % 2][:, t * F:(t + 1) * F],
                                    three(ot_hi[:, toks], ot_lo[:, toks], wo_hi[:], wo_lo[:]))
                mm.then_inc(out_made, 1)

            def unit(p, par, project, attend, finish):
                for j in range(8):
                    g = 8 * p + j
                    if turns(j, attend, finish):
                        pe.wait_ge(exped, g - 1)
                        wait(pe, t_copied, g - 2)
                        for n in range(4):
                            mm = pe.transpose(p_t[:, n * P:(n + 1) * P], prob[(j - 2) % 4][:, n, :], c["ident"][:])
                        mm.then_inc(turned, 1)
                    if values(j, attend, finish):
                        jj, vp = (j - 3) % 8, par if j >= 3 else 1 - par
                        pe.wait_ge(t_copied, g - 2)
                        pe.wait_ge(v_copied, 8 * p + (8 if j >= 3 else 0))
                        wait(pe, o_ok, g - 3)
                        for n in range(4):
                            mm = pe.matmul(p_o[:, n * VW0:(n + 1) * VW0], prob_t[jj % 2][:, n, :],
                                           v[vp][:, 4 * (jj % 4) + n, jj // 4, :], start=True, stop=True)
                        mm.then_inc(valued, 1)
                    if finish and j < 4:
                        pe.wait_ge(o_ok, 8 * p - 3 + j)
                        if j < 2:
                            wait(pe, out_added, 8 * p - 8)
                        else:
                            pe.wait_ge(ot_lo_ok, 4 * p - 4 + j - 1)
                        for n in range(4):
                            mm = pe.transpose(p_out[j % 2][:, n * P:(n + 1) * P], o[1 - par][:, 4 * j + n, :],
                                              c["ident"][:])
                        mm.then_inc(o_turned, 1)
                    if attend:
                        rows = slice((j // 4) * D0, (j // 4 + 1) * D0)
                        pe.wait_ge(qk_copied, 8 * p + 8)
                        wait(pe, shifted, g - 1)
                        pe.matmul(p_s[j % 2][:], c["ident_b"][:], c["mask"][:].unsqueeze(1).to_broadcast([P, 4, P]),
                                  start=True, stop=False, skip_group_check=True)
                        for n in range(4):
                            toks = slice((4 * (j % 4) + n) * P, (4 * (j % 4) + n + 1) * P)
                            mm = pe.matmul(p_s[j % 2][:, n * P:(n + 1) * P], q_k[par][rows, 0, toks],
                                           q_k[par][rows, 1, toks], start=False, stop=n == 3,
                                           skip_group_check=True)
                        mm.then_inc(scored, 1)
                    if project:
                        project_qk(p + 1, j)
                    if finish and j >= 4:
                        project_out(p - 1, 2 * (j - 4))
                    if project:
                        project_v(p + 1, j)
                    if finish and j >= 4:
                        project_out(p - 1, 2 * (j - 4) + 1)

            run(pe, unit)

        @block.scalar
        def _(act):
            norm.scalar(act)
            act.wait_ge(small_in, 64)

            def unit(p, par, project, attend, finish):
                if project:
                    act.wait_ge(w_in[1 - par], 8 * (p + 1 - (1 - par)) + 16)
                    wait(act, v_made, 8 * (p + 1))
                    wait(act, qk_copied, 8 * (p + 1))
                    act.copy(w_hi[:], w_raw[1 - par][:]).then_inc(w_hi_ok, 1)
                    act.copy(bias[:], bqk[:, p + 1, :] if isinstance(p, int) else
                             bqk[:, bass.ds(p + 1, 1), :].squeeze(1)).then_inc(bias_ok, 1)
                for j in range(8):
                    g = 8 * p + j
                    if turns(j, attend, finish):
                        act.wait_ge(turned, g - 1)
                        wait(act, valued, g - 3)
                        act.copy(prob_t[j % 2][:], p_t[:].rearrange("p (n c) -> p n c", n=4))\
                            .then_inc(t_copied, 1)
                    if finish and j < 4:
                        act.wait_ge(o_turned, 4 * p - 4 + j + 1)
                        wait(act, out_made, 8 * p - 8)
                        act.copy(ungrouped(ot_hi, j), out_view(p_out[j % 2])).then_inc(ot_hi_ok, 1)
                    if finish and j == 2:
                        act.copy(wo_hi[:], wo[:, p - 1, :] if isinstance(p, int) else
                                 wo[:, bass.ds(p - 1, 1), :].squeeze(1)).then_inc(wo_hi_ok, 1)
                    if attend:
                        act.wait_ge(shifted, g + 1)
                        act.activation(prob[j % 4][:], prob[j % 4][:], ACT.Exp, scale=float(D0) ** -0.5)\
                            .then_inc(exped, 1)
                    if project:
                        act.wait_ge(qk_made, 8 * (p + 1) + j + 1)
                        wait(act, scored, 8 * p)
                        if j == 0:
                            act.wait_ge(bias_ok, p + 2)
                        act.activation(q_k[1 - par][:, j // 4, (j % 4) * BANK:(j % 4 + 1) * BANK], p_qk[:],
                                       ACT.Identity, bias=bias[:, j // 4:j // 4 + 1]).then_inc(qk_copied, 1)

            run(act, unit)

        @block.vector
        def _(dve):
            norm.vector(dve)
            dve.wait_ge(small_in, 64)

            def copy_v(p, par, j):
                dve.wait_ge(v_made, 8 * p + j + 1)
                wait(dve, valued, 8 * p - 11 + j // 2)
                b = bv[:, bass.ds(p * P, P)] if not isinstance(p, int) else bv[:, p * P:(p + 1) * P]
                dve.tensor_tensor(v[par][:, 2 * j:2 * j + 2, :, 0:D0],
                                  p_v[:, 0:2 * P].rearrange("p (g e d) -> p g e d", g=2, e=2),
                                  b.rearrange("p (e d) -> p e d", e=2).unsqueeze(1).to_broadcast([P, 2, 2, D0]),
                                  ALU.add).then_inc(v_copied, 1)

            def unit(p, par, project, attend, finish):
                if project:
                    dve.wait_ge(w_hi_ok, p + 2)
                    dve.tensor_tensor(w_lo[:], w_raw[1 - par][:], w_hi[:].bitcast(F32), ALU.subtract)\
                        .then_inc(w_lo_ok, 1)
                for j in range(8):
                    g = 8 * p + j
                    if values(j, attend, finish):
                        jj, op = (j - 3) % 8, par if j >= 3 else 1 - par
                        dve.wait_ge(valued, g - 2)
                        if j == 3:
                            wait(dve, o_turned, 4 * p - 4)
                        po = p_o[:, 0:4 * VW0].rearrange("p (n d) -> p n d", n=4)
                        dve.reciprocal(inv[j % 2][:], po[:, :, D0]).then_inc(inv_ok, 1)
                        dve.wait_ge(inv_ok, g - 2)
                        dve.tensor_tensor(o[op][:, 4 * (jj % 4):4 * (jj % 4) + 4, (jj // 4) * D0:(jj // 4 + 1) * D0],
                                          po[:, :, 0:D0], inv[j % 2][:].unsqueeze(2).to_broadcast([P, 4, D0]),
                                          ALU.mult).then_inc(o_ok, 1)
                    if attend:
                        ps = p_s[j % 2][:].rearrange("p (n c) -> p n c", n=4)
                        dve.wait_ge(scored, g + 1)
                        dve.tensor_reduce(top[j % 2][:], ps, axis=X, op=ALU.max).then_inc(top_ok, 1)
                        dve.wait_ge(top_ok, g + 1)
                        wait(dve, turned, g - 3)
                        dve.tensor_tensor(prob[j % 4][:], ps, top[j % 2][:].unsqueeze(2).to_broadcast([P, 4, P]),
                                          ALU.subtract).then_inc(shifted, 1)
                    if finish and j < 4:
                        dve.wait_ge(ot_hi_ok, 4 * p - 4 + j + 1)
                        dve.tensor_tensor(ungrouped(ot_lo, j), out_view(p_out[j % 2]),
                                          ungrouped(ot_hi, j).bitcast(F32), ALU.subtract)\
                            .then_inc(ot_lo_ok, 1)
                    if finish and j == 2:
                        w = wo[:, p - 1, :] if isinstance(p, int) else wo[:, bass.ds(p - 1, 1), :].squeeze(1)
                        dve.wait_ge(wo_hi_ok, p)
                        dve.tensor_tensor(wo_lo[:], w, wo_hi[:].bitcast(F32), ALU.subtract).then_inc(wo_lo_ok, 1)
                    if project:
                        copy_v(p + 1, 1 - par, j)
                    if finish and j >= 4:
                        for q in (2 * (j - 4), 2 * (j - 4) + 1):
                            dve.wait_ge(out_made, 8 * p - 8 + q + 1)
                            dve.wait_ge(bo_ok, S)
                            dve.tensor_tensor(h[:, 2 * q:2 * q + 2, :], h[:, 2 * q:2 * q + 2, :],
                                              p_out[q % 2][:].rearrange("p (t f) -> p t f", t=2), ALU.add)\
                                .then_inc(out_added, 1)

            run(dve, unit)
    sp.close()


def build_ffn0(nc, c, h, gate_d, gate_b_d, w_d, b1_d, b2_d):
    NE = E0 + 1
    with ExitStack() as ctx:
        sp = Space(nc, ctx, "f0")
        x_hi, x_lo = sp.sb("x_hi", [P, K, T], F32R), sp.sb("x_lo", [P, K, T], F32R)
        gate = sp.sb("gate", [P, K, E0])
        gate_hi, gate_lo = sp.sb("gate_hi", [P, K, E0], F32R), sp.sb("gate_lo", [P, K, E0], F32R)
        gate_b = sp.sb("gate_b", [P, E0])
        b1 = sp.sb("b1", [P, NE, K])
        b1_now = [sp.sb(f"b1_now{i}", [P, K]) for i in range(2)]
        b2 = sp.sb("b2", [NE, F])
        logit, prob = sp.sb("logit", [P, S, E0]), sp.sb("prob", [P, S, E0])
        row = sp.sb("row", [P, S])
        best, best_i = sp.sb("best", [P, S, 8]), sp.sb("best_i", [P, S, 8], U32)
        best_f, pick = sp.sb("best_f", [P, S, 8]), sp.sb("pick", [P, S, E0])
        combine = sp.sb("combine", [P, S, NE])
        combine_t = sp.sb("combine_t", [NE, T])
        w_raw = [sp.sb(f"w_raw{i}", [P, 2, K, F]) for i in range(2)]
        w_hi = [sp.sb(f"w_hi{i}", [P, 2, K, F], F32R) for i in range(2)]
        w_lo = [sp.sb(f"w_lo{i}", [P, 2, K, F], F32R) for i in range(2)]
        hid = [sp.sb(f"hid{i}", [P, K, BANK]) for i in range(2)]
        hid_hi = [sp.sb(f"hid_hi{i}", [P, K, BANK], F32R) for i in range(2)]
        hid_lo = [sp.sb(f"hid_lo{i}", [P, K, BANK], F32R) for i in range(2)]
        p_hid = [[sp.ps(f"p_hid{i}{m}", [P, BANK]) for m in range(K)] for i in range(2)]
        p_y = [sp.ps(f"p_y{i}", [P, BANK]) for i in range(2)]
        p_misc = [sp.ps(f"p_misc{i}", [P, BANK]) for i in range(2)]
        norm = Norm(sp, c, h, x_hi, x_lo, False, p_misc)

        w_in = [sp.sem(f"w_in{i}") for i in range(2)]
        small_in, one_ok = sp.sem("small_in"), sp.sem("one_ok")
        gate_hi_ok, gate_lo_ok = sp.sem("gate_hi_ok"), sp.sem("gate_lo_ok")
        logits_made, gate_shifted, gate_exped = sp.sem("logits_made"), sp.sem("gate_shifted"), sp.sem("gate_exped")
        gate_chain, combine_ok = sp.sem("gate_chain"), sp.sem("combine_ok")
        combine_turned, combine_copied = sp.sem("combine_turned"), sp.sem("combine_copied")
        w_hi_ok, w_lo_ok, b1_ok = sp.sem("w_hi_ok"), sp.sem("w_lo_ok"), sp.sem("b1_ok")
        hid_made, hid_ok = sp.sem("hid_made"), sp.sem("hid_ok")
        hid_hi_ok, hid_lo_ok = sp.sem("hid_hi_ok"), sp.sem("hid_lo_ok")
        y_made, y_added = sp.sem("y_made"), sp.sem("y_added")
        block = ctx.enter_context(nc.Block())

        def run(engine, expert):
            expert(0, 0, True)
            with engine.Fori(0, (NE - 3) // 2) as i:
                expert(2 * i + 1, 1, True)
                expert(2 * i + 2, 0, True)
            expert(NE - 2, 1, True)
            expert(NE - 1, 0, False)

        @block.sync
        def _(sync):
            for dst, src in ((gate[:], gate_d), (gate_b[:], gate_b_d[0:1].partition_broadcast(P)),
                             (b1[:], b1_d), (b2[:], b2_d)):
                sync.dma_start(dst, src).then_inc(small_in, 16)
            for e in range(NE):
                wait(sync, w_lo_ok, e - 1)
                sync.dma_start(w_raw[e % 2][:], w_d[e]).then_inc(w_in[e % 2], 16)

        @block.gpsimd
        def _(pool):
            pool.memset(combine[:, :, E0:NE], 1.0).then_inc(one_ok, 1)

        @block.tensor
        def _(pe):
            norm.tensor(pe)
            pe.wait_ge(norm.lo_ok, S)
            pe.wait_ge(gate_lo_ok, 1)
            for s in range(S):
                toks = slice(s * P, (s + 1) * P)
                mm = accumulate(pe, p_misc[0][:, s * E0:(s + 1) * E0], [t for k in range(K) for t in three(
                    x_hi[:, k, toks], x_lo[:, k, toks], gate_hi[:, k, :], gate_lo[:, k, :])])
            mm.then_inc(logits_made, 1)

            def hidden(e, par, cc):
                n = 4 * e + cc
                toks = slice(cc * BANK, (cc + 1) * BANK)
                if cc == 0:
                    pe.wait_ge(w_lo_ok, e + 1)
                for m in range(K):
                    wait(pe, hid_hi_ok, 2 * n + m - 3)
                    accumulate(pe, p_hid[cc % 2][m][:], [t for k in range(K) for t in three(
                        w_hi[par][:, 0, k, m * P:(m + 1) * P], w_lo[par][:, 0, k, m * P:(m + 1) * P],
                        x_hi[:, k, toks], x_lo[:, k, toks])]).then_inc(hid_made, 1)

            def output(e, par, cc):
                n = 4 * e + cc
                pe.wait_ge(hid_lo_ok, 2 * n + 2)
                for b in range(2):
                    wait(pe, y_added, 4 * n + 2 * b - 2)
                    for t in range(2):
                        toks = slice((2 * b + t) * P, (2 * b + t + 1) * P)
                        mm = accumulate(pe, p_y[b][:, t * F:(t + 1) * F], [t3 for k in range(K) for t3 in three(
                            hid_hi[cc % 2][:, k, toks], hid_lo[cc % 2][:, k, toks],
                            w_hi[par][:, 1, k, :], w_lo[par][:, 1, k, :])])
                    mm.then_inc(y_made, 1)

            def expert(e, par, more):
                for cc in range(4):
                    if cc < 3:
                        hidden(e, par, cc + 1)
                    elif more:
                        hidden(e + 1, 1 - par, 0)
                    output(e, par, cc)

            hidden(0, 0, 0)
            run(pe, expert)
            pe.wait_ge(combine_ok, 1)
            pe.wait_ge(hid_hi_ok, 8 * NE)
            for i in range(4):
                bank = p_hid[i // 2][i % 2]
                for t in range(4):
                    mm = pe.transpose(bank[0:NE, t * P:(t + 1) * P], combine[:, 4 * i + t, :], c["ident"][:])
                mm.then_inc(combine_turned, 1)
            for i in range(S // 2):
                pe.wait_ge(combine_copied, i // 2 + 1)
                pe.wait_ge(y_added, 16 * NE + 2 * i - 2)
                for t in range(2):
                    toks = slice((2 * i + t) * P, (2 * i + t + 1) * P)
                    mm = pe.matmul(p_y[i % 2][:, t * F:(t + 1) * F], combine_t[:, toks], b2[:], start=True, stop=True)
                mm.then_inc(y_made, 1)

        @block.scalar
        def _(act):
            norm.scalar(act)
            act.wait_ge(small_in, 64)
            act.copy(gate_hi[:], gate[:]).then_inc(gate_hi_ok, 1)

            def cut(e, par):
                act.wait_ge(w_in[par], 8 * (e - par) + 16)
                wait(act, y_made, 8 * (e - 1))
                wait(act, hid_hi_ok, 8 * (e - 1))
                act.copy(w_hi[par][:], w_raw[par][:]).then_inc(w_hi_ok, 1)
                act.copy(b1_now[par][:], b1[:, e, :] if isinstance(e, int) else
                         b1[:, bass.ds(e, 1), :].squeeze(1)).then_inc(b1_ok, 1)

            def gelu(e, par, cc):
                n = 4 * e + cc
                for m in range(K):
                    act.wait_ge(hid_made, 2 * n + m + 1)
                    if cc == 0:
                        act.wait_ge(b1_ok, e + 1)
                    wait(act, hid_lo_ok, 2 * n + m - 3)
                    act.activation(hid[cc % 2][:, m, :], p_hid[cc % 2][m][:], ACT.Gelu,
                                   bias=b1_now[par][:, m:m + 1]).then_inc(hid_ok, 1)
                    wait(act, y_made, 2 * n - 2)
                    act.activation(hid_hi[cc % 2][:, m, :], p_hid[cc % 2][m][:], ACT.Gelu,
                                   bias=b1_now[par][:, m:m + 1]).then_inc(hid_hi_ok, 1)

            def expert(e, par, more):
                for cc in range(4):
                    if cc == 1 and more:
                        cut(e + 1, 1 - par)
                    if cc < 3:
                        gelu(e, par, cc + 1)
                    elif more:
                        gelu(e + 1, 1 - par, 0)

            act.wait_ge(gate_shifted, 1)
            act.activation(prob[:], prob[:], ACT.Exp).then_inc(gate_exped, 1)
            cut(0, 0)
            gelu(0, 0, 0)
            run(act, expert)
            for i in range(4):
                act.wait_ge(combine_turned, i + 1)
                act.copy(combine_t[:, i * BANK:(i + 1) * BANK], p_hid[i // 2][i % 2][0:NE, :])\
                    .then_inc(combine_copied, 1)

        @block.vector
        def _(dve):
            norm.vector(dve)
            dve.wait_ge(gate_hi_ok, 1)
            dve.tensor_tensor(gate_lo[:], gate[:], gate_hi[:].bitcast(F32), ALU.subtract).then_inc(gate_lo_ok, 1)
            wide = [P, S, E0]
            chain = Chain(dve, gate_chain)
            dve.wait_ge(logits_made, 1)
            dve.wait_ge(small_in, 64)
            chain(dve.tensor_tensor(logit[:], p_misc[0][:, 0:S * E0].rearrange("p (s e) -> p s e", e=E0),
                                    gate_b[:].unsqueeze(1).to_broadcast(wide), ALU.add))
            chain(dve.tensor_reduce(row[:], logit[:], axis=X, op=ALU.max))
            dve.tensor_tensor(prob[:], logit[:], row[:].unsqueeze(2).to_broadcast(wide), ALU.subtract)\
                .then_inc(gate_shifted, 1)
            dve.wait_ge(gate_exped, 1)
            chain(dve.tensor_reduce(row[:], prob[:], axis=X, op=ALU.add))
            chain(dve.reciprocal(row[:], row[:]))
            chain(dve.tensor_tensor(prob[:], prob[:], row[:].unsqueeze(2).to_broadcast(wide), ALU.mult))
            for s in range(S):
                ins = dve.max(best[:, s, :], prob[:, s, :])
                if s < S - 1:
                    ins.then_inc(gate_chain, 1)
                    chain.n += 1
            chain(ins)
            for s in range(S):
                ins = dve.max_index(best_i[:, s, :], best[:, s, :], prob[:, s, :])
                if s < S - 1:
                    ins.then_inc(gate_chain, 1)
                    chain.n += 1
            chain(ins)
            chain(dve.tensor_copy(best_f[:], best_i[:]))
            places = c["iota_p"][:, 0:E0].unsqueeze(1).to_broadcast(wide)
            chain(dve.tensor_tensor(pick[:], places, best_f[:, :, 0:1].to_broadcast(wide), ALU.is_equal))
            chain(dve.tensor_tensor(combine[:, :, 0:E0], pick[:], best[:, :, 0:1].to_broadcast(wide), ALU.mult))
            chain(dve.tensor_tensor(pick[:], places, best_f[:, :, 1:2].to_broadcast(wide), ALU.is_equal))
            chain(dve.tensor_tensor(pick[:], pick[:], best[:, :, 1:2].to_broadcast(wide), ALU.mult))
            dve.wait_ge(one_ok, 1)
            dve.tensor_tensor(combine[:, :, 0:E0], combine[:, :, 0:E0], pick[:], ALU.add).then_inc(combine_ok, 1)
            dve.wait_ge(combine_ok, 1)

            def cut_weights(e, par):
                dve.wait_ge(w_hi_ok, e + 1)
                dve.tensor_tensor(w_lo[par][:], w_raw[par][:], w_hi[par][:].bitcast(F32), ALU.subtract)\
                    .then_inc(w_lo_ok, 1)

            def cut_hidden(e, cc):
                n = 4 * e + cc
                for m in range(K):
                    dve.wait_ge(hid_hi_ok, 2 * n + m + 1)
                    dve.tensor_tensor(hid_lo[cc % 2][:, m, :], hid[cc % 2][:, m, :],
                                      hid_hi[cc % 2][:, m, :].bitcast(F32), ALU.subtract).then_inc(hid_lo_ok, 1)

            def expert(e, par, more):
                for cc in range(4):
                    n = 4 * e + cc
                    if cc == 1 and more:
                        cut_weights(e + 1, 1 - par)
                    if cc < 3:
                        cut_hidden(e, cc + 1)
                    elif more:
                        cut_hidden(e + 1, 0)
                    for t in range(4):
                        s = 4 * cc + t
                        weight = combine[:, s, e:e + 1] if isinstance(e, int) else combine[:, s, bass.ds(e, 1)]
                        dve.wait_ge(y_made, 2 * n + t // 2 + 1)
                        wait(dve, y_added, 4 * n + t - 15)
                        dve.scalar_tensor_tensor(h[:, s, :], p_y[t // 2][:, (t % 2) * F:(t % 2 + 1) * F], weight,
                                                 h[:, s, :], ALU.mult, ALU.add).then_inc(y_added, 1)

            cut_weights(0, 0)
            cut_hidden(0, 0)
            run(dve, expert)
            for i in range(S // 2):
                dve.wait_ge(y_made, 8 * NE + i + 1)
                dve.wait_ge(y_added, 16 * NE - 14 + 2 * i)
                dve.tensor_tensor(h[:, 2 * i:2 * i + 2, :], h[:, 2 * i:2 * i + 2, :],
                                  p_y[i % 2][:].rearrange("p (t f) -> p t f", t=2), ALU.add).then_inc(y_added, 2)
    sp.close()


def build_attention1(nc, c, h, wqk_d, bqk_d, wv_d, bv_d, pos_d, wp_d, bp_d, rw_d, rr_d, wo_d, bo_d):
    STEPS = 4 * HG
    JOBS = 12
    with ExitStack() as ctx:
        sp = Space(nc, ctx, "a1")
        x_hi, x_lo = sp.sb("x_hi", [P, K, T], F32R), sp.sb("x_lo", [P, K, T], F32R)
        wqk = [sp.sb(f"wqk{i}", [P, K, 2, P]) for i in range(2)]
        wqk_hi = [sp.sb(f"wqk_hi{i}", [P, K, 2, P], F32R) for i in range(2)]
        wqk_lo = [sp.sb(f"wqk_lo{i}", [P, K, 2, P], F32R) for i in range(2)]
        bqk = sp.sb("bqk", [P, HG, 2])
        wv, wv_hi, wv_lo = sp.sb("wv", [P, K, F]), sp.sb("wv_hi", [P, K, F], F32R), sp.sb("wv_lo", [P, K, F], F32R)
        wo, wo_hi, wo_lo = sp.sb("wo", [P, K, F]), sp.sb("wo_hi", [P, K, F], F32R), sp.sb("wo_lo", [P, K, F], F32R)
        bv, bo = sp.sb("bv", [P, F]), sp.sb("bo", [P, F])
        pos, wp, bp = sp.sb("pos", [P, K, NPOS + 1]), sp.sb("wp", [P, K, HG, P]), sp.sb("bp", [P, HG])
        rw, rr = sp.sb("rw", [P, HG]), sp.sb("rr", [P, HG])
        bq_rr, rw_rr = sp.sb("bq_rr", [P, HG]), sp.sb("rw_rr", [P, HG])
        p_t = sp.sb("p_t", [P, HG, NPOS + 1])
        shift = [sp.sb(f"shift{i}", [P, S, P]) for i in range(2)]
        hot = sp.sb("hot", [P, P])
        q0 = sp.sb("q_rr", [P, T])
        q = [sp.sb(f"q_all{i}", [P, T]) for i in range(2)]
        k1 = [sp.sb(f"k{i}", [P, T]) for i in range(2)]
        v = sp.sb("v", [P, NG, H1, VW1])
        prob = [sp.sb(f"prob{i}", [P, 4, P]) for i in range(3)]
        prob_t = [sp.sb(f"prob_t{i}", [P, 4, P]) for i in range(2)]
        top = [sp.sb(f"top{i}", [P, 4]) for i in range(2)]
        inv = [sp.sb(f"inv{i}", [P, 4]) for i in range(2)]
        o = sp.sb("o", [P, NG, F])
        p_s = [sp.ps(f"p_s{i}", [P, BANK]) for i in range(2)]
        p_turn, p_o = sp.ps("p_turn", [P, BANK]), sp.ps("p_o", [P, BANK])
        p_work = [sp.ps(f"p_work{i}", [P, BANK]) for i in range(2)]
        p_out = [sp.ps(f"p_out{i}", [P, BANK]) for i in range(2)]
        norm = Norm(sp, c, h, x_hi, x_lo, True, p_out)

        w_in = [sp.sem(f"w_in{i}") for i in range(2)]
        small_in, pool_ok, bo_ok = sp.sem("small_in"), sp.sem("pool_ok"), sp.sem("bo_ok")
        const_hi, const_lo, bias_ok = sp.sem("const_hi"), sp.sem("const_lo"), sp.sem("bias_ok")
        pos_made, pos_ok, shift_ok = sp.sem("pos_made"), sp.sem("pos_ok"), sp.sem("shift_ok")
        w_hi_ok, w_lo_ok = sp.sem("w_hi_ok"), sp.sem("w_lo_ok")
        work_made, work_free = sp.sem("work_made"), [sp.sem(f"work_free{i}") for i in range(2)]
        scored, top_ok, shifted, exped = sp.sem("scored"), sp.sem("top_ok"), sp.sem("shifted"), sp.sem("exped")
        turned, t_copied = sp.sem("turned"), sp.sem("t_copied")
        valued, inv_ok, o_ok = sp.sem("valued"), sp.sem("inv_ok"), sp.sem("o_ok")
        o_turned, ot_hi_ok, ot_lo_ok = sp.sem("o_turned"), sp.sem("ot_hi_ok"), sp.sem("ot_lo_ok")
        out_made, out_added = sp.sem("out_made"), sp.sem("out_added")
        block = ctx.enter_context(nc.Block())
        NV = NG // 2

        def job(u, i):
            return NV + JOBS * u + i

        def steps(step):
            for u in range(-1, HG + 1):
                for j in range(STEPS if u < HG else 4):
                    step(u, j, STEPS * u + j)

        def freed(bank_job):
            return bank_job // 2

        def outs(u, j):
            if u == HG - 1 and 4 <= j < 8:
                return j - 4
            if u == HG and j < 4:
                return 4 + j
            return None

        def out_view(bank):
            return bank[:].rearrange("p (g t c) -> p g t c", t=S, c=GB)

        def ungrouped(x, r):
            return x[:, r // 4, :].rearrange("p (t g c) -> p g t c", t=S, g=NG)[:, 4 * (r % 4):4 * (r % 4) + 4, :, :]

        def at_time(x, t):
            return x[:].rearrange("p (g t c) -> p t g c", t=S, c=GB)[:, t, :, :]

        @block.sync
        def _(sync):
            small = ((bqk[:], bqk_d), (wv[:], wv_d), (wo[:], wo_d), (bv[:], bv_d[0:1].partition_broadcast(P)),
                     (bo[:], bo_d[0:1].partition_broadcast(P)), (pos[:], pos_d), (wp[:], wp_d), (bp[:], bp_d),
                     (rw[:], rw_d), (rr[:], rr_d))
            for dst, src in small:
                sync.dma_start(dst, src).then_inc(small_in, 16)
            for u in range(HG):
                wait(sync, w_lo_ok, u - 1)
                sync.dma_start(wqk[u % 2][:], wqk_d[u]).then_inc(w_in[u % 2], 16)

        N_SMALL = 10 * 16

        @block.gpsimd
        def _(pool):
            chain = Chain(pool, pool_ok)
            chain(pool.memset(hot[:], 0.0))
            for n in range(4):
                rows = slice(32 * n, 32 * n + 32)
                chain(pool.affine_select(out=hot[rows, :].rearrange("p (t c) -> p t c", t=S),
                                         in_=hot[rows, :].rearrange("p (t c) -> p t c", t=S),
                                         compare_op=ALU.not_equal, fill=1.0, base=-D1,
                                         pattern=[[-1, S], [0, GB]], channel_multiplier=1))
            for i in range(2):
                chain(pool.memset(shift[i][:], 0.0))
            chain(pool.memset(v[:, :, :, D1:VW1], 1.0))
            pool.wait_ge(norm.xn_ok, S)
            pool.wait_ge(small_in, N_SMALL)
            for s in range(S):
                pool.tensor_tensor(h[:, s, :], h[:, s, :], bo[:], ALU.add).then_inc(bo_ok, 1)

        POOL_ALL = 8

        @block.tensor
        def _(pe):
            pe.wait_ge(small_in, N_SMALL)
            for u in range(HG):
                mm = accumulate(pe, p_work[0][:, u * (NPOS + 1):(u + 1) * (NPOS + 1)],
                                [(wp[:, k, u, :], pos[:, k, :]) for k in range(K)])
            mm.then_inc(pos_made, 1)
            norm.tensor(pe)
            pe.wait_ge(norm.lo_ok, S)
            pe.wait_ge(pool_ok, POOL_ALL)
            pe.wait_ge(const_lo, 2)
            pe.wait_ge(pos_ok, 1)
            for i in range(NV):
                wait(pe, work_free[i % 2], freed(i))
                for n in range(2):
                    toks = slice((2 * i + n) * P, (2 * i + n + 1) * P)
                    mm = accumulate(pe, p_work[i % 2][:, n * F:(n + 1) * F], [t for k in range(K) for t in three(
                        x_hi[:, k, toks], x_lo[:, k, toks], wv_hi[:, k, :], wv_lo[:, k, :])])
                mm.then_inc(work_made, 1)

            def project(u, i):
                n = job(u, i)
                bank = p_work[n % 2]
                pe.wait_ge(work_free[n % 2], freed(n))
                if i < 4 or i >= 8:
                    a, toks = i // 8, slice((i % 4) * BANK, (i % 4 + 1) * BANK)
                    pe.wait_ge(w_lo_ok, u + 1)
                    mm = accumulate(pe, bank[:], [t for k in range(K) for t in three(
                        wqk_hi[u % 2][:, k, a, :], wqk_lo[u % 2][:, k, a, :], x_hi[:, k, toks], x_lo[:, k, toks])])
                else:
                    pe.wait_ge(shift_ok, 4 * u + 4)
                    pe.wait_ge(work_free[0], freed(job(u, 4)))
                    pe.wait_ge(work_free[1], freed(job(u, 4)))
                    for t in range(4):
                        time = 4 * (i - 4) + t
                        mm = pe.matmul(bank[:, t * P:(t + 1) * P], shift[u % 2][:, time, :],
                                       at_time(q0, time),
                                       start=True, stop=True)
                mm.then_inc(work_made, 1)

            def step(u, j, g):
                if 2 <= g <= STEPS * HG + 1:
                    pe.wait_ge(exped, g - 1)
                    wait(pe, t_copied, g - 2)
                    for n in range(4):
                        mm = pe.transpose(p_turn[:, n * P:(n + 1) * P], prob[(g - 2) % 3][:, n, :], c["ident"][:])
                    mm.then_inc(turned, 1)
                if 3 <= g <= STEPS * HG + 2:
                    head, b = (g - 3) // 4, (g - 3) % 4
                    pe.wait_ge(t_copied, g - 2)
                    wait(pe, o_ok, g - 3)
                    for n in range(4):
                        mm = pe.matmul(p_o[:, n * VW1:(n + 1) * VW1], prob_t[(g - 3) % 2][:, n, :],
                                       v[:, 4 * b + n, head, :], start=True, stop=True)
                    mm.then_inc(valued, 1)
                r = outs(u, j)
                if r is not None:
                    pe.wait_ge(o_ok, min(STEPS * HG, 32 * (r // 4 + 1)) if r // 4 == 0 else 60 + r % 4 + 1)
                    wait(pe, ot_lo_ok, r - 1)
                    for n in range(4):
                        mm = pe.transpose(p_out[r % 2][:, n * P:(n + 1) * P],
                                          o[:, 4 * (r % 4) + n, (r // 4) * P:(r // 4 + 1) * P], c["ident"][:])
                    mm.then_inc(o_turned, 1)
                if 0 <= u < HG:
                    rows = slice(32 * (j // 4), 32 * (j // 4) + 32)
                    if j == 0:
                        for b in range(2):
                            pe.wait_ge(work_free[b], freed(job(u + 1, 0)))
                    wait(pe, shifted, g - 1)
                    pe.matmul(p_s[g % 2][:], c["ident_b"][:], c["mask"][:].unsqueeze(1).to_broadcast([P, 4, P]),
                              start=True, stop=False, skip_group_check=True)
                    for n in range(4):
                        toks = slice((4 * (j % 4) + n) * P, (4 * (j % 4) + n + 1) * P)
                        mm = pe.matmul(p_s[g % 2][:, n * P:(n + 1) * P], q[u % 2][rows, toks], k1[u % 2][rows, toks],
                                       start=False, stop=n == 3, skip_group_check=True)
                    mm.then_inc(scored, 1)
                if u < HG - 1 and j < JOBS:
                    project(u + 1, j)

            steps(step)
            for i in range(S // 2):
                pe.wait_ge(ot_lo_ok, 8)
                wait(pe, out_added, i - 1)
                for n in range(2):
                    toks = slice((2 * i + n) * P, (2 * i + n + 1) * P)
                    mm = accumulate(pe, p_out[i % 2][:, n * F:(n + 1) * F], [t for k in range(K) for t in three(
                        x_hi[:, k, toks], x_lo[:, k, toks], wo_hi[:, k, :], wo_lo[:, k, :])])
                mm.then_inc(out_made, 1)

        @block.scalar
        def _(act):
            act.wait_ge(small_in, N_SMALL)
            act.copy(wv_hi[:], wv[:]).then_inc(const_hi, 1)
            act.copy(wo_hi[:], wo[:]).then_inc(const_hi, 1)
            norm.scalar(act)
            act.wait_ge(bias_ok, 2)

            def cut(u):
                act.wait_ge(w_in[u % 2], 16 * (u // 2 + 1))
                wait(act, work_made, job(u - 1, 0) if u >= 2 else 0)
                act.copy(wqk_hi[u % 2][:], wqk[u % 2][:]).then_inc(w_hi_ok, 1)

            def step(u, j, g):
                if u < HG - 1 and j == 0:
                    cut(u + 1)
                if 2 <= g <= STEPS * HG + 1:
                    act.wait_ge(turned, g - 1)
                    wait(act, valued, g - 3)
                    act.copy(prob_t[g % 2][:], p_turn[:].rearrange("p (n c) -> p n c", n=4))\
                        .then_inc(t_copied, 1)
                r = outs(u, j)
                if r is not None:
                    act.wait_ge(o_turned, r + 1)
                    act.copy(ungrouped(x_hi, r), out_view(p_out[r % 2])).then_inc(ot_hi_ok, 1)
                if 0 <= u < HG:
                    act.wait_ge(shifted, g + 1)
                    act.activation(prob[g % 3][:], prob[g % 3][:], ACT.Exp, scale=float(D1) ** -0.5)\
                        .then_inc(exped, 1)
                if u < HG - 1 and j < 4:
                    n = job(u + 1, j)
                    act.wait_ge(work_made, n + 1)
                    if u >= 0:
                        for b in range(2):
                            act.wait_ge(work_free[b], freed(job(u, 8)))
                    act.activation(q0[:, j * BANK:(j + 1) * BANK], p_work[n % 2][:], ACT.Identity,
                                   bias=bq_rr[:, u + 1:u + 2]).then_inc(work_free[n % 2], 1)

            steps(step)

        @block.vector
        def _(dve):
            dve.wait_ge(small_in, N_SMALL)
            dve.tensor_tensor(bq_rr[:], bqk[:, :, 0], rr[:], ALU.add).then_inc(bias_ok, 1)
            dve.tensor_tensor(rw_rr[:], rw[:], rr[:], ALU.subtract).then_inc(bias_ok, 1)
            dve.wait_ge(pos_made, 1)
            dve.tensor_tensor(p_t[:], p_work[0][:, 0:HG * (NPOS + 1)].rearrange("p (u r) -> p u r", u=HG),
                              bp[:].unsqueeze(2).to_broadcast([P, HG, NPOS + 1]), ALU.add).then_inc(pos_ok, 1)
            dve.wait_ge(const_hi, 2)
            dve.tensor_tensor(wv_lo[:], wv[:], wv_hi[:].bitcast(F32), ALU.subtract).then_inc(const_lo, 1)
            dve.tensor_tensor(wo_lo[:], wo[:], wo_hi[:].bitcast(F32), ALU.subtract).then_inc(const_lo, 1)
            norm.vector(dve)
            dve.wait_ge(pos_ok, 1)
            dve.wait_ge(bias_ok, 2)
            dve.wait_ge(pool_ok, POOL_ALL)
            for i in range(NV):
                dve.wait_ge(work_made, i + 1)
                dve.tensor_tensor(v[:, 2 * i:2 * i + 2, :, 0:D1],
                                  p_work[i % 2][:].rearrange("p (g e d) -> p g e d", g=2, e=H1),
                                  bv[:].rearrange("p (e d) -> p e d", e=H1).unsqueeze(1)
                                  .to_broadcast([P, 2, H1, D1]), ALU.add).then_inc(work_free[i % 2], 1)

            def fill_shift(u):
                if u >= 2:
                    dve.wait_ge(work_made, job(u - 2, 8))
                for n in range(4):
                    rows = slice(32 * n, 32 * n + 32)
                    src = p_t[rows, u, :]
                    part = list(src.ap[0])
                    window = bass.AP(src.tensor, src.offset + S - 1, [part, [-1, S], [1, S]])
                    dve.tensor_copy(shift[u % 2][rows, :, 32 * n + D1:32 * n + 2 * D1], window).then_inc(shift_ok, 1)

            def step(u, j, g):
                if u < HG - 1 and j == 0:
                    dve.wait_ge(w_hi_ok, u + 2)
                    dve.tensor_tensor(wqk_lo[(u + 1) % 2][:], wqk[(u + 1) % 2][:],
                                      wqk_hi[(u + 1) % 2][:].bitcast(F32), ALU.subtract).then_inc(w_lo_ok, 1)
                    fill_shift(u + 1)
                if 3 <= g <= STEPS * HG + 2:
                    head, b = (g - 3) // 4, (g - 3) % 4
                    dve.wait_ge(valued, g - 2)
                    po = p_o[:, 0:4 * VW1].rearrange("p (n d) -> p n d", n=4)
                    dve.reciprocal(inv[g % 2][:], po[:, :, D1]).then_inc(inv_ok, 1)
                    dve.wait_ge(inv_ok, g - 2)
                    dve.tensor_tensor(o[:, 4 * b:4 * b + 4, head * D1:(head + 1) * D1], po[:, :, 0:D1],
                                      inv[g % 2][:].unsqueeze(2).to_broadcast([P, 4, D1]), ALU.mult).then_inc(o_ok, 1)
                if 0 <= u < HG:
                    ps = p_s[g % 2][:].rearrange("p (n c) -> p n c", n=4)
                    dve.wait_ge(scored, g + 1)
                    dve.tensor_reduce(top[g % 2][:], ps, axis=X, op=ALU.max).then_inc(top_ok, 1)
                    dve.wait_ge(top_ok, g + 1)
                    wait(dve, turned, g - 2)
                    dve.tensor_tensor(prob[g % 3][:], ps, top[g % 2][:].unsqueeze(2).to_broadcast([P, 4, P]),
                                      ALU.subtract).then_inc(shifted, 1)
                r = outs(u, j)
                if r is not None:
                    dve.wait_ge(ot_hi_ok, r + 1)
                    dve.tensor_tensor(ungrouped(x_lo, r), out_view(p_out[r % 2]), ungrouped(x_hi, r).bitcast(F32),
                                      ALU.subtract).then_inc(ot_lo_ok, 1)
                if u < HG - 1 and 4 <= j < 8:
                    n = job(u + 1, j)
                    dve.wait_ge(work_made, n + 1)
                    if u >= 1:
                        dve.wait_ge(scored, STEPS * u)
                    for t in range(4):
                        made = p_work[n % 2][:, t * P:(t + 1) * P].rearrange("p (g c) -> p g c", c=GB)
                        ins = dve.scalar_tensor_tensor(at_time(q[(u + 1) % 2], 4 * (j - 4) + t), made,
                                                       rw_rr[:, u + 1:u + 2], at_time(q0, 4 * (j - 4) + t),
                                                       ALU.add, ALU.add)
                    ins.then_inc(work_free[n % 2], 1)
                if u < HG - 1 and 8 <= j < 12:
                    n = job(u + 1, j)
                    dve.wait_ge(work_made, n + 1)
                    if u >= 1:
                        dve.wait_ge(scored, STEPS * u)
                    toks = slice((j - 8) * BANK, (j - 7) * BANK)
                    dve.scalar_tensor_tensor(k1[(u + 1) % 2][:, toks].rearrange("p (g c) -> p g c", g=4),
                                             p_work[n % 2][:].rearrange("p (g c) -> p g c", g=4),
                                             bqk[:, u + 1, 1:2], hot[:].unsqueeze(1).to_broadcast([P, 4, P]),
                                             ALU.add, ALU.add).then_inc(work_free[n % 2], 1)

            steps(step)
            dve.wait_ge(bo_ok, S)
            for i in range(S // 2):
                dve.wait_ge(out_made, i + 1)
                dve.tensor_tensor(h[:, 2 * i:2 * i + 2, :], h[:, 2 * i:2 * i + 2, :],
                                  p_out[i % 2][:].rearrange("p (t f) -> p t f", t=2), ALU.add).then_inc(out_added, 1)
    sp.close()


def build_router(nc, c, h, xn, slot_i, slot_w, r1_d, r2_d):
    HALVES = S * E1 // P
    with ExitStack() as ctx:
        sp = Space(nc, ctx, "router")
        x_hi, x_lo = sp.sb("x_hi", [P, K, T], F32R), sp.sb("x_lo", [P, K, T], F32R)
        r1, r1_hi, r1_lo = sp.sb("r1", [P, K, RH]), sp.sb("r1_hi", [P, K, RH], F32R), sp.sb("r1_lo", [P, K, RH], F32R)
        r2 = sp.sb("r2", [RH, E1])
        act1 = sp.sb("act1", [P, T])
        logit = sp.sb("logit", [P, HALVES, P])
        prob, best = sp.sb("prob", [P, HALVES, P]), sp.sb("best", [P, HALVES, CAP])
        best_i = sp.sb("best_i", [P, HALVES, CAP], U32)
        row = sp.sb("row", [P, HALVES])
        twice = sp.sb("twice", [P, 2, HALVES, 2, CAP])
        p_norm = [sp.ps(f"p_norm{i}", [P, BANK]) for i in range(2)]
        p_r1 = [sp.ps(f"p_r1{i}", [P, BANK]) for i in range(2)]
        p_logit, p_rows, p_slot = sp.ps("p_logit", [P, BANK]), sp.ps("p_rows", [P, BANK]), sp.ps("p_slot", [P, BANK])
        norm = Norm(sp, c, h, x_hi, x_lo, False, p_norm, keep=xn)
        small_in, r1_hi_ok, r1_lo_ok = sp.sem("small_in"), sp.sem("r1_hi_ok"), sp.sem("r1_lo_ok")
        r1_made, act1_ok = sp.sem("r1_made"), sp.sem("act1_ok")
        logits_made, logits_ok, rows_made = sp.sem("logits_made"), sp.sem("logits_ok"), sp.sem("rows_made")
        shifted, exped, steps = sp.sem("shifted"), sp.sem("exped"), sp.sem("steps")
        none_ok = sp.sem("none_ok")
        twice_ok, slots_made, slots_ok = sp.sem("twice_ok"), sp.sem("slots_made"), sp.sem("slots_ok")
        block = ctx.enter_context(nc.Block())

        @block.gpsimd
        def _(pool):
            pool.memset(slot_i[:], -1.0).then_inc(none_ok, 1)
            norm.gpsimd(pool)

        @block.sync
        def _(sync):
            sync.dma_start(r1[:], r1_d).then_inc(small_in, 16)
            sync.dma_start(r2[:], r2_d).then_inc(small_in, 16)

        @block.tensor
        def _(pe):
            norm.tensor(pe)
            pe.wait_ge(r1_lo_ok, 1)
            pe.wait_ge(norm.lo_ok, S)
            for i in range(CH):
                toks = slice(i * BANK, (i + 1) * BANK)
                wait(pe, act1_ok, i - 1)
                accumulate(pe, p_r1[i % 2][:], [t for k in range(K) for t in three(
                    r1_hi[:, k, :], r1_lo[:, k, :], x_hi[:, k, toks], x_lo[:, k, toks])]).then_inc(r1_made, 1)
            for s in range(S):
                pe.wait_ge(act1_ok, s // 4 + 1)
                mm = pe.matmul(p_logit[:, s * E1:(s + 1) * E1], act1[:, s * P:(s + 1) * P], r2[:],
                               start=True, stop=True)
            mm.then_inc(logits_made, 1)
            pe.wait_ge(logits_ok, 1)
            for i in range(HALVES):
                mm = pe.transpose(p_rows[:, i * P:(i + 1) * P], logit[:, i, :], c["ident"][:])
            mm.then_inc(rows_made, 1)
            pe.wait_ge(twice_ok, 2)
            for a in range(2):
                for i in range(HALVES):
                    n = HALVES * a + i
                    mm = pe.transpose(p_slot[:, n * P:(n + 1) * P], twice[:, a, i, :, :]
                                      .rearrange("p r c -> p (r c)"), c["ident"][:])
            mm.then_inc(slots_made, 1)

        @block.scalar
        def _(act):
            act.wait_ge(small_in, 32)
            act.copy(r1_hi[:], r1[:]).then_inc(r1_hi_ok, 1)
            norm.scalar(act)
            for i in range(CH):
                act.wait_ge(r1_made, i + 1)
                act.activation(act1[:, i * BANK:(i + 1) * BANK], p_r1[i % 2][:], ACT.Silu).then_inc(act1_ok, 1)
            act.wait_ge(shifted, 1)
            act.activation(prob[:], prob[:], ACT.Exp).then_inc(exped, 1)

        @block.vector
        def _(dve):
            dve.wait_ge(r1_hi_ok, 1)
            dve.tensor_tensor(r1_lo[:], r1[:], r1_hi[:].bitcast(F32), ALU.subtract).then_inc(r1_lo_ok, 1)
            norm.vector(dve)
            wide = [P, HALVES, P]
            chain = Chain(dve, steps)
            dve.wait_ge(logits_made, 1)
            dve.tensor_copy(logit[:], p_logit[:, 0:HALVES * P].rearrange("p (i r) -> p i r", i=HALVES))\
                .then_inc(logits_ok, 1)
            dve.wait_ge(rows_made, 1)
            rows = p_rows[:, 0:HALVES * P].rearrange("p (i c) -> p i c", i=HALVES)
            chain(dve.tensor_reduce(row[:], rows, axis=X, op=ALU.max))
            dve.tensor_tensor(prob[:], rows, row[:].unsqueeze(2).to_broadcast(wide), ALU.subtract)\
                .then_inc(shifted, 1)
            dve.wait_ge(exped, 1)
            chain(dve.tensor_reduce(row[:], prob[:], axis=X, op=ALU.add))
            chain(dve.reciprocal(row[:], row[:]))
            chain(dve.tensor_tensor(prob[:], prob[:], row[:].unsqueeze(2).to_broadcast(wide), ALU.mult))
            for r in range(CAP // 8):
                cols = slice(8 * r, 8 * r + 8)
                for i in range(HALVES):
                    chain(dve.max(best[:, i, cols], prob[:, i, :]))
                    chain(dve.max_index(best_i[:, i, cols], best[:, i, cols], prob[:, i, :]))
                    chain(dve.match_replace(prob[:, i, :], best[:, i, cols], prob[:, i, :], -1.0))
            chain(dve.tensor_reduce(row[:], best[:], axis=X, op=ALU.add))
            chain(dve.tensor_scalar_add(row[:], row[:], 1e-9))
            chain(dve.reciprocal(row[:], row[:]))
            both = [P, HALVES, 2, CAP]
            chain(dve.tensor_tensor(best[:], best[:], row[:].unsqueeze(2).to_broadcast([P, HALVES, CAP]), ALU.mult))
            dve.tensor_copy(twice[:, 0], best[:].unsqueeze(2).to_broadcast(both)).then_inc(twice_ok, 1)
            dve.tensor_copy(twice[:, 1], best_i[:].unsqueeze(2).to_broadcast(both)).then_inc(twice_ok, 1)
            dve.wait_ge(slots_made, 1)
            dve.wait_ge(none_ok, 1)
            for odd in range(2):
                rows = slice(CAP * odd, CAP * odd + CAP)
                src = p_slot[rows, :].rearrange("p (a b odd e) -> p a b odd e", a=2, odd=2, e=E1)
                dve.tensor_copy(slot_w[rows, :, :], src[:, 0, :, odd, :]).then_inc(slots_ok, 1)
                dve.tensor_copy(slot_i[rows, :, :].rearrange("p (b odd) e -> p b odd e", odd=2)[:, :, odd, :],
                                src[:, 1, :, odd, :]).then_inc(slots_ok, 1)
    sp.close()


def build_ffn1(nc, c, h, r1_d, r2_d, w12_d, w3_d):
    NB = S // 2
    with ExitStack() as outer:
        keep = Space(nc, outer, "f1")
        xn = [keep.sb(f"xn{i}", [P, S, F], BF16) for i in range(3)]
        slot_i, slot_w = keep.sb("slot_i", [P, S, E1]), keep.sb("slot_w", [P, NB, E1])
        build_router(nc, c, h, xn, slot_i, slot_w, r1_d, r2_d)
        ctx = outer.enter_context(ExitStack())
        sp = Space(nc, ctx, "f1")
        w12, w3 = sp.sb("w12", [P, 2, K, FF1]), sp.sb("w3", [P, M1, F])
        w12_hi = [sp.sb(f"w12_hi{i}", [P, 2, K, FF1], F32R) for i in range(2)]
        w12_lo = [sp.sb(f"w12_lo{i}", [P, 2, K, FF1], F32R) for i in range(2)]
        w3_hi = [sp.sb(f"w3_hi{i}", [P, M1, F], F32R) for i in range(2)]
        w3_lo = [sp.sb(f"w3_lo{i}", [P, M1, F], F32R) for i in range(2)]
        put = [sp.sb(f"put{i}", [P, S, P], F32R) for i in range(2)]
        place = [sp.sb(f"place{i}", [P, S]) for i in range(2)]
        ident_r = sp.sb("ident_r", [P, P], F32R)
        take = [sp.sb(f"take{i}", [P, S, CAP], BF16) for i in range(2)]
        weight = [sp.sb(f"weight{i}", [P, NB]) for i in range(2)]
        xe = [[sp.sb(f"xe{i}{z}", [P, K, BANK], F32R) for z in ("hi", "lo")] for i in range(2)]
        silu = [sp.sb(f"silu{i}", [P, BANK]) for i in range(2)]
        hid = [sp.sb(f"hid{i}", [P, BANK]) for i in range(2)]
        hid_hi, hid_lo = sp.sb("hid_hi", [P, M1, BANK], F32R), sp.sb("hid_lo", [P, M1, BANK], F32R)
        y_hi, y_lo = sp.sb("y_hi", [P, 4, F], F32R), sp.sb("y_lo", [P, 4, F], F32R)
        p_gate = [sp.ps(f"p_gate{i}", [P, BANK]) for i in range(2)]
        p_value = [sp.ps(f"p_value{i}", [P, BANK]) for i in range(2)]
        p_y = [sp.ps(f"p_y{i}", [P, BANK]) for i in range(2)]
        p_take, p_put = sp.ps("p_take", [P, BANK]), sp.ps("p_put", [P, BANK])

        w12_in, w3_in = sp.sem("w12_in"), sp.sem("w3_in")
        w_hi_ok, w_lo_ok = sp.sem("w_hi_ok"), sp.sem("w_lo_ok")
        put_begun = sp.sem("put_begun")
        put_ok, take_made, take_ok = sp.sem("put_ok"), sp.sem("take_made"), sp.sem("take_ok")
        weight_ok, ident_ok = sp.sem("weight_ok"), sp.sem("ident_ok")
        taken, xe_hi_ok, xe_lo_ok = sp.sem("taken"), sp.sem("xe_hi_ok"), sp.sem("xe_lo_ok")
        gate_made, value_made = sp.sem("gate_made"), sp.sem("value_made")
        silu_ok, hid_ok, hid_hi_ok, hid_lo_ok = sp.sem("silu_ok"), sp.sem("hid_ok"), sp.sem("hid_hi_ok"), sp.sem("hid_lo_ok")
        y_made, y_hi_ok, y_lo_ok = sp.sem("y_made"), sp.sem("y_hi_ok"), sp.sem("y_lo_ok")
        put_made, added = sp.sem("put_made"), sp.sem("added")
        block = ctx.enter_context(nc.Block())

        def run(engine, expert):
            expert(0, 0, False, True)
            with engine.Fori(0, (E1 - 2) // 2) as i:
                expert(2 * i + 1, 1, True, True)
                expert(2 * i + 2, 0, True, True)
            expert(E1 - 1, 1, True, False)

        def column(x, e):
            return x[:, :, e:e + 1] if isinstance(e, int) else x[:, :, bass.ds(e, 1)]

        @block.sync
        def _(sync):
            sync.dma_start(w12[:], w12_d[0]).then_inc(w12_in, 16)
            sync.dma_start(w3[:], w3_d[0]).then_inc(w3_in, 16)
            with sync.Fori(1, E1) as e:
                sync.wait_ge(w_lo_ok, 3 * e)
                sync.dma_start(w12[:], w12_d[bass.ds(e, 1)].squeeze(0)).then_inc(w12_in, 16)
                sync.dma_start(w3[:], w3_d[bass.ds(e, 1)].squeeze(0)).then_inc(w3_in, 16)

        @block.gpsimd
        def _(pool):
            def build_put(e, par):
                pool.wait_ge(weight_ok, 2 * e + 2)
                wait(pool, put_made, 8 * e - 12)
                pool.sem_inc(put_begun, 1)
                for s in range(S):
                    if s >= NB and s % 2 == 0 and not (isinstance(e, int) and e < 2):
                        pool.wait_ge(put_made, 8 * e - 12 + (s - NB) // 2 + 1)
                        pool.sem_inc(put_begun, 1)
                    pool.tensor_scalar(put[par][:, s, :], c["iota_p"][:], place[par][:, s:s + 1], None,
                                       ALU.is_equal).then_inc(put_ok, 1)

            def expert(e, par, before, more):
                if more:
                    build_put(e + 1, 1 - par)

            build_put(0, 0)
            run(pool, expert)

        @block.tensor
        def _(pe):
            def turn_put(e, par, i):
                n = 2 * e + i
                pe.wait_ge(put_ok, S * e + NB * (i + 1))
                wait(pe, xe_lo_ok, 2 * n)
                wait(pe, take_ok, n)
                for b in range(4):
                    mm = accumulate(pe, p_take[:, b * P:(b + 1) * P],
                                    [(put[par][:, 2 * (4 * i + b) + odd, :], ident_r[:]) for odd in range(2)])
                mm.then_inc(take_made, 1)

            def take_tiles(e, par, cc, k):
                n = 2 * e + cc
                pe.wait_ge(take_ok, 2 * e + 1 + cc)
                wait(pe, xe_lo_ok, 2 * n + k)
                for b in range(NB):
                    mm = accumulate(pe, p_take[:, b * CAP:(b + 1) * CAP],
                                    [(part[:, NB * cc + b, k * P:(k + 1) * P], take[par][:, NB * cc + b, :])
                                     for part in xn])
                mm.then_inc(taken, 1)

            def put_back(e, par, cc, q):
                m = 2 * e + cc
                pe.wait_ge(y_lo_ok, 4 * m + q + 1)
                wait(pe, added, 4 * m + q)
                for odd in range(2):
                    mm = accumulate(pe, p_put[:, odd * F:(odd + 1) * F],
                                    [(put[par][:, 2 * (4 * cc + q) + odd, :], y[:, q, :]) for y in (y_hi, y_lo)])
                mm.then_inc(put_made, 1)

            def expand(par, cc, n, f, a, bank, free, made):
                wait(pe, free, 4 * n + f - 1)
                cols = slice(f * P, (f + 1) * P)
                accumulate(pe, bank[f % 2][:], [t for k in range(K) for t in three(
                    w12_hi[par][:, a, k, cols], w12_lo[par][:, a, k, cols],
                    xe[cc][0][:, k, :], xe[cc][1][:, k, :])]).then_inc(made, 1)

            def reduce(par, q, fs, last):
                pairs = [t for f in fs for t in three(
                    hid_hi[:, f, q * P:(q + 1) * P], hid_lo[:, f, q * P:(q + 1) * P],
                    w3_hi[par][:, f, :], w3_lo[par][:, f, :])]
                return accumulate(pe, p_y[q % 2][:, 0:F], pairs, first=fs[0] == 0, last=last)

            def expert(e, par, before, more):
                for cc in range(2):
                    n = 2 * e + cc
                    pe.wait_ge(xe_lo_ok, 2 * n + 2)
                    pe.wait_ge(w_lo_ok, 3 * e + 3)
                    for f in range(M1):
                        expand(par, cc, n, f, 0, p_gate, silu_ok, gate_made)
                        if cc == 1:
                            put_back(e, par, 0, f)
                        elif before:
                            put_back(e - 1, 1 - par, 1, f)
                        expand(par, cc, n, f, 1, p_value, hid_ok, value_made)
                        if cc == 0 and f % 2:
                            take_tiles(e, par, 1, f // 2)
                        elif more and f % 2:
                            take_tiles(e + 1, 1 - par, 0, f // 2)
                    for q in range(2):
                        wait(pe, y_lo_ok, 4 * n + q - 1)
                        pe.wait_ge(hid_lo_ok, 4 * n + 3)
                        reduce(par, q, (0, 1, 2), False)
                    pe.wait_ge(hid_lo_ok, 4 * n + 4)
                    for q in range(2):
                        reduce(par, q, (3,), True).then_inc(y_made, 1)
                    if more:
                        turn_put(e + 1, 1 - par, cc)
                    for q in range(2, 4):
                        pe.wait_ge(y_lo_ok, 4 * n + q - 1)
                        reduce(par, q, (0, 1, 2, 3), True).then_inc(y_made, 1)

            pe.wait_ge(ident_ok, 1)
            turn_put(0, 0, 0)
            for k in range(K):
                take_tiles(0, 0, 0, k)
            turn_put(0, 0, 1)
            run(pe, expert)
            for q in range(4):
                put_back(E1 - 1, 1, 1, q)

        @block.scalar
        def _(act):
            def cut(e, par, i):
                act.wait_ge(w3_in if i == 2 else w12_in, 16 * e + 16)
                wait(act, y_made, 8 * (e - 1))
                if i < 2:
                    act.copy(w12_hi[par][:, i], w12[:, i]).then_inc(w_hi_ok, 1)
                else:
                    act.copy(w3_hi[par][:], w3[:]).then_inc(w_hi_ok, 1)

            def copy_take(e, par, i):
                act.wait_ge(take_made, 2 * e + i + 1)
                wait(act, taken, 4 * (e - 1))
                act.copy(take[par][:, NB * i:NB * (i + 1), :], p_take[:].rearrange("p (b c) -> p b c", c=CAP))\
                    .then_inc(take_ok, 1)

            def copy_xe(e, cc, k):
                n = 2 * e + cc
                act.wait_ge(taken, 2 * n + k + 1)
                wait(act, value_made, 4 * (n - 1))
                act.copy(xe[cc][0][:, k, :], p_take[:]).then_inc(xe_hi_ok, 1)

            def expert(e, par, before, more):
                for cc in range(2):
                    n = 2 * e + cc
                    for f in range(M1):
                        act.wait_ge(gate_made, 4 * n + f + 1)
                        wait(act, hid_ok, 4 * n + f - 1)
                        act.activation(silu[f % 2][:], p_gate[f % 2][:], ACT.Silu).then_inc(silu_ok, 1)
                        if cc == 0 and more and f >= 1:
                            cut(e + 1, 1 - par, f - 1)
                        if cc == 0 and f % 2:
                            copy_xe(e, 1, f // 2)
                        elif more and f % 2:
                            copy_xe(e + 1, 0, f // 2)
                        act.wait_ge(hid_ok, 4 * n + f + 1)
                        wait(act, y_made, 4 * n)
                        act.copy(hid_hi[:, f, :], hid[f % 2][:]).then_inc(hid_hi_ok, 1)
                    for q in range(4):
                        act.wait_ge(y_made, 4 * n + q + 1)
                        act.wait_ge(weight_ok, 2 * e + 1)
                        wait(act, put_made, 4 * n - 3 + q)
                        act.activation(y_hi[:, q, :], p_y[q % 2][:, 0:F], ACT.Copy,
                                       scale=weight[par][:, 4 * cc + q:4 * cc + q + 1]).then_inc(y_hi_ok, 1)
                        if more and q == 1:
                            copy_take(e + 1, 1 - par, cc)

            for i in range(3):
                cut(0, 0, i)
            copy_take(0, 0, 0)
            for k in range(K):
                copy_xe(0, 0, k)
            copy_take(0, 0, 1)
            run(act, expert)

        @block.vector
        def _(dve):
            def cut(e, par, i):
                dve.wait_ge(w_hi_ok, 3 * e + i + 1)
                hi, lo, raw = (w12_hi[par][:, i], w12_lo[par][:, i], w12[:, i]) if i < 2 else \
                    (w3_hi[par][:], w3_lo[par][:], w3[:])
                dve.tensor_tensor(lo, raw, hi.bitcast(F32), ALU.subtract).then_inc(w_lo_ok, 1)

            def take_slots(e, par):
                wait(dve, y_hi_ok, 8 * (e - 1))
                wait(dve, y_lo_ok, 8 * (e - 1))
                wait(dve, put_ok, S * (e - 1))
                dve.tensor_copy(weight[par][:].unsqueeze(2), column(slot_w, e)).then_inc(weight_ok, 1)
                dve.tensor_copy(place[par][:].unsqueeze(2), column(slot_i, e)).then_inc(weight_ok, 1)

            def cut_xe(e, cc, k):
                n = 2 * e + cc
                dve.wait_ge(xe_hi_ok, 2 * n + k + 1)
                dve.tensor_tensor(xe[cc][1][:, k, :], p_take[:], xe[cc][0][:, k, :].bitcast(F32), ALU.subtract)\
                    .then_inc(xe_lo_ok, 1)

            def add(cc, m, q):
                s = 2 * (4 * cc + q)
                dve.wait_ge(put_made, 4 * m + q + 1)
                wait(dve, added, 4 * m + q)
                dve.tensor_tensor(h[:, s:s + 2, :], h[:, s:s + 2, :], p_put[:].rearrange("p (b f) -> p b f", b=2),
                                  ALU.add).then_inc(added, 1)

            def expert(e, par, before, more):
                for cc in range(2):
                    n = 2 * e + cc
                    if cc == 0 and more:
                        take_slots(e + 1, 1 - par)
                    for f in range(M1):
                        if cc == 1:
                            add(0, n - 1, f)
                        elif before:
                            add(1, n - 1, f)
                        dve.wait_ge(value_made, 4 * n + f + 1)
                        dve.wait_ge(silu_ok, 4 * n + f + 1)
                        wait(dve, hid_lo_ok, 4 * n + f - 1)
                        dve.tensor_tensor(hid[f % 2][:], p_value[f % 2][:], silu[f % 2][:], ALU.mult)\
                            .then_inc(hid_ok, 1)
                        if cc == 0 and more and f >= 1:
                            cut(e + 1, 1 - par, f - 1)
                        if cc == 0 and f % 2:
                            cut_xe(e, 1, f // 2)
                        elif more and f % 2:
                            cut_xe(e + 1, 0, f // 2)
                        dve.wait_ge(hid_hi_ok, 4 * n + f + 1)
                        dve.tensor_tensor(hid_lo[:, f, :], hid[f % 2][:], hid_hi[:, f, :].bitcast(F32),
                                          ALU.subtract).then_inc(hid_lo_ok, 1)
                    for q in range(4):
                        dve.wait_ge(y_hi_ok, 4 * n + q + 1)
                        dve.scalar_tensor_tensor(y_lo[:, q, :], p_y[q % 2][:, 0:F],
                                                 weight[par][:, 4 * cc + q:4 * cc + q + 1],
                                                 y_hi[:, q, :].bitcast(F32), ALU.mult, ALU.subtract)\
                            .then_inc(y_lo_ok, 1)

            dve.tensor_copy(ident_r[:], c["ident"][:]).then_inc(ident_ok, 1)
            take_slots(0, 0)
            for i in range(3):
                cut(0, 0, i)
            for k in range(K):
                cut_xe(0, 0, k)
            run(dve, expert)
            for q in range(4):
                add(1, 2 * E1 - 1, q)


def build(nc, a, out):
    with ExitStack() as ctx:
        sp = Space(nc, ctx, "all")
        h = sp.sb("h", [P, S, F])
        c = {
            "ident": sp.sb("ident", [P, P]),
            "ident_b": sp.sb("ident_b", [P, P], BF16),
            "iota_p": sp.sb("iota_p", [P, P]),
            "block_i": sp.sb("block_i", [P, P], I32),
            "block_f": sp.sb("block_f", [P, P]),
            "mask": sp.sb("mask", [P, P], BF16),
        }
        build_constants(nc, c)
        build_tokens(nc, c, h, a["ids"], a["dmap"], a["emb"], a["wexp"], a["wproj"])
        build_attention0(nc, c, h, a["a0_w"], a["a0_bqk"], a["a0_bv"], a["a0_wo"], a["a0_bo"])
        build_ffn0(nc, c, h, a["f0_gate"], a["f0_gate_b"], a["f0_w"], a["f0_b1"], a["f0_b2"])
        build_attention1(nc, c, h, a["a1_wqk"], a["a1_bqk"], a["a1_wv"], a["a1_bv"], a["a1_pos"], a["a1_wp"],
                         a["a1_bp"], a["a1_rw"], a["a1_rr"], a["a1_wo"], a["a1_bo"])
        build_ffn1(nc, c, h, a["f1_r1"], a["f1_r2"], a["f1_w12"], a["f1_w3"])
        stored = sp.sem("stored")
        block = ctx.enter_context(nc.Block())

        @block.sync
        def _(sync):
            sync.dma_start(out.rearrange("s b f -> b s f"), h[:]).then_inc(stored, 16)
            sync.wait_ge(stored, 16)


def kernel(**inputs):
    import numpy as _np
    import concourse.bacc as _bacc
    from concourse import mybir as _mybir
    from concourse.bass_utils import run_bass_kernel_spmd as _run

    g = {k: _np.asarray(v) for k, v in inputs.items()}

    def halves(w):
        w = w.reshape(w.shape[:-2] + (w.shape[-2] // P, P, w.shape[-1]))
        return _np.moveaxis(w, -3, -2)

    def heads32(w):
        out = _np.zeros((H1, 32) + w.shape[1:], w.dtype)
        out[:, 0:D1] = w.reshape((H1, D1) + w.shape[1:])
        return out.reshape((HG, P) + w.shape[1:])

    w_in0, b_in0 = g["L0_attn_in_proj_weight"], g["L0_attn_in_proj_bias"]
    w_in1, b_in1 = g["L1_attn_in_proj_weight"], g["L1_attn_in_proj_bias"]
    w12 = _np.stack([g["L1_ffn_w1"], g["L1_ffn_w2"]], 1)
    ffn0_in = _np.concatenate([g["L0_ffn_w1"], g["L0_ffn_sw1"][None]])
    ffn0_out = _np.concatenate([g["L0_ffn_w2"], g["L0_ffn_sw2"][None]])
    host = {
        "ids": g["x"].T,
        "dmap": g["L0_tok_domain_map"][:, None],
        "emb": g["L0_tok_emb_table"],
        "wexp": halves(g["L0_tok_W_exp"].reshape(F, F).T),
        "wproj": halves(g["L0_tok_W_proj"].transpose(0, 2, 1).reshape(F, F)),
        "a0_w": w_in0.reshape(3, PAIRS, P, K, P).transpose(1, 4, 3, 0, 2),
        "a0_bqk": b_in0.reshape(3, PAIRS, P)[0:2].transpose(2, 1, 0),
        "a0_bv": b_in0[2 * H0 * D0:][None],
        "a0_wo": halves(g["L0_attn_out_proj_weight"].T),
        "a0_bo": g["L0_attn_out_proj_bias"][None],
        "f0_gate": halves(g["L0_ffn_gate_w"]),
        "f0_gate_b": g["L0_ffn_gate_b"][None],
        "f0_w": _np.stack([halves(ffn0_in), halves(ffn0_out)], 2),
        "f0_b1": _np.concatenate([g["L0_ffn_b1"], g["L0_ffn_sb1"][None]]).reshape(E0 + 1, K, P).transpose(2, 0, 1),
        "f0_b2": _np.concatenate([g["L0_ffn_b2"], g["L0_ffn_sb2"][None]]),
        "a1_wqk": _np.stack([halves(heads32(w_in1[i * F:(i + 1) * F]).transpose(0, 2, 1)) for i in range(2)], 3),
        "a1_bqk": _np.stack([heads32(b_in1[i * F:(i + 1) * F]) for i in range(2)], 0).transpose(2, 1, 0),
        "a1_wv": halves(w_in1[2 * F:].T),
        "a1_bv": b_in1[2 * F:][None],
        "a1_pos": halves(_np.concatenate([g["L1_attn_pos"][0:NPOS, 0], _np.zeros((1, F), _np.float32)]).T),
        "a1_wp": _np.moveaxis(halves(heads32(g["L1_attn_pos_proj_weight"]).transpose(0, 2, 1)), 0, 2),
        "a1_bp": heads32(g["L1_attn_pos_proj_bias"]).T,
        "a1_rw": heads32(g["L1_attn_r_w_bias"].reshape(F)).T,
        "a1_rr": heads32(g["L1_attn_r_r_bias"].reshape(F)).T,
        "a1_wo": halves(g["L1_attn_out_proj_weight"].T),
        "a1_bo": g["L1_attn_out_proj_bias"][None],
        "f1_r1": halves(g["L1_ffn_router_w1"]),
        "f1_r2": g["L1_ffn_router_w2"],
        "f1_w12": halves(w12).transpose(0, 2, 1, 3, 4),
        "f1_w3": halves(g["L1_ffn_w3"]),
    }
    nc = _bacc.Bacc("TRN2", target_bir_lowering=False, num_devices=1)
    arrays, args = {}, {}
    for name, v in host.items():
        v = _np.ascontiguousarray(v)
        arrays[f"in_{name}"] = v
        args[name] = nc.dram_tensor(f"in_{name}", v.shape, _mybir.dt.from_np(v.dtype), kind="ExternalInput").ap()
    out = nc.dram_tensor("out", (S, P, F), _mybir.dt.float32, kind="ExternalOutput").ap()
    build(nc, args, out)
    r = _run(nc, [arrays], core_ids=[0])
    return r.results[0]["out"]
```

```python
from contextlib import ExitStack

import concourse.bass as bass
import numpy as np
from concourse import mybir

F32 = mybir.dt.float32
F32R = mybir.dt.float32r
BF16 = mybir.dt.bfloat16
I32 = mybir.dt.int32
U32 = mybir.dt.uint32
ALU = mybir.AluOpType
ACT = mybir.ActivationFunctionType
X = mybir.AxisListType.X

P = 128
S = 16
F = 256
K = F // P
T = S * P
GB = P // S
NG = P // GB
BANK = 512
CH = T // BANK
EPS = 1e-5

NDOM, DEXP = 8, 32

H0, D0 = 16, 64
PAIRS = H0 // 2
VB = 4 * D0
VW0 = D0 + 1

E0, FF0 = 8, 256

H1, D1 = 16, 16
HG = 4
VW1 = D1 + 1
NPOS = 2 * S - 1

E1, FF1, CAP = 16, 512, 64
RH = 128
M1 = FF1 // P


def wait(engine, sem, value):
    if isinstance(value, int) and value <= 0:
        return
    engine.wait_ge(sem, value)


def three(hi_l, lo_l, hi_r, lo_r):
    return [(hi_l, hi_r), (hi_l, lo_r), (lo_l, hi_r)]


def accumulate(pe, out, pairs, first=True, last=True):
    for n, (lhs, rhs) in enumerate(pairs):
        mm = pe.matmul(out, lhs, rhs, start=first and n == 0, stop=last and n == len(pairs) - 1)
    return mm


class Chain:

    def __init__(self, engine, sem):
        self.engine, self.sem, self.n = engine, sem, 0

    def __call__(self, ins):
        self.n += 1
        ins.then_inc(self.sem, 1)
        self.engine.wait_ge(self.sem, self.n)

    def free(self, ins):
        self.n += 1
        ins.then_inc(self.sem, 1)

    def settle(self):
        self.engine.wait_ge(self.sem, self.n)


def group_view(x):
    return x.rearrange("p k (g t c) -> p k g t c", t=S, c=GB)


class Space:

    def __init__(self, nc, ctx, stage):
        self.nc, self.ctx, self.stage, self.sems = nc, ctx, stage, []

    def sb(self, name, shape, dt=F32):
        return self.ctx.enter_context(self.nc.sbuf_tensor(f"{self.stage}_{name}", shape, dt))

    def ps(self, name, shape, dt=F32):
        return self.ctx.enter_context(self.nc.psum_tensor(f"{self.stage}_{name}", shape, dt))

    def sem(self, name):
        self.sems.append(self.nc.alloc_semaphore(f"{self.stage}_{name}"))
        return self.sems[-1]

    def close(self):
        self.nc.clear_and_free_semaphores(self.sems)
        self.nc.all_engine_barrier()


def build_constants(nc, c):
    with ExitStack() as ctx:
        sp = Space(nc, ctx, "const")
        written = sp.sem("written")
        filled = sp.sem("filled")
        diag = sp.sem("diag")
        block = ctx.enter_context(nc.Block())

        @block.gpsimd
        def _(pool):
            pool.memset(c["ident"][:], 0.0).then_inc(filled, 1)
            pool.wait_ge(filled, 1)
            pool.affine_select(out=c["ident"][:], in_=c["ident"][:], compare_op=ALU.not_equal, fill=1.0,
                               base=0, pattern=[[-1, P]], channel_multiplier=1).then_inc(diag, 1)
            pool.iota(c["iota_p"][:], pattern=[[1, P]], base=0, channel_multiplier=0,
                      allow_small_or_imprecise_dtypes=True).then_inc(diag, 1)
            pool.iota(c["block_i"][:], pattern=[[0, S], [1, GB]], base=P, channel_multiplier=-1)\
                .then_inc(diag, 1)

        @block.vector
        def _(dve):
            dve.wait_ge(diag, 3)
            dve.tensor_copy(c["ident_b"][:], c["ident"][:]).then_inc(written, 1)
            dve.tensor_single_scalar(c["block_i"][:], c["block_i"][:], GB - 1, op=ALU.bitwise_and)\
                .then_inc(written, 1)
            dve.wait_ge(written, 2)
            dve.tensor_copy(c["block_f"][:], c["block_i"][:]).then_inc(written, 1)
            dve.wait_ge(written, 3)
            dve.tensor_scalar(c["mask"][:], c["block_f"][:], 0.0, -1e30, ALU.not_equal, ALU.mult)\
                .then_inc(written, 1)
    sp.close()


def build_tokens(nc, c, h, stats, ids_d, dmap_d, emb_d, wexp_d, wproj_d):
    with ExitStack() as ctx:
        sp = Space(nc, ctx, "tok")
        ids = sp.sb("ids", [P, S], I32)
        dom = sp.sb("dom", [P, S], I32)
        dom_f = sp.sb("dom_f", [P, S])
        keep = sp.sb("keep", [P, S, NDOM])
        wexp = sp.sb("wexp", [P, K, F])
        wproj = sp.sb("wproj", [P, K, F])
        base_t = [sp.sb(f"base_t{i}", [P, K, P]) for i in range(2)]
        kept = [sp.sb(f"kept{i}", [P, F]) for i in range(2)]
        kept_t = [sp.sb(f"kept_t{i}", [P, K, P]) for i in range(2)]
        p_base = [sp.ps(f"p_base{i}", [P, BANK]) for i in range(2)]
        p_exp = [sp.ps(f"p_exp{i}", [P, BANK]) for i in range(2)]
        p_kept = [sp.ps(f"p_kept{i}", [P, BANK]) for i in range(2)]
        p_corr = [sp.ps(f"p_corr{i}", [P, BANK]) for i in range(2)]
        ids_in, w_in = sp.sem("ids_in"), sp.sem("w_in")
        row_in = [sp.sem(f"row_in{s}") for s in range(S)]
        dom_ok, keep_ok = sp.sem("dom_ok"), sp.sem("keep_ok")
        base_turned, base_copied = sp.sem("base_turned"), sp.sem("base_copied")
        expanded, masked = sp.sem("expanded"), sp.sem("masked")
        kept_turned, kept_copied = sp.sem("kept_turned"), sp.sem("kept_copied")
        corrected, added = sp.sem("corrected"), sp.sem("added")
        stats.open(sp)
        block = ctx.enter_context(nc.Block())

        @block.sync
        def _(sync):
            sync.dma_start(ids[:], ids_d).then_inc(ids_in, 16)
            sync.dma_start(wexp[:], wexp_d).then_inc(w_in, 16)
            sync.dma_start(wproj[:], wproj_d).then_inc(w_in, 16)

        @block.gpsimd
        def _(pool):
            pool.wait_ge(ids_in, 16)
            for s in range(S):
                at = bass.IndirectOffsetOnAxis(ap=ids[:, s:s + 1].bitcast(U32), axis=0)
                pool.indirect_dma_start(out=h[:, s, :], out_offset=None, in_=emb_d, in_offset=at)\
                    .then_inc(row_in[s], 16)
                pool.indirect_dma_start(out=dom[:, s:s + 1], out_offset=None, in_=dmap_d, in_offset=at)\
                    .then_inc(row_in[s], 16)

        @block.tensor
        def _(pe):
            pe.wait_ge(w_in, 32)
            for t in range(S + 3):
                if t < S:
                    pe.wait_ge(row_in[t], 32)
                    wait(pe, base_copied, t - 1)
                    for k in range(K):
                        mm = pe.transpose(p_base[t % 2][:, k * P:(k + 1) * P], h[:, t, k * P:(k + 1) * P],
                                          c["ident"][:])
                    mm.then_inc(base_turned, 1)
                if 0 <= t - 1 < S:
                    s = t - 1
                    pe.wait_ge(base_copied, s + 1)
                    wait(pe, masked, s - 1)
                    accumulate(pe, p_exp[s % 2][:, 0:F],
                               [(base_t[s % 2][:, k, :], wexp[:, k, :]) for k in range(K)]).then_inc(expanded, 1)
                if 0 <= t - 2 < S:
                    s = t - 2
                    pe.wait_ge(masked, s + 1)
                    wait(pe, kept_copied, s - 1)
                    for k in range(K):
                        mm = pe.transpose(p_kept[s % 2][:, k * P:(k + 1) * P],
                                          kept[s % 2][:, k * P:(k + 1) * P], c["ident"][:])
                    mm.then_inc(kept_turned, 1)
                if 0 <= t - 3 < S:
                    s = t - 3
                    pe.wait_ge(kept_copied, s + 1)
                    wait(pe, added, s - 1)
                    accumulate(pe, p_corr[s % 2][:, 0:F],
                               [(kept_t[s % 2][:, k, :], wproj[:, k, :]) for k in range(K)]).then_inc(corrected, 1)

        @block.scalar
        def _(act):
            for t in range(S + 2):
                if t < S:
                    act.wait_ge(base_turned, t + 1)
                    wait(act, expanded, t - 1)
                    act.copy(base_t[t % 2][:], p_base[t % 2][:, 0:F]
                             .rearrange("p (k c) -> p k c", k=K)).then_inc(base_copied, 1)
                if t >= 2:
                    s = t - 2
                    act.wait_ge(kept_turned, s + 1)
                    wait(act, corrected, s - 1)
                    act.copy(kept_t[s % 2][:], p_kept[s % 2][:, 0:F]
                             .rearrange("p (k c) -> p k c", k=K)).then_inc(kept_copied, 1)

        @block.vector
        def _(dve):
            for t in range(S + 4):
                if t < S:
                    dve.wait_ge(row_in[t], 32)
                    dve.tensor_copy(dom_f[:, t:t + 1], dom[:, t:t + 1]).then_inc(dom_ok, 1)
                    dve.wait_ge(dom_ok, t + 1)
                    dve.tensor_scalar(keep[:, t, :], c["iota_p"][:, 0:NDOM], dom_f[:, t:t + 1], 0.1,
                                      ALU.is_equal, ALU.mult).then_inc(keep_ok, 1)
                if 0 <= t - 1 < S:
                    s = t - 1
                    dve.wait_ge(expanded, s + 1)
                    dve.wait_ge(keep_ok, s + 1)
                    wait(dve, kept_turned, s - 1)
                    dve.tensor_tensor(kept[s % 2][:].rearrange("p (d e) -> p d e", e=DEXP),
                                      p_exp[s % 2][:, 0:F].rearrange("p (d e) -> p d e", e=DEXP),
                                      keep[:, s, :].unsqueeze(2).to_broadcast([P, NDOM, DEXP]),
                                      ALU.mult).then_inc(masked, 1)
                if 0 <= t - 3 < S:
                    s = t - 3
                    dve.wait_ge(corrected, s + 1)
                    dve.tensor_tensor(h[:, s, :], h[:, s, :], p_corr[s % 2][:, 0:F], ALU.add)\
                        .then_inc(added, 1)
                if t >= 4:
                    dve.wait_ge(added, t - 3)
                    stats.rows(dve, t - 4)
    sp.close()


class Stats:

    def __init__(self, sp, h):
        self.h = h
        self.stats, self.mv = sp.sb("stats", [P, S, 6]), sp.sb("mv", [P, S, 2])

    def open(self, sp):
        self.taken = sp.sem("stats_taken")

    def rows(self, dve, s):
        dve.bn_stats(self.stats[:, s, :], self.h[:, s, :]).then_inc(self.taken, 1)
        if s >= 1:
            self.aggregate(dve, s - 1)
        if s == S - 1:
            self.aggregate(dve, s)

    def aggregate(self, dve, s):
        dve.wait_ge(self.taken, s + 1)
        dve.bn_aggr(self.mv[:, s, :], self.stats[:, s, :])


class Norm:

    def __init__(self, sp, c, h, mv, x_hi, x_lo, grouped, bank, keep=None):
        self.c, self.h, self.x_hi, self.x_lo, self.grouped, self.keep = c, h, x_hi, x_lo, grouped, keep
        self.mv = mv
        self.var = sp.sb("ln_var", [P, S])
        self.std = sp.sb("ln_std", [P, S])
        self.rstd = sp.sb("ln_rstd", [P, S])
        self.xn = sp.sb("ln_xn", [P, 4, F])
        self.bank = bank
        self.var_ok = sp.sem("ln_var_ok")
        self.std_ok, self.rstd_ok = sp.sem("ln_std_ok"), sp.sem("ln_rstd_ok")
        self.xn_ok, self.turned = sp.sem("ln_xn_ok"), sp.sem("ln_turned")
        self.hi_ok, self.lo_ok = sp.sem("ln_hi_ok"), sp.sem("ln_lo_ok")
        if keep:
            self.rest = sp.sb("ln_rest", [P, 4, F])
            self.kept, self.rest_ok, self.kept3 = sp.sem("ln_kept"), sp.sem("ln_rest_ok"), sp.sem("ln_kept3")

    def columns(self, x, s):
        if self.grouped:
            return group_view(x)[:, :, :, s, :]
        return x[:, :, s * P:(s + 1) * P].rearrange("p k (g c) -> p k g c", c=GB)

    def turned_bank(self, s):
        return self.bank[s % 4][:, 0:F].rearrange("p (k g c) -> p k g c", k=K, c=GB)

    def vector(self, dve):
        dve.tensor_scalar_add(self.var[:], self.mv[:, :, 1], EPS).then_inc(self.var_ok, 1)
        dve.wait_ge(self.std_ok, 1)
        dve.reciprocal(self.rstd[:], self.std[:]).then_inc(self.rstd_ok, 1)
        dve.wait_ge(self.rstd_ok, 1)
        LAG = 2
        for s in range(S + LAG):
            if s < S:
                wait(dve, self.turned, s - 3)
                if self.keep:
                    wait(dve, self.rest_ok, s - 3)
                dve.tensor_scalar(self.xn[:, s % 4, :], self.h[:, s, :], self.mv[:, s, 0:1],
                                  self.rstd[:, s:s + 1], ALU.subtract, ALU.mult).then_inc(self.xn_ok, 1)
            if s >= LAG:
                z = s - LAG
                dve.wait_ge(self.hi_ok, z + 1)
                dve.tensor_tensor(self.columns(self.x_lo, z), self.turned_bank(z),
                                  self.columns(self.x_hi, z).bitcast(F32), ALU.subtract)\
                    .then_inc(self.lo_ok, 1)
                if self.keep and z >= 2:
                    self.third(dve, z - 2)
        if self.keep:
            for z in (S - 2, S - 1):
                self.third(dve, z)

    def third(self, dve, s):
        dve.wait_ge(self.kept, min(2 * s + 3, 2 * S))
        dve.tensor_tensor(self.keep[2][:, s, :], self.rest[:, s % 4, :], self.keep[1][:, s, :], ALU.subtract)\
            .then_inc(self.kept3, 1)

    def second(self, act, s):
        act.wait_ge(self.rest_ok, s + 1)
        act.copy(self.keep[1][:, s, :], self.rest[:, s % 4, :]).then_inc(self.kept, 1)

    def gpsimd(self, pool):
        for s in range(S):
            pool.wait_ge(self.kept, 2 * s + 1 if s == 0 else 2 * s)
            wait(pool, self.kept3, s - 3)
            pool.tensor_tensor(self.rest[:, s % 4, :], self.xn[:, s % 4, :], self.keep[0][:, s, :], ALU.subtract)\
                .then_inc(self.rest_ok, 1)

    def scalar(self, act, beside=None):
        act.wait_ge(self.var_ok, 1)
        act.activation(self.std[:], self.var[:], ACT.Sqrt).then_inc(self.std_ok, 1)
        for s in range(S):
            act.wait_ge(self.turned, s + 1)
            act.copy(self.columns(self.x_hi, s), self.turned_bank(s)).then_inc(self.hi_ok, 1)
            if self.keep:
                act.copy(self.keep[0][:, s, :], self.xn[:, s % 4, :]).then_inc(self.kept, 1)
                if s >= 1:
                    self.second(act, s - 1)
            if beside:
                beside(s)
        if self.keep:
            self.second(act, S - 1)

    def tensor(self, pe, beside=None):
        for s in range(S):
            pe.wait_ge(self.xn_ok, s + 1)
            wait(pe, self.lo_ok, s - 3)
            for k in range(K):
                mm = pe.transpose(self.bank[s % 4][:, k * P:(k + 1) * P],
                                  self.xn[:, s % 4, k * P:(k + 1) * P], self.c["ident"][:])
            mm.then_inc(self.turned, 1)
            if beside:
                beside(s)


def build_attention0(nc, c, h, stats, w_d, wv_d, bqk_d, bv_d, wo_d, bo_d):
    with ExitStack() as ctx:
        sp = Space(nc, ctx, "a0")
        x_hi, x_lo = sp.sb("x_hi", [P, K, T], F32R), sp.sb("x_lo", [P, K, T], F32R)
        w_raw = [sp.sb(f"w_raw{i}", [P, K, 2 * P]) for i in range(2)]
        w_hi, w_lo = sp.sb("w_hi", [P, K, 2 * P], F32R), sp.sb("w_lo", [P, K, 2 * P], F32R)
        wv, wv_hi, wv_lo = sp.sb("wv", [P, K, VB]), sp.sb("wv_hi", [P, K, VB], F32R), sp.sb("wv_lo", [P, K, VB], F32R)
        bqk = sp.sb("bqk", [P, PAIRS, 2])
        bias = sp.sb("bias", [P, 2])
        bv = sp.sb("bv", [P, H0 * D0])
        bo = sp.sb("bo", [P, F])
        wo = sp.sb("wo", [P, PAIRS, F])
        wo_hi, wo_lo = sp.sb("wo_hi", [P, F], F32R), sp.sb("wo_lo", [P, F], F32R)
        q_k = [sp.sb(f"q_k{i}", [P, 2, T]) for i in range(2)]
        v = sp.sb("v", [P, 2, NG, 4, VW0])
        prob = [sp.sb(f"prob{i}", [P, 4, P]) for i in range(4)]
        prob_t = [sp.sb(f"prob_t{i}", [P, 4, P]) for i in range(2)]
        top = [sp.sb(f"top{i}", [P, 4]) for i in range(2)]
        inv = [sp.sb(f"inv{i}", [P, 4]) for i in range(2)]
        o = [sp.sb(f"o{i}", [P, NG, P]) for i in range(2)]
        ot_hi, ot_lo = sp.sb("ot_hi", [P, T], F32R), sp.sb("ot_lo", [P, T], F32R)
        p_s = [sp.ps(f"p_s{i}", [P, BANK]) for i in range(2)]
        p_t, p_o = sp.ps("p_t", [P, BANK]), sp.ps("p_o", [P, BANK])
        p_qk, p_v = sp.ps("p_qk", [P, BANK]), sp.ps("p_v", [P, BANK])
        p_out = [sp.ps(f"p_out{i}", [P, BANK]) for i in range(2)]
        stats.open(sp)
        norm = Norm(sp, c, h, stats.mv, x_hi, x_lo, True, p_out + p_s)

        w_in = [sp.sem(f"w_in{i}") for i in range(2)]
        wv_in, wv_hi_ok, wv_lo_ok = sp.sem("wv_in"), sp.sem("wv_hi_ok"), sp.sem("wv_lo_ok")
        small_in, ones_ok, bo_ok = sp.sem("small_in"), sp.sem("ones_ok"), sp.sem("bo_ok")
        bias_ok = sp.sem("bias_ok")
        w_hi_ok, w_lo_ok = sp.sem("w_hi_ok"), sp.sem("w_lo_ok")
        wo_hi_ok, wo_lo_ok = sp.sem("wo_hi_ok"), sp.sem("wo_lo_ok")
        qk_made, qk_copied = sp.sem("qk_made"), sp.sem("qk_copied")
        v_made, v_copied = sp.sem("v_made"), sp.sem("v_copied")
        scored, top_ok, shifted, exped = sp.sem("scored"), sp.sem("top_ok"), sp.sem("shifted"), sp.sem("exped")
        turned, t_copied = sp.sem("turned"), sp.sem("t_copied")
        valued, inv_ok, o_ok = sp.sem("valued"), sp.sem("inv_ok"), sp.sem("o_ok")
        o_turned, ot_hi_ok, ot_lo_ok = sp.sem("o_turned"), sp.sem("ot_hi_ok"), sp.sem("ot_lo_ok")
        out_made, out_added = sp.sem("out_made"), sp.sem("out_added")
        block = ctx.enter_context(nc.Block())

        def run(engine, unit):
            unit(-1, 1, -1, project=True, project_vs=True, attend=False, finish=False)
            unit(0, 0, 0, project=True, project_vs=True, attend=True, finish=False)
            unit(1, 1, 0, project=True, project_vs=True, attend=True, finish=True)
            with engine.Fori(1, PAIRS // 2 - 1) as i:
                unit(2 * i, 0, i, project=True, project_vs=True, attend=True, finish=True)
                unit(2 * i + 1, 1, i, project=True, project_vs=True, attend=True, finish=True)
            blk = PAIRS // 2 - 1
            unit(PAIRS - 2, 0, blk, project=True, project_vs=False, attend=True, finish=True)
            unit(PAIRS - 1, 1, blk, project=False, project_vs=False, attend=True, finish=True)
            unit(PAIRS, 0, blk + 1, project=False, project_vs=False, attend=False, finish=True)

        def attends(p):
            return not isinstance(p, int) or p >= 0

        def v_heads(blk):
            return v[:, blk % 2] if isinstance(blk, int) else v[:, bass.ds(blk & 1, 1)].squeeze(1)

        def v_steps(p, j):
            n = 8 * p + (8 if j >= 3 else 0)
            return min(n, 8 * (PAIRS - 1)) if isinstance(p, int) else n

        def turns(j, attend, finish):
            return (attend and j >= 2) or (finish and j < 2)

        def values(j, attend, finish):
            return (attend and j >= 3) or (finish and j < 3)

        def ungrouped(x, j):
            return x[:].rearrange("p (t g c) -> p g t c", t=S, g=NG)[:, 4 * j:4 * j + 4, :, :]

        def out_view(bank):
            return bank[:].rearrange("p (g t c) -> p g t c", t=S, c=GB)

        @block.sync
        def _(sync):
            for p in range(2):
                sync.dma_start(w_raw[p][:], w_d[p]).then_inc(w_in[p], 16)
            sync.dma_start(wv[:], wv_d[0]).then_inc(wv_in, 16)
            for dst, src in ((bqk[:], bqk_d), (bv[:], bv_d[0:1].partition_broadcast(P)),
                             (bo[:], bo_d[0:1].partition_broadcast(P)), (wo[:], wo_d)):
                sync.dma_start(dst, src).then_inc(small_in, 16)
            for p in range(2, PAIRS):
                sync.wait_ge(w_lo_ok, p - 1)
                sync.dma_start(w_raw[p % 2][:], w_d[p]).then_inc(w_in[p % 2], 16)
                if p % 2 == 0:
                    sync.wait_ge(wv_lo_ok, p // 2)
                    sync.dma_start(wv[:], wv_d[p // 2]).then_inc(wv_in, 16)

        @block.gpsimd
        def _(pool):
            for i in range(2):
                pool.memset(v[:, i, :, :, D0:VW0], 1.0).then_inc(ones_ok, 1)
            pool.wait_ge(norm.xn_ok, S)
            pool.wait_ge(small_in, 64)
            for s in range(S):
                pool.tensor_tensor(h[:, s, :], h[:, s, :], bo[:], ALU.add).then_inc(bo_ok, 1)

        @block.tensor
        def _(pe):
            norm.tensor(pe)
            pe.wait_ge(norm.lo_ok, S)
            pe.wait_ge(ones_ok, 2)

            def project_qk(p, j):
                pe.wait_ge(w_lo_ok, p + 1)
                wait(pe, qk_copied, 8 * p + j)
                cols = slice((j // 4) * P, (j // 4 + 1) * P)
                toks = slice((j % 4) * BANK, (j % 4 + 1) * BANK)
                accumulate(pe, p_qk[:], [t for k in range(K) for t in three(
                    w_hi[:, k, cols], w_lo[:, k, cols], x_hi[:, k, toks], x_lo[:, k, toks])]).then_inc(qk_made, 1)

            def project_v(p, par, blk, j):
                pe.wait_ge(wv_lo_ok, blk + 2)
                wait(pe, v_copied, 8 * (p + 1) + j)
                groups = (8 * par + j,) if attends(p) else (2 * j, 2 * j + 1)
                for n, g in enumerate(groups):
                    toks = slice(g * P, (g + 1) * P)
                    mm = accumulate(pe, p_v[:, n * VB:(n + 1) * VB], [t for k in range(K) for t in three(
                        x_hi[:, k, toks], x_lo[:, k, toks], wv_hi[:, k, :], wv_lo[:, k, :])])
                mm.then_inc(v_made, 1)

            def project_out(p, q):
                pe.wait_ge(ot_lo_ok, 4 * p + 4)
                pe.wait_ge(wo_lo_ok, p + 1)
                if q >= 2:
                    pe.wait_ge(out_added, 8 * p + q - 1)
                for t in range(2):
                    toks = slice((2 * q + t) * P, (2 * q + t + 1) * P)
                    mm = accumulate(pe, p_out[q % 2][:, t * F:(t + 1) * F],
                                    three(ot_hi[:, toks], ot_lo[:, toks], wo_hi[:], wo_lo[:]))
                mm.then_inc(out_made, 1)

            def unit(p, par, blk, project, project_vs, attend, finish):
                for j in range(8):
                    g = 8 * p + j
                    if turns(j, attend, finish):
                        pe.wait_ge(exped, g - 1)
                        wait(pe, t_copied, g - 2)
                        for n in range(4):
                            mm = pe.transpose(p_t[:, n * P:(n + 1) * P], prob[(j - 2) % 4][:, n, :], c["ident"][:])
                        mm.then_inc(turned, 1)
                    if values(j, attend, finish):
                        jj, vp = (j - 3) % 8, par if j >= 3 else 1 - par
                        vs = v_heads(blk if j >= 3 or par == 1 else blk + 1)
                        pe.wait_ge(t_copied, g - 2)
                        pe.wait_ge(v_copied, v_steps(p, j))
                        wait(pe, o_ok, g - 3)
                        for n in range(4):
                            mm = pe.matmul(p_o[:, n * VW0:(n + 1) * VW0], prob_t[jj % 2][:, n, :],
                                           vs[:, 4 * (jj % 4) + n, 2 * vp + jj // 4, :], start=True, stop=True)
                        mm.then_inc(valued, 1)
                    if finish and j < 4:
                        pe.wait_ge(o_ok, 8 * p - 3 + j)
                        if j < 2:
                            wait(pe, out_added, 8 * p - 8)
                        else:
                            pe.wait_ge(ot_lo_ok, 4 * p - 4 + j - 1)
                        for n in range(4):
                            mm = pe.transpose(p_out[j % 2][:, n * P:(n + 1) * P], o[1 - par][:, 4 * j + n, :],
                                              c["ident"][:])
                        mm.then_inc(o_turned, 1)
                    if attend:
                        rows = slice((j // 4) * D0, (j // 4 + 1) * D0)
                        pe.wait_ge(qk_copied, 8 * p + 8)
                        wait(pe, shifted, g - 1)
                        pe.matmul(p_s[j % 2][:], c["ident_b"][:], c["mask"][:].unsqueeze(1).to_broadcast([P, 4, P]),
                                  start=True, stop=False, skip_group_check=True)
                        for n in range(4):
                            toks = slice((4 * (j % 4) + n) * P, (4 * (j % 4) + n + 1) * P)
                            mm = pe.matmul(p_s[j % 2][:, n * P:(n + 1) * P], q_k[par][rows, 0, toks],
                                           q_k[par][rows, 1, toks], start=False, stop=n == 3,
                                           skip_group_check=True)
                        mm.then_inc(scored, 1)
                    if project:
                        project_qk(p + 1, j)
                    if finish and j >= 4:
                        project_out(p - 1, 2 * (j - 4))
                    if project_vs:
                        project_v(p, par, blk, j)
                    if finish and j >= 4:
                        project_out(p - 1, 2 * (j - 4) + 1)

            run(pe, unit)

        @block.scalar
        def _(act):
            norm.scalar(act)
            act.wait_ge(small_in, 64)

            def unit(p, par, blk, project, project_vs, attend, finish):
                if project:
                    act.wait_ge(w_in[1 - par], 8 * (p + 1 - (1 - par)) + 16)
                    wait(act, qk_copied, 8 * (p + 1))
                    act.copy(w_hi[:], w_raw[1 - par][:]).then_inc(w_hi_ok, 1)
                    act.copy(bias[:], bqk[:, p + 1, :] if isinstance(p, int) else
                             bqk[:, bass.ds(p + 1, 1), :].squeeze(1)).then_inc(bias_ok, 1)
                if project_vs and (par == 0 or not attends(p)):
                    act.wait_ge(wv_in, 16 * blk + 32)
                    wait(act, v_made, 8 * (p + 1))
                    act.copy(wv_hi[:], wv[:]).then_inc(wv_hi_ok, 1)
                for j in range(8):
                    g = 8 * p + j
                    if turns(j, attend, finish):
                        act.wait_ge(turned, g - 1)
                        wait(act, valued, g - 3)
                        act.copy(prob_t[j % 2][:], p_t[:].rearrange("p (n c) -> p n c", n=4))\
                            .then_inc(t_copied, 1)
                    if finish and j < 4:
                        act.wait_ge(o_turned, 4 * p - 4 + j + 1)
                        wait(act, out_made, 8 * p - 8)
                        act.copy(ungrouped(ot_hi, j), out_view(p_out[j % 2])).then_inc(ot_hi_ok, 1)
                    if finish and j == 2:
                        act.copy(wo_hi[:], wo[:, p - 1, :] if isinstance(p, int) else
                                 wo[:, bass.ds(p - 1, 1), :].squeeze(1)).then_inc(wo_hi_ok, 1)
                    if attend:
                        act.wait_ge(shifted, g + 1)
                        act.activation(prob[j % 4][:], prob[j % 4][:], ACT.Exp, scale=float(D0) ** -0.5)\
                            .then_inc(exped, 1)
                    if project:
                        act.wait_ge(qk_made, 8 * (p + 1) + j + 1)
                        wait(act, scored, 8 * p)
                        if j == 0:
                            act.wait_ge(bias_ok, p + 2)
                        act.activation(q_k[1 - par][:, j // 4, (j % 4) * BANK:(j % 4 + 1) * BANK], p_qk[:],
                                       ACT.Identity, bias=bias[:, j // 4:j // 4 + 1]).then_inc(qk_copied, 1)

            run(act, unit)

        @block.vector
        def _(dve):
            norm.vector(dve)
            dve.wait_ge(small_in, 64)

            def copy_v(p, par, blk, j):
                dve.wait_ge(v_made, 8 * (p + 1) + j + 1)
                if attends(p):
                    wait(dve, valued, 8 * (p - par) - 3 + (8 * par + j) // 4)
                    groups = slice(8 * par + j, 8 * par + j + 1)
                else:
                    groups = slice(2 * j, 2 * j + 2)
                n = groups.stop - groups.start
                b = bv[:, bass.ds((blk + 1) * VB, VB)] if not isinstance(p, int) else \
                    bv[:, (blk + 1) * VB:(blk + 2) * VB]
                dve.tensor_tensor(v_heads(blk + 1)[:, groups, :, 0:D0],
                                  p_v[:, 0:n * VB].rearrange("p (g e d) -> p g e d", g=n, e=4),
                                  b.rearrange("p (e d) -> p e d", e=4).unsqueeze(1).to_broadcast([P, n, 4, D0]),
                                  ALU.add).then_inc(v_copied, 1)

            def rows_after(q, p):
                if q >= 0:
                    dve.wait_ge(out_added, 8 * p - 8 + q + 1)
                    for s in (2 * q, 2 * q + 1):
                        stats.rows(dve, s)

            def unit(p, par, blk, project, project_vs, attend, finish):
                if project:
                    dve.wait_ge(w_hi_ok, p + 2)
                    dve.tensor_tensor(w_lo[:], w_raw[1 - par][:], w_hi[:].bitcast(F32), ALU.subtract)\
                        .then_inc(w_lo_ok, 1)
                if project_vs and (par == 0 or not attends(p)):
                    dve.wait_ge(wv_hi_ok, blk + 2)
                    dve.tensor_tensor(wv_lo[:], wv[:], wv_hi[:].bitcast(F32), ALU.subtract).then_inc(wv_lo_ok, 1)
                for j in range(8):
                    g = 8 * p + j
                    if values(j, attend, finish):
                        jj, op = (j - 3) % 8, par if j >= 3 else 1 - par
                        dve.wait_ge(valued, g - 2)
                        if j == 3:
                            wait(dve, o_turned, 4 * p - 4)
                        po = p_o[:, 0:4 * VW0].rearrange("p (n d) -> p n d", n=4)
                        dve.reciprocal(inv[j % 2][:], po[:, :, D0]).then_inc(inv_ok, 1)
                        dve.wait_ge(inv_ok, g - 2)
                        dve.tensor_tensor(o[op][:, 4 * (jj % 4):4 * (jj % 4) + 4, (jj // 4) * D0:(jj // 4 + 1) * D0],
                                          po[:, :, 0:D0], inv[j % 2][:].unsqueeze(2).to_broadcast([P, 4, D0]),
                                          ALU.mult).then_inc(o_ok, 1)
                    if attend:
                        ps = p_s[j % 2][:].rearrange("p (n c) -> p n c", n=4)
                        dve.wait_ge(scored, g + 1)
                        dve.tensor_reduce(top[j % 2][:], ps, axis=X, op=ALU.max).then_inc(top_ok, 1)
                        dve.wait_ge(top_ok, g + 1)
                        wait(dve, turned, g - 3)
                        dve.tensor_tensor(prob[j % 4][:], ps, top[j % 2][:].unsqueeze(2).to_broadcast([P, 4, P]),
                                          ALU.subtract).then_inc(shifted, 1)
                    if finish and j < 4:
                        dve.wait_ge(ot_hi_ok, 4 * p - 4 + j + 1)
                        dve.tensor_tensor(ungrouped(ot_lo, j), out_view(p_out[j % 2]),
                                          ungrouped(ot_hi, j).bitcast(F32), ALU.subtract)\
                            .then_inc(ot_lo_ok, 1)
                    if finish and j == 2:
                        w = wo[:, p - 1, :] if isinstance(p, int) else wo[:, bass.ds(p - 1, 1), :].squeeze(1)
                        dve.wait_ge(wo_hi_ok, p)
                        dve.tensor_tensor(wo_lo[:], w, wo_hi[:].bitcast(F32), ALU.subtract).then_inc(wo_lo_ok, 1)
                    if project_vs:
                        copy_v(p, par, blk, j)
                    if finish and j >= 4:
                        for q in (2 * (j - 4), 2 * (j - 4) + 1):
                            dve.wait_ge(out_made, 8 * p - 8 + q + 1)
                            dve.wait_ge(bo_ok, S)
                            dve.tensor_tensor(h[:, 2 * q:2 * q + 2, :], h[:, 2 * q:2 * q + 2, :],
                                              p_out[q % 2][:].rearrange("p (t f) -> p t f", t=2), ALU.add)\
                                .then_inc(out_added, 1)
                            if not project and not attend:
                                rows_after(q - 1, p)

            run(dve, unit)
            rows_after(S // 2 - 1, PAIRS)
    sp.close()


def build_ffn0(nc, c, h, stats, gate_d, gate_b_d, w_d, b1_d, b2_d):
    NE = E0 + 1
    with ExitStack() as ctx:
        sp = Space(nc, ctx, "f0")
        x_hi, x_lo = sp.sb("x_hi", [P, K, T], F32R), sp.sb("x_lo", [P, K, T], F32R)
        gate = sp.sb("gate", [P, K, E0])
        gate_hi, gate_lo = sp.sb("gate_hi", [P, K, E0], F32R), sp.sb("gate_lo", [P, K, E0], F32R)
        gate_b = sp.sb("gate_b", [P, E0])
        b1 = sp.sb("b1", [P, NE, K])
        b1_now = [sp.sb(f"b1_now{i}", [P, K]) for i in range(2)]
        b2 = sp.sb("b2", [NE, F])
        logit, prob = sp.sb("logit", [P, S, E0]), sp.sb("prob", [P, S, E0])
        row = sp.sb("row", [P, S])
        best, best_i = sp.sb("best", [P, S, 8]), sp.sb("best_i", [P, S, 8], U32)
        best_f, pick = sp.sb("best_f", [P, S, 8]), sp.sb("pick", [P, S, E0])
        combine = sp.sb("combine", [P, S, NE])
        combine_t = sp.sb("combine_t", [NE, T])
        w_raw = [sp.sb(f"w_raw{i}", [P, 2, K, F]) for i in range(2)]
        w_hi = [sp.sb(f"w_hi{i}", [P, 2, K, F], F32R) for i in range(2)]
        w_lo = [sp.sb(f"w_lo{i}", [P, 2, K, F], F32R) for i in range(2)]
        hid = [sp.sb(f"hid{i}", [P, K, BANK]) for i in range(2)]
        hid_hi = [sp.sb(f"hid_hi{i}", [P, K, BANK], F32R) for i in range(2)]
        hid_lo = [sp.sb(f"hid_lo{i}", [P, K, BANK], F32R) for i in range(2)]
        p_hid = [[sp.ps(f"p_hid{i}{m}", [P, BANK]) for m in range(K)] for i in range(2)]
        p_y = [sp.ps(f"p_y{i}", [P, BANK]) for i in range(2)]
        p_misc = [sp.ps(f"p_misc{i}", [P, BANK]) for i in range(2)]
        stats.open(sp)
        p_gate = p_y[1]
        norm = Norm(sp, c, h, stats.mv, x_hi, x_lo, False, p_misc + p_hid[1])

        w_in = [sp.sem(f"w_in{i}") for i in range(2)]
        small_in, one_ok = sp.sem("small_in"), sp.sem("one_ok")
        gate_hi_ok, gate_lo_ok = sp.sem("gate_hi_ok"), sp.sem("gate_lo_ok")
        logits_made, gate_shifted, gate_exped = sp.sem("logits_made"), sp.sem("gate_shifted"), sp.sem("gate_exped")
        gate_chain, combine_ok = sp.sem("gate_chain"), sp.sem("combine_ok")
        combine_turned, combine_copied = sp.sem("combine_turned"), sp.sem("combine_copied")
        w_hi_ok, w_lo_ok, b1_ok = sp.sem("w_hi_ok"), sp.sem("w_lo_ok"), sp.sem("b1_ok")
        hid_made, hid_ok = sp.sem("hid_made"), sp.sem("hid_ok")
        hid_hi_ok, hid_lo_ok = sp.sem("hid_hi_ok"), sp.sem("hid_lo_ok")
        b2_made, b2_added = sp.sem("b2_made"), sp.sem("b2_added")
        y_made, y_added = sp.sem("y_made"), sp.sem("y_added")
        block = ctx.enter_context(nc.Block())

        def run(engine, expert):
            expert(0, 0, True)
            with engine.Fori(0, (NE - 3) // 2) as i:
                expert(2 * i + 1, 1, True)
                expert(2 * i + 2, 0, True)
            expert(NE - 2, 1, True)
            expert(NE - 1, 0, False)

        @block.sync
        def _(sync):
            for dst, src in ((gate[:], gate_d), (gate_b[:], gate_b_d[0:1].partition_broadcast(P)),
                             (b1[:], b1_d), (b2[:], b2_d)):
                sync.dma_start(dst, src).then_inc(small_in, 16)
            for e in range(NE):
                wait(sync, w_lo_ok, e - 1)
                sync.dma_start(w_raw[e % 2][:], w_d[e]).then_inc(w_in[e % 2], 16)

        @block.gpsimd
        def _(pool):
            pool.memset(combine[:, :, 0:1], 1.0).then_inc(one_ok, 1)
            pool.wait_ge(gate_hi_ok, 1)
            pool.tensor_tensor(gate_lo[:], gate[:], gate_hi[:].bitcast(F32), ALU.subtract).then_inc(gate_lo_ok, 1)
            pool.wait_ge(w_hi_ok, 1)
            pool.tensor_tensor(w_lo[0][:], w_raw[0][:], w_hi[0][:].bitcast(F32), ALU.subtract).then_inc(w_lo_ok, 1)

        @block.tensor
        def _(pe):
            def gate(s):
                pe.wait_ge(norm.lo_ok, s + 1)
                pe.wait_ge(gate_lo_ok, 1)
                toks = slice(s * P, (s + 1) * P)
                mm = accumulate(pe, p_gate[:, s * E0:(s + 1) * E0], [t for k in range(K) for t in three(
                    x_hi[:, k, toks], x_lo[:, k, toks], gate_hi[:, k, :], gate_lo[:, k, :])])
                if s == S - 1:
                    mm.then_inc(logits_made, 1)

            LAG = 5
            norm.tensor(pe, beside=lambda s: gate(s - LAG) if s >= LAG else None)
            for s in range(S - LAG, S):
                gate(s)

            def hidden(e, par, cc):
                n = 4 * e + cc
                toks = slice(cc * BANK, (cc + 1) * BANK)
                if cc == 0:
                    pe.wait_ge(w_lo_ok, e + 1)
                for m in range(K):
                    wait(pe, hid_hi_ok, 2 * n + m - 3)
                    accumulate(pe, p_hid[cc % 2][m][:], [t for k in range(K) for t in three(
                        w_hi[par][:, 0, k, m * P:(m + 1) * P], w_lo[par][:, 0, k, m * P:(m + 1) * P],
                        x_hi[:, k, toks], x_lo[:, k, toks])]).then_inc(hid_made, 1)

            def output(e, par, cc):
                n = 4 * e + cc
                pe.wait_ge(hid_lo_ok, 2 * n + 2)
                for b in range(2):
                    wait(pe, y_added, 4 * n + 2 * b - 2)
                    for t in range(2):
                        toks = slice((2 * b + t) * P, (2 * b + t + 1) * P)
                        mm = accumulate(pe, p_y[b][:, t * F:(t + 1) * F], [t3 for k in range(K) for t3 in three(
                            hid_hi[cc % 2][:, k, toks], hid_lo[cc % 2][:, k, toks],
                            w_hi[par][:, 1, k, :], w_lo[par][:, 1, k, :])])
                    mm.then_inc(y_made, 1)

            def turn_combine(i):
                pe.wait_ge(combine_ok, 1)
                wait(pe, combine_copied, i)
                for t in range(4):
                    mm = pe.transpose(p_misc[0][0:NE, t * P:(t + 1) * P], combine[:, 4 * i + t, :], c["ident"][:])
                mm.then_inc(combine_turned, 1)

            def weigh_b2(cc):
                pe.wait_ge(combine_copied, 4)
                for i in (2 * cc, 2 * cc + 1):
                    wait(pe, b2_added, i - 1)
                    for t in range(2):
                        toks = slice((2 * i + t) * P, (2 * i + t + 1) * P)
                        mm = pe.matmul(p_misc[i % 2][:, t * F:(t + 1) * F], combine_t[:, toks], b2[:],
                                       start=True, stop=True)
                    mm.then_inc(b2_made, 1)

            def expert(e, par, more):
                for cc in range(4):
                    if cc < 3:
                        hidden(e, par, cc + 1)
                    elif more:
                        hidden(e + 1, 1 - par, 0)
                    if isinstance(e, int) and e == NE - 1:
                        weigh_b2(cc)
                    output(e, par, cc)
                    if isinstance(e, int) and e == NE - 2:
                        turn_combine(cc)

            hidden(0, 0, 0)
            pe.wait_ge(gate_chain, 1)
            run(pe, expert)

        @block.scalar
        def _(act):
            act.wait_ge(small_in, 64)
            act.copy(gate_hi[:], gate[:]).then_inc(gate_hi_ok, 1)

            def cut(e, par):
                act.wait_ge(w_in[par], 8 * (e - par) + 16)
                wait(act, y_made, 8 * (e - 1))
                wait(act, hid_hi_ok, 8 * (e - 1))
                act.copy(w_hi[par][:], w_raw[par][:]).then_inc(w_hi_ok, 1)
                act.copy(b1_now[par][:], b1[:, e, :] if isinstance(e, int) else
                         b1[:, bass.ds(e, 1), :].squeeze(1)).then_inc(b1_ok, 1)

            def gelu(e, par, cc):
                n = 4 * e + cc
                for m in range(K):
                    act.wait_ge(hid_made, 2 * n + m + 1)
                    if cc == 0:
                        act.wait_ge(b1_ok, e + 1)
                    wait(act, hid_lo_ok, 2 * n + m - 3)
                    act.activation(hid[cc % 2][:, m, :], p_hid[cc % 2][m][:], ACT.Gelu,
                                   bias=b1_now[par][:, m:m + 1]).then_inc(hid_ok, 1)
                    wait(act, y_made, 2 * n - 2)
                    act.activation(hid_hi[cc % 2][:, m, :], p_hid[cc % 2][m][:], ACT.Gelu,
                                   bias=b1_now[par][:, m:m + 1]).then_inc(hid_hi_ok, 1)

            def expert(e, par, more):
                for cc in range(4):
                    if cc == 1 and more:
                        cut(e + 1, 1 - par)
                    if cc < 3:
                        gelu(e, par, cc + 1)
                    elif more:
                        gelu(e + 1, 1 - par, 0)
                    if isinstance(e, int) and e == NE - 2:
                        act.wait_ge(combine_turned, cc + 1)
                        act.copy(combine_t[:, cc * BANK:(cc + 1) * BANK], p_misc[0][0:NE, :])\
                            .then_inc(combine_copied, 1)

            norm.scalar(act, beside=lambda s: cut(0, 0) if s == 3 else None)
            act.wait_ge(gate_shifted, 1)
            act.activation(prob[:], prob[:], ACT.Exp).then_inc(gate_exped, 1)
            gelu(0, 0, 0)
            run(act, expert)

        @block.vector
        def _(dve):
            norm.vector(dve)
            wide = [P, S, E0]
            chain = Chain(dve, gate_chain)
            dve.wait_ge(logits_made, 1)
            dve.wait_ge(small_in, 64)
            chain(dve.tensor_tensor(logit[:], p_gate[:, 0:S * E0].rearrange("p (s e) -> p s e", e=E0),
                                    gate_b[:].unsqueeze(1).to_broadcast(wide), ALU.add))
            chain(dve.tensor_reduce(row[:], logit[:], axis=X, op=ALU.max))
            dve.tensor_tensor(prob[:], logit[:], row[:].unsqueeze(2).to_broadcast(wide), ALU.subtract)\
                .then_inc(gate_shifted, 1)

            def gate_part(part):
                if part == 0:
                    dve.wait_ge(gate_exped, 1)
                    chain(dve.tensor_reduce(row[:], prob[:], axis=X, op=ALU.add))
                    chain(dve.reciprocal(row[:], row[:]))
                    chain(dve.tensor_tensor(prob[:], prob[:], row[:].unsqueeze(2).to_broadcast(wide), ALU.mult))
                elif part == 1:
                    for s in range(S):
                        chain.free(dve.max(best[:, s, :], prob[:, s, :]))
                elif part == 2:
                    chain.settle()
                    for s in range(S):
                        chain.free(dve.max_index(best_i[:, s, :], best[:, s, :], prob[:, s, :]))
                else:
                    chain.settle()
                    places = c["iota_p"][:, 0:E0].unsqueeze(1).to_broadcast(wide)
                    routed = combine[:, :, 1:NE]
                    chain(dve.tensor_copy(best_f[:], best_i[:]))
                    chain(dve.tensor_tensor(pick[:], places, best_f[:, :, 0:1].to_broadcast(wide), ALU.is_equal))
                    chain(dve.tensor_tensor(routed, pick[:], best[:, :, 0:1].to_broadcast(wide), ALU.mult))
                    chain(dve.tensor_tensor(pick[:], places, best_f[:, :, 1:2].to_broadcast(wide), ALU.is_equal))
                    chain(dve.tensor_tensor(pick[:], pick[:], best[:, :, 1:2].to_broadcast(wide), ALU.mult))
                    dve.tensor_tensor(routed, routed, pick[:], ALU.add).then_inc(combine_ok, 1)

            def cut_weights(e, par):
                dve.wait_ge(w_hi_ok, e + 1)
                dve.tensor_tensor(w_lo[par][:], w_raw[par][:], w_hi[par][:].bitcast(F32), ALU.subtract)\
                    .then_inc(w_lo_ok, 1)

            def cut_hidden(e, cc):
                n = 4 * e + cc
                for m in range(K):
                    dve.wait_ge(hid_hi_ok, 2 * n + m + 1)
                    dve.tensor_tensor(hid_lo[cc % 2][:, m, :], hid[cc % 2][:, m, :],
                                      hid_hi[cc % 2][:, m, :].bitcast(F32), ALU.subtract).then_inc(hid_lo_ok, 1)

            def add_b2(cc):
                dve.wait_ge(y_added, 16 * (NE - 1) + 4 * cc)
                for i in (2 * cc, 2 * cc + 1):
                    dve.wait_ge(b2_made, i + 1)
                    dve.tensor_tensor(h[:, 2 * i:2 * i + 2, :], h[:, 2 * i:2 * i + 2, :],
                                      p_misc[i % 2][:].rearrange("p (t f) -> p t f", t=2), ALU.add)\
                        .then_inc(b2_added, 1)
                dve.wait_ge(b2_added, 2 * cc + 2)

            def rows_after(cc):
                dve.wait_ge(y_added, 16 * (NE - 1) + 4 * cc + 4)
                for s in range(4 * cc, 4 * cc + 4):
                    stats.rows(dve, s)

            def expert(e, par, more):
                for cc in range(4):
                    n = 4 * e + cc
                    if cc == 1 and more:
                        cut_weights(e + 1, 1 - par)
                    if cc < 3:
                        cut_hidden(e, cc + 1)
                    elif more:
                        cut_hidden(e + 1, 0)
                    first, final = (isinstance(e, int) and e == 0), (isinstance(e, int) and e == NE - 1)
                    if first:
                        gate_part(cc)
                    if cc == 0:
                        dve.wait_ge(one_ok, 1)
                        if not first:
                            dve.wait_ge(combine_ok, 1)
                    if final:
                        add_b2(cc)
                    for t in range(4):
                        s = 4 * cc + t
                        weight = combine[:, s, e:e + 1] if isinstance(e, int) else combine[:, s, bass.ds(e, 1)]
                        dve.wait_ge(y_made, 2 * n + t // 2 + 1)
                        wait(dve, y_added, 4 * n + t - 15)
                        dve.scalar_tensor_tensor(h[:, s, :], p_y[t // 2][:, (t % 2) * F:(t % 2 + 1) * F], weight,
                                                 h[:, s, :], ALU.mult, ALU.add).then_inc(y_added, 1)
                    if final and cc >= 1:
                        rows_after(cc - 1)

            cut_hidden(0, 0)
            run(dve, expert)
            rows_after(3)
    sp.close()


def build_attention1(nc, c, h, stats, wqk_d, bqk_d, wv_d, bv_d, pos_d, wp_d, bp_d, rw_d, rr_d, wo_d, bo_d):
    STEPS = 4 * HG
    JOBS = 12
    with ExitStack() as ctx:
        sp = Space(nc, ctx, "a1")
        x_hi, x_lo = sp.sb("x_hi", [P, K, T], F32R), sp.sb("x_lo", [P, K, T], F32R)
        wqk = [sp.sb(f"wqk{i}", [P, K, 2, P]) for i in range(2)]
        wqk_hi = [sp.sb(f"wqk_hi{i}", [P, K, 2, P], F32R) for i in range(2)]
        wqk_lo = [sp.sb(f"wqk_lo{i}", [P, K, 2, P], F32R) for i in range(2)]
        bqk = sp.sb("bqk", [P, HG, 2])
        wv, wv_hi, wv_lo = sp.sb("wv", [P, K, F]), sp.sb("wv_hi", [P, K, F], F32R), sp.sb("wv_lo", [P, K, F], F32R)
        wo, wo_hi, wo_lo = sp.sb("wo", [P, K, F]), sp.sb("wo_hi", [P, K, F], F32R), sp.sb("wo_lo", [P, K, F], F32R)
        bv, bo = sp.sb("bv", [P, F]), sp.sb("bo", [P, F])
        pos, wp, bp = sp.sb("pos", [P, K, NPOS + 1]), sp.sb("wp", [P, K, HG, P]), sp.sb("bp", [P, HG])
        rw, rr = sp.sb("rw", [P, HG]), sp.sb("rr", [P, HG])
        bq_rr, rw_rr = sp.sb("bq_rr", [P, HG]), sp.sb("rw_rr", [P, HG])
        p_t = sp.sb("p_t", [P, HG, NPOS + 1])
        shift = [sp.sb(f"shift{i}", [P, S, P]) for i in range(2)]
        hot = sp.sb("hot", [P, P])
        q0 = sp.sb("q_rr", [P, T])
        q = [sp.sb(f"q_all{i}", [P, T]) for i in range(2)]
        k1 = [sp.sb(f"k{i}", [P, T]) for i in range(2)]
        v = sp.sb("v", [P, NG, H1, VW1])
        prob = [sp.sb(f"prob{i}", [P, 4, P]) for i in range(3)]
        prob_t = [sp.sb(f"prob_t{i}", [P, 4, P]) for i in range(2)]
        top = [sp.sb(f"top{i}", [P, 4]) for i in range(2)]
        inv = [sp.sb(f"inv{i}", [P, 4]) for i in range(2)]
        o = sp.sb("o", [P, NG, F])
        p_s = [sp.ps(f"p_s{i}", [P, BANK]) for i in range(2)]
        p_turn, p_o = sp.ps("p_turn", [P, BANK]), sp.ps("p_o", [P, BANK])
        p_work = [sp.ps(f"p_work{i}", [P, BANK]) for i in range(2)]
        p_out = [sp.ps(f"p_out{i}", [P, BANK]) for i in range(2)]
        stats.open(sp)
        norm = Norm(sp, c, h, stats.mv, x_hi, x_lo, True, p_out + p_s)

        w_in = [sp.sem(f"w_in{i}") for i in range(2)]
        small_in, pool_ok, bo_ok = sp.sem("small_in"), sp.sem("pool_ok"), sp.sem("bo_ok")
        const_hi, const_lo, bias_ok = sp.sem("const_hi"), sp.sem("const_lo"), sp.sem("bias_ok")
        pos_made, pos_ok, shift_ok = sp.sem("pos_made"), sp.sem("pos_ok"), sp.sem("shift_ok")
        w_hi_ok, w_lo_ok = sp.sem("w_hi_ok"), sp.sem("w_lo_ok")
        work_made, work_free = sp.sem("work_made"), [sp.sem(f"work_free{i}") for i in range(2)]
        scored, top_ok, shifted, exped = sp.sem("scored"), sp.sem("top_ok"), sp.sem("shifted"), sp.sem("exped")
        turned, t_copied = sp.sem("turned"), sp.sem("t_copied")
        valued, inv_ok, o_ok = sp.sem("valued"), sp.sem("inv_ok"), sp.sem("o_ok")
        o_turned, ot_hi_ok, ot_lo_ok = sp.sem("o_turned"), sp.sem("ot_hi_ok"), sp.sem("ot_lo_ok")
        out_made, out_added = sp.sem("out_made"), sp.sem("out_added")
        block = ctx.enter_context(nc.Block())
        NV = NG // 2

        def job(u, i):
            return NV + JOBS * u + i

        def steps(step):
            for u in range(-1, HG + 1):
                for j in range(STEPS if u < HG else 4):
                    step(u, j, STEPS * u + j)

        def freed(bank_job):
            return bank_job // 2

        def outs(u, j):
            if u == HG - 1 and 4 <= j < 8:
                return j - 4
            if u == HG and j < 4:
                return 4 + j
            return None

        def out_job(u, j):
            return j - 8 if u == HG - 1 and 8 <= j < 16 else None

        def out_view(bank):
            return bank[:].rearrange("p (g t c) -> p g t c", t=S, c=GB)

        def ungrouped(x, r):
            return x[:, r // 4, :].rearrange("p (t g c) -> p g t c", t=S, g=NG)[:, 4 * (r % 4):4 * (r % 4) + 4, :, :]

        def at_time(x, t):
            return x[:].rearrange("p (g t c) -> p t g c", t=S, c=GB)[:, t, :, :]

        @block.sync
        def _(sync):
            small = ((bqk[:], bqk_d), (wv[:], wv_d), (wo[:], wo_d), (bv[:], bv_d[0:1].partition_broadcast(P)),
                     (bo[:], bo_d[0:1].partition_broadcast(P)), (pos[:], pos_d), (wp[:], wp_d), (bp[:], bp_d),
                     (rw[:], rw_d), (rr[:], rr_d))
            for dst, src in small:
                sync.dma_start(dst, src).then_inc(small_in, 16)
            for u in range(HG):
                wait(sync, w_lo_ok, u - 1)
                sync.dma_start(wqk[u % 2][:], wqk_d[u]).then_inc(w_in[u % 2], 16)

        N_SMALL = 10 * 16

        @block.gpsimd
        def _(pool):
            chain = Chain(pool, pool_ok)
            chain(pool.memset(hot[:], 0.0))
            for n in range(4):
                rows = slice(32 * n, 32 * n + 32)
                chain(pool.affine_select(out=hot[rows, :].rearrange("p (t c) -> p t c", t=S),
                                         in_=hot[rows, :].rearrange("p (t c) -> p t c", t=S),
                                         compare_op=ALU.not_equal, fill=1.0, base=-D1,
                                         pattern=[[-1, S], [0, GB]], channel_multiplier=1))
            for i in range(2):
                chain(pool.memset(shift[i][:], 0.0))
            chain(pool.memset(v[:, :, :, D1:VW1], 1.0))
            pool.wait_ge(norm.xn_ok, S)
            pool.wait_ge(small_in, N_SMALL)
            for s in range(S):
                pool.tensor_tensor(h[:, s, :], h[:, s, :], bo[:], ALU.add).then_inc(bo_ok, 1)

        POOL_ALL = 8

        @block.tensor
        def _(pe):
            norm.tensor(pe)
            pe.wait_ge(small_in, N_SMALL)
            for u in range(HG):
                mm = accumulate(pe, p_work[0][:, u * (NPOS + 1):(u + 1) * (NPOS + 1)],
                                [(wp[:, k, u, :], pos[:, k, :]) for k in range(K)])
            mm.then_inc(pos_made, 1)
            pe.wait_ge(norm.lo_ok, S)
            pe.wait_ge(pool_ok, POOL_ALL)
            pe.wait_ge(const_lo, 2)
            pe.wait_ge(pos_ok, 1)
            for i in range(NV):
                wait(pe, work_free[i % 2], freed(i))
                for n in range(2):
                    toks = slice((2 * i + n) * P, (2 * i + n + 1) * P)
                    mm = accumulate(pe, p_work[i % 2][:, n * F:(n + 1) * F], [t for k in range(K) for t in three(
                        x_hi[:, k, toks], x_lo[:, k, toks], wv_hi[:, k, :], wv_lo[:, k, :])])
                mm.then_inc(work_made, 1)

            def project(u, i):
                n = job(u, i)
                bank = p_work[n % 2]
                pe.wait_ge(work_free[n % 2], freed(n))
                if i < 4 or i >= 8:
                    a, toks = i // 8, slice((i % 4) * BANK, (i % 4 + 1) * BANK)
                    pe.wait_ge(w_lo_ok, u + 1)
                    mm = accumulate(pe, bank[:], [t for k in range(K) for t in three(
                        wqk_hi[u % 2][:, k, a, :], wqk_lo[u % 2][:, k, a, :], x_hi[:, k, toks], x_lo[:, k, toks])])
                else:
                    pe.wait_ge(shift_ok, 4 * u + 4)
                    pe.wait_ge(work_free[0], freed(job(u, 4)))
                    pe.wait_ge(work_free[1], freed(job(u, 4)))
                    for t in range(4):
                        time = 4 * (i - 4) + t
                        mm = pe.matmul(bank[:, t * P:(t + 1) * P], shift[u % 2][:, time, :],
                                       at_time(q0, time),
                                       start=True, stop=True)
                mm.then_inc(work_made, 1)

            def project_out(k, i):
                pe.wait_ge(ot_lo_ok, 4 * k + 4)
                wait(pe, out_added, 8 * k + i - 1)
                for n in range(2):
                    toks = slice((2 * i + n) * P, (2 * i + n + 1) * P)
                    mm = accumulate(pe, p_out[i % 2][:, n * F:(n + 1) * F], three(
                        x_hi[:, k, toks], x_lo[:, k, toks], wo_hi[:, k, :], wo_lo[:, k, :]))
                mm.then_inc(out_made, 1)

            def step(u, j, g):
                if 2 <= g <= STEPS * HG + 1:
                    pe.wait_ge(exped, g - 1)
                    wait(pe, t_copied, g - 2)
                    for n in range(4):
                        mm = pe.transpose(p_turn[:, n * P:(n + 1) * P], prob[(g - 2) % 3][:, n, :], c["ident"][:])
                    mm.then_inc(turned, 1)
                if 3 <= g <= STEPS * HG + 2:
                    head, b = (g - 3) // 4, (g - 3) % 4
                    pe.wait_ge(t_copied, g - 2)
                    wait(pe, o_ok, g - 3)
                    for n in range(4):
                        mm = pe.matmul(p_o[:, n * HG * VW1:(n + 1) * HG * VW1], prob_t[(g - 3) % 2][:, n, :],
                                       v[:, 4 * b + n, head - head % HG:head - head % HG + HG, :]
                                       .rearrange("p e d -> p (e d)"), start=True, stop=True)
                    mm.then_inc(valued, 1)
                r = outs(u, j)
                if r is not None:
                    pe.wait_ge(o_ok, min(STEPS * HG, 32 * (r // 4 + 1)) if r // 4 == 0 else 60 + r % 4 + 1)
                    wait(pe, ot_lo_ok, r - 1)
                    if r >= 4:
                        pe.wait_ge(out_added, 8)
                    for n in range(4):
                        mm = pe.transpose(p_out[r % 2][:, n * P:(n + 1) * P],
                                          o[:, 4 * (r % 4) + n, (r // 4) * P:(r // 4 + 1) * P], c["ident"][:])
                    mm.then_inc(o_turned, 1)
                if 0 <= u < HG:
                    rows = slice(32 * (j // 4), 32 * (j // 4) + 32)
                    if j == 0:
                        for b in range(2):
                            pe.wait_ge(work_free[b], freed(job(u + 1, 0)))
                    wait(pe, shifted, g - 1)
                    pe.matmul(p_s[g % 2][:], c["ident_b"][:], c["mask"][:].unsqueeze(1).to_broadcast([P, 4, P]),
                              start=True, stop=False, skip_group_check=True)
                    for n in range(4):
                        toks = slice((4 * (j % 4) + n) * P, (4 * (j % 4) + n + 1) * P)
                        mm = pe.matmul(p_s[g % 2][:, n * P:(n + 1) * P], q[u % 2][rows, toks], k1[u % 2][rows, toks],
                                       start=False, stop=n == 3, skip_group_check=True)
                    mm.then_inc(scored, 1)
                if u < HG - 1 and j < JOBS:
                    project(u + 1, j)
                if out_job(u, j) is not None:
                    project_out(0, out_job(u, j))

            steps(step)
            for i in range(S // 2):
                project_out(1, i)

        @block.scalar
        def _(act):
            def constants(s):
                if s == 9:
                    act.wait_ge(small_in, N_SMALL)
                    act.copy(wv_hi[:], wv[:]).then_inc(const_hi, 1)
                    act.copy(wo_hi[:], wo[:]).then_inc(const_hi, 1)

            norm.scalar(act, beside=constants)
            act.wait_ge(bias_ok, 2)

            def cut(u):
                act.wait_ge(w_in[u % 2], 16 * (u // 2 + 1))
                wait(act, work_made, job(u - 1, 0) if u >= 2 else 0)
                act.copy(wqk_hi[u % 2][:], wqk[u % 2][:]).then_inc(w_hi_ok, 1)

            def step(u, j, g):
                if u < HG - 1 and j == 0:
                    cut(u + 1)
                if 2 <= g <= STEPS * HG + 1:
                    act.wait_ge(turned, g - 1)
                    wait(act, valued, g - 3)
                    act.copy(prob_t[g % 2][:], p_turn[:].rearrange("p (n c) -> p n c", n=4))\
                        .then_inc(t_copied, 1)
                r = outs(u, j)
                if r is not None:
                    act.wait_ge(o_turned, r + 1)
                    act.copy(ungrouped(x_hi, r), out_view(p_out[r % 2])).then_inc(ot_hi_ok, 1)
                if 0 <= u < HG:
                    act.wait_ge(shifted, g + 1)
                    act.activation(prob[g % 3][:], prob[g % 3][:], ACT.Exp, scale=float(D1) ** -0.5)\
                        .then_inc(exped, 1)
                if u < HG - 1 and j < 4:
                    n = job(u + 1, j)
                    act.wait_ge(work_made, n + 1)
                    if u >= 0:
                        for b in range(2):
                            act.wait_ge(work_free[b], freed(job(u, 8)))
                    act.activation(q0[:, j * BANK:(j + 1) * BANK], p_work[n % 2][:], ACT.Identity,
                                   bias=bq_rr[:, u + 1:u + 2]).then_inc(work_free[n % 2], 1)

            steps(step)

        @block.vector
        def _(dve):
            norm.vector(dve)
            dve.wait_ge(const_hi, 2)
            dve.tensor_tensor(wv_lo[:], wv[:], wv_hi[:].bitcast(F32), ALU.subtract).then_inc(const_lo, 1)
            dve.wait_ge(small_in, N_SMALL)
            dve.tensor_tensor(bq_rr[:], bqk[:, :, 0], rr[:], ALU.add).then_inc(bias_ok, 1)
            dve.tensor_tensor(rw_rr[:], rw[:], rr[:], ALU.subtract).then_inc(bias_ok, 1)
            dve.wait_ge(pos_made, 1)
            dve.tensor_tensor(p_t[:], p_work[0][:, 0:HG * (NPOS + 1)].rearrange("p (u r) -> p u r", u=HG),
                              bp[:].unsqueeze(2).to_broadcast([P, HG, NPOS + 1]), ALU.add).then_inc(pos_ok, 1)
            dve.tensor_tensor(wo_lo[:], wo[:], wo_hi[:].bitcast(F32), ALU.subtract).then_inc(const_lo, 1)
            dve.wait_ge(pos_ok, 1)
            dve.wait_ge(bias_ok, 2)
            dve.wait_ge(pool_ok, POOL_ALL)
            for i in range(NV):
                dve.wait_ge(work_made, i + 1)
                dve.tensor_tensor(v[:, 2 * i:2 * i + 2, :, 0:D1],
                                  p_work[i % 2][:].rearrange("p (g e d) -> p g e d", g=2, e=H1),
                                  bv[:].rearrange("p (e d) -> p e d", e=H1).unsqueeze(1)
                                  .to_broadcast([P, 2, H1, D1]), ALU.add).then_inc(work_free[i % 2], 1)

            def add_out(k, i):
                dve.wait_ge(bo_ok, S)
                dve.wait_ge(out_made, 8 * k + i + 1)
                wait(dve, out_added, 8 * k - 8 + i + 1)
                dve.tensor_tensor(h[:, 2 * i:2 * i + 2, :], h[:, 2 * i:2 * i + 2, :],
                                  p_out[i % 2][:].rearrange("p (t f) -> p t f", t=2), ALU.add).then_inc(out_added, 1)

            def fill_shift(u):
                if u >= 2:
                    dve.wait_ge(work_made, job(u - 2, 8))
                for n in range(4):
                    rows = slice(32 * n, 32 * n + 32)
                    src = p_t[rows, u, :]
                    part = list(src.ap[0])
                    window = bass.AP(src.tensor, src.offset + S - 1, [part, [-1, S], [1, S]])
                    dve.tensor_copy(shift[u % 2][rows, :, 32 * n + D1:32 * n + 2 * D1], window).then_inc(shift_ok, 1)

            def step(u, j, g):
                if u < HG - 1 and j == 0:
                    dve.wait_ge(w_hi_ok, u + 2)
                    dve.tensor_tensor(wqk_lo[(u + 1) % 2][:], wqk[(u + 1) % 2][:],
                                      wqk_hi[(u + 1) % 2][:].bitcast(F32), ALU.subtract).then_inc(w_lo_ok, 1)
                    fill_shift(u + 1)
                if 3 <= g <= STEPS * HG + 2:
                    head, b = (g - 3) // 4, (g - 3) % 4
                    dve.wait_ge(valued, g - 2)
                    po = p_o[:, 0:4 * HG * VW1].rearrange("p (n e d) -> p n e d", n=4, e=HG)[:, :, head % HG, :]
                    dve.reciprocal(inv[g % 2][:], po[:, :, D1]).then_inc(inv_ok, 1)
                    dve.wait_ge(inv_ok, g - 2)
                    dve.tensor_tensor(o[:, 4 * b:4 * b + 4, head * D1:(head + 1) * D1], po[:, :, 0:D1],
                                      inv[g % 2][:].unsqueeze(2).to_broadcast([P, 4, D1]), ALU.mult).then_inc(o_ok, 1)
                if 0 <= u < HG:
                    ps = p_s[g % 2][:].rearrange("p (n c) -> p n c", n=4)
                    dve.wait_ge(scored, g + 1)
                    dve.tensor_reduce(top[g % 2][:], ps, axis=X, op=ALU.max).then_inc(top_ok, 1)
                    dve.wait_ge(top_ok, g + 1)
                    wait(dve, turned, g - 2)
                    dve.tensor_tensor(prob[g % 3][:], ps, top[g % 2][:].unsqueeze(2).to_broadcast([P, 4, P]),
                                      ALU.subtract).then_inc(shifted, 1)
                last = out_job(u, j - 1) if u == HG - 1 else 7 if u == HG and j == 0 else None
                if last is not None:
                    add_out(0, last)
                r = outs(u, j)
                if r is not None:
                    dve.wait_ge(ot_hi_ok, r + 1)
                    dve.tensor_tensor(ungrouped(x_lo, r), out_view(p_out[r % 2]), ungrouped(x_hi, r).bitcast(F32),
                                      ALU.subtract).then_inc(ot_lo_ok, 1)
                if u < HG - 1 and 4 <= j < 8:
                    n = job(u + 1, j)
                    dve.wait_ge(work_made, n + 1)
                    if u >= 1:
                        dve.wait_ge(scored, STEPS * u)
                    for t in range(4):
                        made = p_work[n % 2][:, t * P:(t + 1) * P].rearrange("p (g c) -> p g c", c=GB)
                        ins = dve.scalar_tensor_tensor(at_time(q[(u + 1) % 2], 4 * (j - 4) + t), made,
                                                       rw_rr[:, u + 1:u + 2], at_time(q0, 4 * (j - 4) + t),
                                                       ALU.add, ALU.add)
                    ins.then_inc(work_free[n % 2], 1)
                if u < HG - 1 and 8 <= j < 12:
                    n = job(u + 1, j)
                    dve.wait_ge(work_made, n + 1)
                    if u >= 1:
                        dve.wait_ge(scored, STEPS * u)
                    toks = slice((j - 8) * BANK, (j - 7) * BANK)
                    dve.scalar_tensor_tensor(k1[(u + 1) % 2][:, toks].rearrange("p (g c) -> p g c", g=4),
                                             p_work[n % 2][:].rearrange("p (g c) -> p g c", g=4),
                                             bqk[:, u + 1, 1:2], hot[:].unsqueeze(1).to_broadcast([P, 4, P]),
                                             ALU.add, ALU.add).then_inc(work_free[n % 2], 1)

            def rows_after(q):
                dve.wait_ge(out_added, 8 + q + 1)
                for s in (2 * q, 2 * q + 1):
                    stats.rows(dve, s)

            steps(step)
            for i in range(S // 2):
                add_out(1, i)
                if i >= 1:
                    rows_after(i - 1)
            rows_after(S // 2 - 1)
    sp.close()


class Weights:

    def __init__(self, sp, w12_d, w3_d):
        self.w12_d, self.w3_d = w12_d, w3_d
        self.w12, self.w3 = sp.sb("w12", [P, 2, K, FF1]), sp.sb("w3", [P, M1, F])
        self.w12_hi = [sp.sb(f"w12_hi{i}", [P, 2, K, FF1], F32R) for i in range(2)]
        self.w12_lo = [sp.sb(f"w12_lo{i}", [P, 2, K, FF1], F32R) for i in range(2)]
        self.w3_hi = [sp.sb(f"w3_hi{i}", [P, M1, F], F32R) for i in range(2)]
        self.w3_lo = [sp.sb(f"w3_lo{i}", [P, M1, F], F32R) for i in range(2)]
        self.in12, self.in3 = sp.sem("w12_in"), sp.sem("w3_in")
        self.hi_ok, self.lo_ok = sp.sem("w_hi_ok"), sp.sem("w_lo_ok")

    def load12(self, sync, src):
        sync.dma_start(self.w12[:], src).then_inc(self.in12, 16)

    def load3(self, sync, src):
        sync.dma_start(self.w3[:], src).then_inc(self.in3, 16)

    def third(self, par, i):
        if i < 2:
            return self.w12_hi[par][:, i], self.w12_lo[par][:, i], self.w12[:, i]
        return self.w3_hi[par][:], self.w3_lo[par][:], self.w3[:]

    def cut_hi(self, act, e, par, i):
        hi, _, raw = self.third(par, i)
        act.wait_ge(self.in3 if i == 2 else self.in12, 16 * e + 16)
        act.copy(hi, raw).then_inc(self.hi_ok, 1)

    def cut_lo(self, dve, e, par, i):
        hi, lo, raw = self.third(par, i)
        dve.wait_ge(self.hi_ok, 3 * e + i + 1)
        dve.tensor_tensor(lo, raw, hi.bitcast(F32), ALU.subtract).then_inc(self.lo_ok, 1)


def build_router(nc, c, h, stats, xn, slot_i, slot_w, weights, r1_d, r2_d):
    HALVES = S * E1 // P
    with ExitStack() as ctx:
        sp = Space(nc, ctx, "router")
        x_hi, x_lo = sp.sb("x_hi", [P, K, T], F32R), sp.sb("x_lo", [P, K, T], F32R)
        r1, r1_hi, r1_lo = sp.sb("r1", [P, K, RH]), sp.sb("r1_hi", [P, K, RH], F32R), sp.sb("r1_lo", [P, K, RH], F32R)
        r2 = sp.sb("r2", [RH, E1])
        act1 = sp.sb("act1", [P, T])
        logit = sp.sb("logit", [P, HALVES, P])
        prob, best = sp.sb("prob", [P, HALVES, P]), sp.sb("best", [P, HALVES, CAP])
        best_i = sp.sb("best_i", [P, HALVES, CAP], U32)
        row = sp.sb("row", [P, HALVES])
        twice = sp.sb("twice", [P, 2, HALVES, 2, CAP])
        p_norm = [sp.ps(f"p_norm{i}", [P, BANK]) for i in range(2)]
        p_r1 = [sp.ps(f"p_r1{i}", [P, BANK]) for i in range(2)]
        p_logit, p_rows, p_slot = sp.ps("p_logit", [P, BANK]), sp.ps("p_rows", [P, BANK]), sp.ps("p_slot", [P, BANK])
        norm = Norm(sp, c, h, stats.mv, x_hi, x_lo, False, p_norm + [p_rows, p_slot], keep=xn)
        small_in, r1_hi_ok, r1_lo_ok = sp.sem("small_in"), sp.sem("r1_hi_ok"), sp.sem("r1_lo_ok")
        r1_made, act1_ok = sp.sem("r1_made"), sp.sem("act1_ok")
        logits_made, logits_ok, rows_made = sp.sem("logits_made"), sp.sem("logits_ok"), sp.sem("rows_made")
        shifted, exped, steps = sp.sem("shifted"), sp.sem("exped"), sp.sem("steps")
        none_ok, half_ok = sp.sem("none_ok"), [sp.sem(f"half_ok{i}") for i in range(HALVES)]
        twice_ok, slots_made, slots_ok = sp.sem("twice_ok"), sp.sem("slots_made"), sp.sem("slots_ok")
        block = ctx.enter_context(nc.Block())

        @block.gpsimd
        def _(pool):
            pool.memset(slot_i[:], -1.0).then_inc(none_ok, 1)
            norm.gpsimd(pool)

        @block.sync
        def _(sync):
            sync.dma_start(r1[:], r1_d).then_inc(small_in, 16)
            sync.dma_start(r2[:], r2_d).then_inc(small_in, 16)
            weights.load12(sync, weights.w12_d[0])
            weights.load3(sync, weights.w3_d[0])

        @block.tensor
        def _(pe):
            norm.tensor(pe)
            pe.wait_ge(r1_lo_ok, 1)
            pe.wait_ge(norm.lo_ok, S)
            for i in range(CH):
                toks = slice(i * BANK, (i + 1) * BANK)
                wait(pe, act1_ok, i - 1)
                accumulate(pe, p_r1[i % 2][:], [t for k in range(K) for t in three(
                    r1_hi[:, k, :], r1_lo[:, k, :], x_hi[:, k, toks], x_lo[:, k, toks])]).then_inc(r1_made, 1)
            for s in range(S):
                pe.wait_ge(act1_ok, s // 4 + 1)
                mm = pe.matmul(p_logit[:, s * E1:(s + 1) * E1], act1[:, s * P:(s + 1) * P], r2[:],
                               start=True, stop=True)
            mm.then_inc(logits_made, 1)
            pe.wait_ge(logits_ok, 1)
            for i in range(HALVES):
                mm = pe.transpose(p_rows[:, i * P:(i + 1) * P], logit[:, i, :], c["ident"][:])
            mm.then_inc(rows_made, 1)
            pe.wait_ge(twice_ok, 2)
            for a in range(2):
                for i in range(HALVES):
                    n = HALVES * a + i
                    mm = pe.transpose(p_slot[:, n * P:(n + 1) * P], twice[:, a, i, :, :]
                                      .rearrange("p r c -> p (r c)"), c["ident"][:])
            mm.then_inc(slots_made, 1)

        @block.scalar
        def _(act):
            act.wait_ge(small_in, 32)
            act.copy(r1_hi[:], r1[:]).then_inc(r1_hi_ok, 1)
            norm.scalar(act)
            for i in range(CH):
                if i < 3:
                    weights.cut_hi(act, 0, 0, i)
                act.wait_ge(r1_made, i + 1)
                act.activation(act1[:, i * BANK:(i + 1) * BANK], p_r1[i % 2][:], ACT.Silu).then_inc(act1_ok, 1)
            act.wait_ge(shifted, 1)
            act.activation(prob[:], prob[:], ACT.Exp).then_inc(exped, 1)

        @block.vector
        def _(dve):
            dve.wait_ge(r1_hi_ok, 1)
            dve.tensor_tensor(r1_lo[:], r1[:], r1_hi[:].bitcast(F32), ALU.subtract).then_inc(r1_lo_ok, 1)
            norm.vector(dve)
            for i in range(3):
                weights.cut_lo(dve, 0, 0, i)
            wide = [P, HALVES, P]
            chain = Chain(dve, steps)
            dve.wait_ge(logits_made, 1)
            dve.tensor_copy(logit[:], p_logit[:, 0:HALVES * P].rearrange("p (i r) -> p i r", i=HALVES))\
                .then_inc(logits_ok, 1)
            dve.wait_ge(rows_made, 1)
            rows = p_rows[:, 0:HALVES * P].rearrange("p (i c) -> p i c", i=HALVES)
            chain(dve.tensor_reduce(row[:], rows, axis=X, op=ALU.max))
            dve.tensor_tensor(prob[:], rows, row[:].unsqueeze(2).to_broadcast(wide), ALU.subtract)\
                .then_inc(shifted, 1)
            dve.wait_ge(exped, 1)
            chain(dve.tensor_reduce(row[:], prob[:], axis=X, op=ALU.add))
            chain(dve.reciprocal(row[:], row[:]))
            chain(dve.tensor_tensor(prob[:], prob[:], row[:].unsqueeze(2).to_broadcast(wide), ALU.mult))
            for r in range(CAP // 8):
                cols = slice(8 * r, 8 * r + 8)
                for step in range(3):
                    for i in range(HALVES):
                        wait(dve, half_ok[i], 3 * r + step)
                        if step == 0:
                            ins = dve.max(best[:, i, cols], prob[:, i, :])
                        elif step == 1:
                            ins = dve.max_index(best_i[:, i, cols], best[:, i, cols], prob[:, i, :])
                        else:
                            ins = dve.match_replace(prob[:, i, :], best[:, i, cols], prob[:, i, :], -1.0)
                        ins.then_inc(half_ok[i], 1)
            for i in range(HALVES):
                dve.wait_ge(half_ok[i], 3 * CAP // 8)
            chain(dve.tensor_reduce(row[:], best[:], axis=X, op=ALU.add))
            chain(dve.tensor_scalar_add(row[:], row[:], 1e-9))
            chain(dve.reciprocal(row[:], row[:]))
            both = [P, HALVES, 2, CAP]
            chain(dve.tensor_tensor(best[:], best[:], row[:].unsqueeze(2).to_broadcast([P, HALVES, CAP]), ALU.mult))
            dve.tensor_copy(twice[:, 0], best[:].unsqueeze(2).to_broadcast(both)).then_inc(twice_ok, 1)
            dve.tensor_copy(twice[:, 1], best_i[:].unsqueeze(2).to_broadcast(both)).then_inc(twice_ok, 1)
            dve.wait_ge(slots_made, 1)
            dve.wait_ge(none_ok, 1)
            for odd in range(2):
                rows = slice(CAP * odd, CAP * odd + CAP)
                src = p_slot[rows, :].rearrange("p (a b odd e) -> p a b odd e", a=2, odd=2, e=E1)
                dve.tensor_copy(slot_w[rows, :, :], src[:, 0, :, odd, :]).then_inc(slots_ok, 1)
                dve.tensor_copy(slot_i[rows, :, :].rearrange("p (b odd) e -> p b odd e", odd=2)[:, :, odd, :],
                                src[:, 1, :, odd, :]).then_inc(slots_ok, 1)
    sp.close()


def build_ffn1(nc, c, h, stats, r1_d, r2_d, w12_d, w3_d):
    NB = S // 2
    AFTER_F0, AFTER_Q2 = ((0, 0), (1, 2)), ((0, 1),)
    with ExitStack() as outer:
        keep = Space(nc, outer, "f1")
        xn = [keep.sb(f"xn{i}", [P, S, F], BF16) for i in range(3)]
        slot_i, slot_w = keep.sb("slot_i", [P, S, E1]), keep.sb("slot_w", [P, NB, E1])
        weights = Weights(keep, w12_d, w3_d)
        build_router(nc, c, h, stats, xn, slot_i, slot_w, weights, r1_d, r2_d)
        ctx = outer.enter_context(ExitStack())
        sp = Space(nc, ctx, "f1")
        put = [sp.sb(f"put{i}", [P, S, P], F32R) for i in range(2)]
        place = [sp.sb(f"place{i}", [P, S]) for i in range(2)]
        ident_r = sp.sb("ident_r", [P, P], F32R)
        take = [sp.sb(f"take{i}", [P, S, CAP], BF16) for i in range(2)]
        weight = [sp.sb(f"weight{i}", [P, NB]) for i in range(2)]
        xe = [[sp.sb(f"xe{i}{z}", [P, K, BANK], F32R) for z in ("hi", "lo")] for i in range(2)]
        silu = [sp.sb(f"silu{i}", [P, BANK]) for i in range(2)]
        hid = [sp.sb(f"hid{i}", [P, BANK]) for i in range(2)]
        hid_hi, hid_lo = sp.sb("hid_hi", [P, M1, BANK], F32R), sp.sb("hid_lo", [P, M1, BANK], F32R)
        y_hi, y_lo = sp.sb("y_hi", [P, 4, F], F32R), sp.sb("y_lo", [P, 4, F], F32R)
        p_gate = [sp.ps(f"p_gate{i}", [P, BANK]) for i in range(2)]
        p_value = [sp.ps(f"p_value{i}", [P, BANK]) for i in range(2)]
        p_y = [sp.ps(f"p_y{i}", [P, BANK]) for i in range(2)]
        p_take, p_put = sp.ps("p_take", [P, BANK]), sp.ps("p_put", [P, BANK])

        w12_hi, w12_lo, w3_hi, w3_lo = weights.w12_hi, weights.w12_lo, weights.w3_hi, weights.w3_lo
        w_lo_ok = weights.lo_ok
        put_begun = sp.sem("put_begun")
        put_ok, take_made, take_ok = sp.sem("put_ok"), sp.sem("take_made"), sp.sem("take_ok")
        weight_ok, ident_ok = sp.sem("weight_ok"), sp.sem("ident_ok")
        taken, xe_hi_ok, xe_lo_ok = sp.sem("taken"), sp.sem("xe_hi_ok"), sp.sem("xe_lo_ok")
        gate_made, value_made = sp.sem("gate_made"), sp.sem("value_made")
        silu_ok, hid_ok, hid_hi_ok, hid_lo_ok = sp.sem("silu_ok"), sp.sem("hid_ok"), sp.sem("hid_hi_ok"), sp.sem("hid_lo_ok")
        y_made, y_hi_ok, y_lo_ok = sp.sem("y_made"), sp.sem("y_hi_ok"), sp.sem("y_lo_ok")
        put_made, added = sp.sem("put_made"), sp.sem("added")
        block = ctx.enter_context(nc.Block())

        def run(engine, expert):
            expert(0, 0, False, True)
            with engine.Fori(0, (E1 - 2) // 2) as i:
                expert(2 * i + 1, 1, True, True)
                expert(2 * i + 2, 0, True, True)
            expert(E1 - 1, 1, True, False)

        def column(x, e):
            return x[:, :, e:e + 1] if isinstance(e, int) else x[:, :, bass.ds(e, 1)]

        @block.sync
        def _(sync):
            with sync.Fori(1, E1) as e:
                sync.wait_ge(w_lo_ok, 3 * e - 1)
                weights.load12(sync, w12_d[bass.ds(e, 1)].squeeze(0))
                sync.wait_ge(w_lo_ok, 3 * e)
                weights.load3(sync, w3_d[bass.ds(e, 1)].squeeze(0))

        @block.gpsimd
        def _(pool):
            def build_put(e, par):
                pool.wait_ge(weight_ok, 2 * e + 2)
                wait(pool, put_made, 8 * e - 12)
                pool.sem_inc(put_begun, 1)
                for s in range(S):
                    if s >= NB and s % 2 == 0 and not (isinstance(e, int) and e < 2):
                        pool.wait_ge(put_made, 8 * e - 12 + (s - NB) // 2 + 1)
                        pool.sem_inc(put_begun, 1)
                    pool.tensor_scalar(put[par][:, s, :], c["iota_p"][:], place[par][:, s:s + 1], None,
                                       ALU.is_equal).then_inc(put_ok, 1)

            def expert(e, par, before, more):
                if more:
                    build_put(e + 1, 1 - par)

            pool.wait_ge(put_ok, S)
            run(pool, expert)

        @block.tensor
        def _(pe):
            def turn_put(e, par, i):
                n = 2 * e + i
                pe.wait_ge(put_ok, S * e + NB * (i + 1))
                wait(pe, xe_lo_ok, 2 * n)
                wait(pe, take_ok, n)
                for b in range(4):
                    mm = accumulate(pe, p_take[:, b * P:(b + 1) * P],
                                    [(put[par][:, 2 * (4 * i + b) + odd, :], ident_r[:]) for odd in range(2)])
                mm.then_inc(take_made, 1)

            def take_tiles(e, par, cc, k):
                n = 2 * e + cc
                pe.wait_ge(take_ok, 2 * e + 1 + cc)
                wait(pe, xe_lo_ok, 2 * n + k)
                for b in range(NB):
                    mm = accumulate(pe, p_take[:, b * CAP:(b + 1) * CAP],
                                    [(part[:, NB * cc + b, k * P:(k + 1) * P], take[par][:, NB * cc + b, :])
                                     for part in xn])
                mm.then_inc(taken, 1)

            def put_back(e, par, cc, q):
                m = 2 * e + cc
                pe.wait_ge(y_lo_ok, 4 * m + q + 1)
                wait(pe, added, 4 * m + q)
                for odd in range(2):
                    mm = accumulate(pe, p_put[:, odd * F:(odd + 1) * F],
                                    [(put[par][:, 2 * (4 * cc + q) + odd, :], y[:, q, :]) for y in (y_hi, y_lo)])
                mm.then_inc(put_made, 1)

            def put_last(e, par, before, cc, q):
                if cc == 1:
                    put_back(e, par, 0, q)
                elif before:
                    put_back(e - 1, 1 - par, 1, q)

            def expand(par, cc, n, f, a, bank, free, made):
                wait(pe, free, 4 * n + f - 1)
                cols = slice(f * P, (f + 1) * P)
                accumulate(pe, bank[f % 2][:], [t for k in range(K) for t in three(
                    w12_hi[par][:, a, k, cols], w12_lo[par][:, a, k, cols],
                    xe[cc][0][:, k, :], xe[cc][1][:, k, :])]).then_inc(made, 1)

            def reduce(par, q, fs, last):
                pairs = [t for f in fs for t in three(
                    hid_hi[:, f, q * P:(q + 1) * P], hid_lo[:, f, q * P:(q + 1) * P],
                    w3_hi[par][:, f, :], w3_lo[par][:, f, :])]
                return accumulate(pe, p_y[q % 2][:, 0:F], pairs, first=fs[0] == 0, last=last)

            def expert(e, par, before, more):
                for cc in range(2):
                    n = 2 * e + cc
                    pe.wait_ge(xe_lo_ok, 2 * n + 2)
                    pe.wait_ge(w_lo_ok, 3 * e + 3)
                    for f in range(M1):
                        expand(par, cc, n, f, 0, p_gate, silu_ok, gate_made)
                        if f < 3:
                            put_last(e, par, before, cc, f)
                        expand(par, cc, n, f, 1, p_value, hid_ok, value_made)
                        if cc == 0 and f % 2:
                            take_tiles(e, par, 1, f // 2)
                        elif more and f % 2:
                            take_tiles(e + 1, 1 - par, 0, f // 2)
                    for q in range(2):
                        wait(pe, y_lo_ok, 4 * n + q - 1)
                        pe.wait_ge(hid_lo_ok, 4 * n + 3)
                        reduce(par, q, (0, 1, 2), False)
                    pe.wait_ge(hid_lo_ok, 4 * n + 4)
                    for q in range(2):
                        reduce(par, q, (3,), True).then_inc(y_made, 1)
                    if more:
                        turn_put(e + 1, 1 - par, cc)
                    put_last(e, par, before, cc, 3)
                    for q in range(2, 4):
                        pe.wait_ge(y_lo_ok, 4 * n + q - 1)
                        reduce(par, q, (0, 1, 2, 3), True).then_inc(y_made, 1)

            pe.wait_ge(ident_ok, 1)
            turn_put(0, 0, 0)
            for k in range(K):
                take_tiles(0, 0, 0, k)
            turn_put(0, 0, 1)
            run(pe, expert)
            for q in range(4):
                put_back(E1 - 1, 1, 1, q)

        @block.scalar
        def _(act):
            def cut(e, par, i):
                wait(act, y_made, 8 * (e - 1))
                weights.cut_hi(act, e, par, i)

            def copy_take(e, par, i):
                act.wait_ge(take_made, 2 * e + i + 1)
                wait(act, taken, 4 * (e - 1))
                act.copy(take[par][:, NB * i:NB * (i + 1), :], p_take[:].rearrange("p (b c) -> p b c", c=CAP))\
                    .then_inc(take_ok, 1)

            def copy_xe(e, cc, k):
                n = 2 * e + cc
                act.wait_ge(taken, 2 * n + k + 1)
                wait(act, value_made, 4 * (n - 1))
                act.copy(xe[cc][0][:, k, :], p_take[:]).then_inc(xe_hi_ok, 1)

            def copy_next(e, more, cc, k):
                if cc == 0:
                    copy_xe(e, 1, k)
                elif more:
                    copy_xe(e + 1, 0, k)

            def expert(e, par, before, more):
                for cc in range(2):
                    n = 2 * e + cc
                    for f in range(M1):
                        act.wait_ge(gate_made, 4 * n + f + 1)
                        wait(act, hid_ok, 4 * n + f - 1)
                        act.activation(silu[f % 2][:], p_gate[f % 2][:], ACT.Silu).then_inc(silu_ok, 1)
                        if f == 1:
                            copy_next(e, more, cc, 0)
                        act.wait_ge(hid_ok, 4 * n + f + 1)
                        wait(act, y_made, 4 * n)
                        act.copy(hid_hi[:, f, :], hid[f % 2][:]).then_inc(hid_hi_ok, 1)
                        for at, i in AFTER_F0:
                            if more and f == 0 and at == cc:
                                cut(e + 1, 1 - par, i)
                    copy_next(e, more, cc, 1)
                    for q in range(4):
                        act.wait_ge(y_made, 4 * n + q + 1)
                        act.wait_ge(weight_ok, 2 * e + 1)
                        wait(act, put_made, 4 * n - 3 + q)
                        act.activation(y_hi[:, q, :], p_y[q % 2][:, 0:F], ACT.Copy,
                                       scale=weight[par][:, 4 * cc + q:4 * cc + q + 1]).then_inc(y_hi_ok, 1)
                        if more and q == 1:
                            copy_take(e + 1, 1 - par, cc)
                        for at, i in AFTER_Q2:
                            if more and q == 2 and at == cc:
                                cut(e + 1, 1 - par, i)

            copy_take(0, 0, 0)
            for k in range(K):
                copy_xe(0, 0, k)
            copy_take(0, 0, 1)
            run(act, expert)

        @block.vector
        def _(dve):
            def take_slots(e, par):
                wait(dve, y_hi_ok, 8 * (e - 1))
                wait(dve, y_lo_ok, 8 * (e - 1))
                wait(dve, put_ok, S * (e - 1))
                dve.tensor_copy(weight[par][:].unsqueeze(2), column(slot_w, e)).then_inc(weight_ok, 1)
                dve.tensor_copy(place[par][:].unsqueeze(2), column(slot_i, e)).then_inc(weight_ok, 1)

            def cut_xe(e, cc, k):
                n = 2 * e + cc
                dve.wait_ge(xe_hi_ok, 2 * n + k + 1)
                dve.tensor_tensor(xe[cc][1][:, k, :], p_take[:], xe[cc][0][:, k, :].bitcast(F32), ALU.subtract)\
                    .then_inc(xe_lo_ok, 1)

            def add(cc, m, q):
                s = 2 * (4 * cc + q)
                dve.wait_ge(put_made, 4 * m + q + 1)
                wait(dve, added, 4 * m + q)
                dve.tensor_tensor(h[:, s:s + 2, :], h[:, s:s + 2, :], p_put[:].rearrange("p (b f) -> p b f", b=2),
                                  ALU.add).then_inc(added, 1)

            def cut_next(e, more, cc, k):
                if cc == 0:
                    cut_xe(e, 1, k)
                elif more:
                    cut_xe(e + 1, 0, k)

            def add_last(before, cc, n, q):
                if cc == 1:
                    add(0, n - 1, q)
                elif before:
                    add(1, n - 1, q)

            def expert(e, par, before, more):
                for cc in range(2):
                    n = 2 * e + cc
                    if cc == 0 and more:
                        take_slots(e + 1, 1 - par)
                    for f in range(M1):
                        if f < 3:
                            add_last(before, cc, n, f)
                        dve.wait_ge(value_made, 4 * n + f + 1)
                        dve.wait_ge(silu_ok, 4 * n + f + 1)
                        wait(dve, hid_lo_ok, 4 * n + f - 1)
                        dve.tensor_tensor(hid[f % 2][:], p_value[f % 2][:], silu[f % 2][:], ALU.mult)\
                            .then_inc(hid_ok, 1)
                        if f == 1:
                            cut_next(e, more, cc, 0)
                        dve.wait_ge(hid_hi_ok, 4 * n + f + 1)
                        dve.tensor_tensor(hid_lo[:, f, :], hid[f % 2][:], hid_hi[:, f, :].bitcast(F32),
                                          ALU.subtract).then_inc(hid_lo_ok, 1)
                        for at, i in AFTER_F0:
                            if more and f == 0 and at == cc:
                                weights.cut_lo(dve, e + 1, 1 - par, i)
                    cut_next(e, more, cc, 1)
                    for q in range(4):
                        dve.wait_ge(y_hi_ok, 4 * n + q + 1)
                        dve.scalar_tensor_tensor(y_lo[:, q, :], p_y[q % 2][:, 0:F],
                                                 weight[par][:, 4 * cc + q:4 * cc + q + 1],
                                                 y_hi[:, q, :].bitcast(F32), ALU.mult, ALU.subtract)\
                            .then_inc(y_lo_ok, 1)
                        if q == 1:
                            add_last(before, cc, n, 3)
                        for at, i in AFTER_Q2:
                            if more and q == 2 and at == cc:
                                weights.cut_lo(dve, e + 1, 1 - par, i)

            dve.tensor_copy(ident_r[:], c["ident"][:]).then_inc(ident_ok, 1)
            take_slots(0, 0)
            dve.wait_ge(weight_ok, 2)
            wide = [P, NB, P]
            for i in range(2):
                tiles = slice(NB * i, NB * i + NB)
                dve.tensor_tensor(put[0][:, tiles, :], c["iota_p"][:].unsqueeze(1).to_broadcast(wide),
                                  place[0][:, tiles].unsqueeze(2).to_broadcast(wide), ALU.is_equal)\
                    .then_inc(put_ok, NB)
            for k in range(K):
                cut_xe(0, 0, k)
            run(dve, expert)
            for q in range(4):
                add(1, 2 * E1 - 1, q)


def build(nc, a, out):
    with ExitStack() as ctx:
        sp = Space(nc, ctx, "all")
        h = sp.sb("h", [P, S, F])
        c = {
            "ident": sp.sb("ident", [P, P]),
            "ident_b": sp.sb("ident_b", [P, P], BF16),
            "iota_p": sp.sb("iota_p", [P, P]),
            "block_i": sp.sb("block_i", [P, P], I32),
            "block_f": sp.sb("block_f", [P, P]),
            "mask": sp.sb("mask", [P, P], BF16),
        }
        stats = Stats(sp, h)
        build_constants(nc, c)
        build_tokens(nc, c, h, stats, a["ids"], a["dmap"], a["emb"], a["wexp"], a["wproj"])
        build_attention0(nc, c, h, stats, a["a0_w"], a["a0_wv"], a["a0_bqk"], a["a0_bv"], a["a0_wo"], a["a0_bo"])
        build_ffn0(nc, c, h, stats, a["f0_gate"], a["f0_gate_b"], a["f0_w"], a["f0_b1"], a["f0_b2"])
        build_attention1(nc, c, h, stats, a["a1_wqk"], a["a1_bqk"], a["a1_wv"], a["a1_bv"], a["a1_pos"], a["a1_wp"],
                             a["a1_bp"], a["a1_rw"], a["a1_rr"], a["a1_wo"], a["a1_bo"])
        build_ffn1(nc, c, h, stats, a["f1_r1"], a["f1_r2"], a["f1_w12"], a["f1_w3"])
        stored = sp.sem("stored")
        block = ctx.enter_context(nc.Block())

        @block.sync
        def _(sync):
            sync.dma_start(out.rearrange("s b f -> b s f"), h[:]).then_inc(stored, 16)
            sync.wait_ge(stored, 16)


def kernel(**inputs):
    import numpy as _np
    import concourse.bacc as _bacc
    from concourse import mybir as _mybir
    from concourse.bass_utils import run_bass_kernel_spmd as _run

    g = {k: _np.asarray(v) for k, v in inputs.items()}

    def halves(w):
        w = w.reshape(w.shape[:-2] + (w.shape[-2] // P, P, w.shape[-1]))
        return _np.moveaxis(w, -3, -2)

    def heads32(w):
        out = _np.zeros((H1, 32) + w.shape[1:], w.dtype)
        out[:, 0:D1] = w.reshape((H1, D1) + w.shape[1:])
        return out.reshape((HG, P) + w.shape[1:])

    w_in0, b_in0 = g["L0_attn_in_proj_weight"], g["L0_attn_in_proj_bias"]
    w_in1, b_in1 = g["L1_attn_in_proj_weight"], g["L1_attn_in_proj_bias"]
    w12 = _np.stack([g["L1_ffn_w1"], g["L1_ffn_w2"]], 1)
    ffn0_in = _np.concatenate([g["L0_ffn_sw1"][None], g["L0_ffn_w1"]])
    ffn0_out = _np.concatenate([g["L0_ffn_sw2"][None], g["L0_ffn_w2"]])
    host = {
        "ids": g["x"].T,
        "dmap": g["L0_tok_domain_map"][:, None],
        "emb": g["L0_tok_emb_table"],
        "wexp": halves(g["L0_tok_W_exp"].reshape(F, F).T),
        "wproj": halves(g["L0_tok_W_proj"].transpose(0, 2, 1).reshape(F, F)),
        "a0_w": w_in0.reshape(3, PAIRS, P, K, P)[0:2].transpose(1, 4, 3, 0, 2).reshape(PAIRS, P, K, 2 * P),
        "a0_wv": w_in0[2 * H0 * D0:].reshape(PAIRS // 2, VB, K, P).transpose(0, 3, 2, 1),
        "a0_bqk": b_in0.reshape(3, PAIRS, P)[0:2].transpose(2, 1, 0),
        "a0_bv": b_in0[2 * H0 * D0:][None],
        "a0_wo": halves(g["L0_attn_out_proj_weight"].T),
        "a0_bo": g["L0_attn_out_proj_bias"][None],
        "f0_gate": halves(g["L0_ffn_gate_w"]),
        "f0_gate_b": g["L0_ffn_gate_b"][None],
        "f0_w": _np.stack([halves(ffn0_in), halves(ffn0_out)], 2),
        "f0_b1": _np.concatenate([g["L0_ffn_sb1"][None], g["L0_ffn_b1"]]).reshape(E0 + 1, K, P).transpose(2, 0, 1),
        "f0_b2": _np.concatenate([g["L0_ffn_sb2"][None], g["L0_ffn_b2"]]),
        "a1_wqk": _np.stack([halves(heads32(w_in1[i * F:(i + 1) * F]).transpose(0, 2, 1)) for i in range(2)], 3),
        "a1_bqk": _np.stack([heads32(b_in1[i * F:(i + 1) * F]) for i in range(2)], 0).transpose(2, 1, 0),
        "a1_wv": halves(w_in1[2 * F:].T),
        "a1_bv": b_in1[2 * F:][None],
        "a1_pos": halves(_np.concatenate([g["L1_attn_pos"][0:NPOS, 0], _np.zeros((1, F), _np.float32)]).T),
        "a1_wp": _np.moveaxis(halves(heads32(g["L1_attn_pos_proj_weight"]).transpose(0, 2, 1)), 0, 2),
        "a1_bp": heads32(g["L1_attn_pos_proj_bias"]).T,
        "a1_rw": heads32(g["L1_attn_r_w_bias"].reshape(F)).T,
        "a1_rr": heads32(g["L1_attn_r_r_bias"].reshape(F)).T,
        "a1_wo": halves(g["L1_attn_out_proj_weight"].T),
        "a1_bo": g["L1_attn_out_proj_bias"][None],
        "f1_r1": halves(g["L1_ffn_router_w1"]),
        "f1_r2": g["L1_ffn_router_w2"],
        "f1_w12": halves(w12).transpose(0, 2, 1, 3, 4),
        "f1_w3": halves(g["L1_ffn_w3"]),
    }
    nc = _bacc.Bacc("TRN2", target_bir_lowering=False, num_devices=1)
    arrays, args = {}, {}
    for name, v in host.items():
        v = _np.ascontiguousarray(v)
        arrays[f"in_{name}"] = v
        args[name] = nc.dram_tensor(f"in_{name}", v.shape, _mybir.dt.from_np(v.dtype), kind="ExternalInput").ap()
    out = nc.dram_tensor("out", (S, P, F), _mybir.dt.float32, kind="ExternalOutput").ap()
    build(nc, args, out)
    r = _run(nc, [arrays], core_ids=[0])
    return r.results[0]["out"]
```
